# Optimizing a Trainium2 kernel written in Bass

```python
import numpy as np
import jax
import jax.numpy as jnp

def _softmax(x, axis=-1):
    return jax.nn.softmax(x, axis=axis)

def _gelu(x):
    return jax.nn.gelu(x, approximate=True)

def _silu(x):
    return jax.nn.silu(x)

def _sigmoid(x):
    return jax.nn.sigmoid(x)

def _layernorm(x, axis=-1, eps=1e-05):
    m = jnp.mean(x, axis=axis, keepdims=True)
    v = jnp.var(x, axis=axis, keepdims=True)
    return (x - m) / jnp.sqrt(v + eps)

def _scatter_add(tgt, idx, src, axis=0):
    return tgt.at[idx].add(src)

def _segment_sum(src, seg, n):
    return jax.ops.segment_sum(src, seg, n)
kernel_name = 'mk_flamingo_gated_d2_seqx_r8_694671'

def setup_inputs(seed: int=0):
    np.random.seed(seed)
    _w = jnp.asarray

    def _rec_inputs():
        import jax
        import jax.numpy as jnp
        _rk = jax.random.key(seed)
        x = -0.0002928 + 1 * jax.random.normal(jax.random.fold_in(_rk, 1), (16, 56, 128), jnp.float32)
        _lenS = 56 - jax.random.randint(jax.random.fold_in(_rk, 7), (16,), 0, max(1, 56 // 4) + 1, jnp.int32)
        _lenS2 = 1500 - jax.random.randint(jax.random.fold_in(_rk, 8), (16,), 0, max(1, 1500 // 4) + 1, jnp.int32)
        _ctx_1024P = jax.random.normal(jax.random.fold_in(_rk, 11), (16, 16, 128), jnp.float32)
        _ctx_1024c = jax.random.dirichlet(jax.random.fold_in(_rk, 511), 0.3 * jnp.ones((16,), jnp.float32), (16, 1500))
        _ctx_1024t = jnp.einsum('bsk,bkd->bsd', _ctx_1024c, _ctx_1024P)
        _ctx_1024t = _ctx_1024t * jax.lax.rsqrt(jnp.mean(jnp.square(_ctx_1024t)) + 1e-12) * 0.953939
        ctx_1024 = -1.52775e-05 + 0.999936 * (_ctx_1024t + 0.3 * jax.random.normal(jax.random.fold_in(_rk, 611), (16, 1500, 128), jnp.float32))
        _validS = jnp.arange(56)[None, :] < _lenS[:, None]
        _validS2 = jnp.arange(1500)[None, :] < _lenS2[:, None]
        _causal = jnp.tril(jnp.ones((56, 56), dtype=bool))
        mask_BxS2_bk0 = jnp.logical_not(jnp.broadcast_to(_validS2[:, :], (16, 1500)))
        mask_BxS_bk0 = jnp.logical_not(jnp.broadcast_to(_validS[:, :], (16, 56)))
        _g = jax.random.normal(jax.random.fold_in(_rk, 9001), (2, 2), jnp.float32)
        _g = jnp.sign(_g) * jnp.maximum(jnp.abs(_g), 1.0) + (_g == 0) * 1.0
        g_xattn = _g[0]
        g_ffn = _g[1]
        return (x, ctx_1024, mask_BxS2_bk0, mask_BxS_bk0, g_xattn, g_ffn)
    x, ctx_1024, mask_BxS2_bk0, mask_BxS_bk0, g_xattn, g_ffn = _rec_inputs()

    def _L0_xattn_setup():
        import jax, jax.numpy as jnp
        import numpy as np
        B, N_TXT, N_IMG, DIM = (8, 64, 512, 128)
        HEADS, DIM_HEAD = (16, 64)
        INNER = HEADS * DIM_HEAD
        key = jax.random.key(seed)
        ks = jax.random.split(key, 8)
        txt = jax.random.normal(ks[0], (B, N_TXT, DIM), dtype=jnp.float32)
        image = jax.random.normal(ks[1], (B, N_IMG, DIM), dtype=jnp.float32)
        kv_mask = jax.random.randint(ks[2], (B, N_IMG), 0, 2).astype(bool)
        q_mask = jax.random.randint(ks[3], (B, N_TXT), 0, 2).astype(bool)
        s = 0.02
        Wq = jax.random.normal(ks[4], (DIM, INNER), dtype=jnp.float32) * s
        Wkv = jax.random.normal(ks[5], (DIM, 2 * INNER), dtype=jnp.float32) * s
        Wout = jax.random.normal(ks[6], (INNER, DIM), dtype=jnp.float32) * s
        bout = jnp.zeros((DIM,), dtype=jnp.float32)
        return {'txt': txt, 'image': image, 'kv_mask': kv_mask, 'q_mask': q_mask, 'Wq': Wq, 'Wkv': Wkv, 'Wout': Wout, 'bout': bout}
    _L0_xattn_all = _L0_xattn_setup()
    _L0_xattn_in = {k: v for k, v in _L0_xattn_all.items() if k in ('Wq', 'Wkv', 'Wout', 'bout')}
    del _L0_xattn_all

    def _L0_ffn_setup():
        import jax, jax.numpy as jnp
        import numpy as np
        from jax import lax
        DIM = 128
        INTER = 64
        N_EXPERTS = 16
        TOPK = 4
        ROUTE_SCALE = 2.5
        VOCAB = 4000

        def _silu_and_mul(gu):
            gate, up = jnp.split(gu, 2, axis=-1)
            return jax.nn.silu(gate) * up
        key = jax.random.key(seed)
        ks = jax.random.split(key, 8)
        x = jax.random.normal(ks[0], (2, 64, DIM), dtype=jnp.float32)
        input_ids = jax.random.randint(ks[1], (2, 64), 0, VOCAB)
        s = 0.02
        gate_w = jax.random.normal(ks[2], (N_EXPERTS, DIM), dtype=jnp.float32) * s
        gate_b = jax.random.normal(ks[3], (N_EXPERTS,), dtype=jnp.float32) * s
        w13 = jax.random.normal(ks[4], (N_EXPERTS, 2 * INTER, DIM), dtype=jnp.float32) * s
        w2 = jax.random.normal(ks[5], (N_EXPERTS, DIM, INTER), dtype=jnp.float32) * s
        w13_s = jax.random.normal(ks[6], (2 * INTER, DIM), dtype=jnp.float32) * s
        w2_s = jax.random.normal(ks[7], (DIM, INTER), dtype=jnp.float32) * s
        return {'x': x, 'input_ids': input_ids, 'gate_w': gate_w, 'gate_b': gate_b, 'w13': w13, 'w2': w2, 'w13_s': w13_s, 'w2_s': w2_s}
    _L0_ffn_all = _L0_ffn_setup()
    _L0_ffn_in = {k: v for k, v in _L0_ffn_all.items() if k in ('input_ids', 'gate_w', 'gate_b', 'w13', 'w2', 'w13_s', 'w2_s')}
    del _L0_ffn_all

    def _L1_xattn_setup():
        import jax, jax.numpy as jnp
        import numpy as np
        D = 128
        NUM_ITERS = 3
        EPS = 1e-06
        SCALE = D ** (-0.5)

        def rmsnorm(x, w, eps=EPS):
            return x * jax.lax.rsqrt(jnp.mean(x * x, axis=-1, keepdims=True) + eps) * w

        def gru_cell(x, h, wih, whh, bih, bhh):
            gx = x @ wih.T + bih
            gh = h @ whh.T + bhh
            xr, xz, xn = jnp.split(gx, 3, axis=-1)
            hr, hz, hn = jnp.split(gh, 3, axis=-1)
            r = jax.nn.sigmoid(xr + hr)
            z = jax.nn.sigmoid(xz + hz)
            n = jnp.tanh(xn + r * hn)
            return (1.0 - z) * n + z * h
        key = jax.random.key(seed)
        ks = jax.random.split(key, 8)
        B, K, M, d = (8, 64, 512, D)
        w_std = d ** (-0.5)
        return {'slots': jax.random.normal(ks[0], (B, K, d), jnp.float32), 'P': jax.random.normal(ks[1], (B, M, d), jnp.float32), 'Wq': jax.random.normal(ks[2], (d, d), jnp.float32) * w_std, 'Wk': jax.random.normal(ks[3], (d, d), jnp.float32) * w_std, 'Wv': jax.random.normal(ks[4], (d, d), jnp.float32) * w_std, 'gru_wih': jax.random.normal(ks[5], (3 * d, d), jnp.float32) * w_std, 'gru_whh': jax.random.normal(ks[6], (3 * d, d), jnp.float32) * w_std, 'gru_bih': jnp.zeros((3 * d,), jnp.float32), 'gru_bhh': jnp.zeros((3 * d,), jnp.float32), 'slot_norm_w': jnp.ones((d,), jnp.float32), 'input_norm_w': jnp.ones((d,), jnp.float32)}
    _L1_xattn_all = _L1_xattn_setup()
    _L1_xattn_in = {k: v for k, v in _L1_xattn_all.items() if k in ('Wq', 'Wk', 'Wv', 'gru_wih', 'gru_whh', 'gru_bih', 'gru_bhh', 'slot_norm_w', 'input_norm_w')}
    del _L1_xattn_all

    def _L1_ffn_setup():
        import jax, jax.numpy as jnp
        import numpy as np
        import math
        E = 32
        K = 2
        CF = 1.2
        D = 128
        F = 512
        key = jax.random.key(seed)
        ks = jax.random.split(key, 7)
        s = 0.02
        return {'x': jax.random.normal(ks[0], (4, 256, D), jnp.float32), 'gate_w': jax.random.normal(ks[1], (D, E), jnp.float32) * s, 'gate_b': jnp.zeros((E,), jnp.float32), 'w1': jax.random.normal(ks[2], (E, D, F), jnp.float32) * s, 'b1': jnp.zeros((E, F), jnp.float32), 'w2': jax.random.normal(ks[3], (E, F, D), jnp.float32) * s, 'b2': jnp.zeros((E, D), jnp.float32)}
    _L1_ffn_all = _L1_ffn_setup()
    _L1_ffn_in = {k: v for k, v in _L1_ffn_all.items() if k in ('gate_w', 'gate_b', 'w1', 'b1', 'w2', 'b2')}
    del _L1_ffn_all
    return {'x': x, 'ctx_1024': ctx_1024, 'mask_BxS2_bk0': mask_BxS2_bk0, 'mask_BxS_bk0': mask_BxS_bk0, 'g_xattn': g_xattn, 'g_ffn': g_ffn, 'L0_xattn_Wq': _L0_xattn_in['Wq'], 'L0_xattn_Wkv': _L0_xattn_in['Wkv'], 'L0_xattn_Wout': _L0_xattn_in['Wout'], 'L0_xattn_bout': _L0_xattn_in['bout'], 'L0_ffn_input_ids': _L0_ffn_in['input_ids'], 'L0_ffn_gate_w': _L0_ffn_in['gate_w'], 'L0_ffn_gate_b': _L0_ffn_in['gate_b'], 'L0_ffn_w13': _L0_ffn_in['w13'], 'L0_ffn_w2': _L0_ffn_in['w2'], 'L0_ffn_w13_s': _L0_ffn_in['w13_s'], 'L0_ffn_w2_s': _L0_ffn_in['w2_s'], 'L1_xattn_Wq': _L1_xattn_in['Wq'], 'L1_xattn_Wk': _L1_xattn_in['Wk'], 'L1_xattn_Wv': _L1_xattn_in['Wv'], 'L1_xattn_gru_wih': _L1_xattn_in['gru_wih'], 'L1_xattn_gru_whh': _L1_xattn_in['gru_whh'], 'L1_xattn_gru_bih': _L1_xattn_in['gru_bih'], 'L1_xattn_gru_bhh': _L1_xattn_in['gru_bhh'], 'L1_xattn_slot_norm_w': _L1_xattn_in['slot_norm_w'], 'L1_xattn_input_norm_w': _L1_xattn_in['input_norm_w'], 'L1_ffn_gate_w': _L1_ffn_in['gate_w'], 'L1_ffn_gate_b': _L1_ffn_in['gate_b'], 'L1_ffn_w1': _L1_ffn_in['w1'], 'L1_ffn_b1': _L1_ffn_in['b1'], 'L1_ffn_w2': _L1_ffn_in['w2'], 'L1_ffn_b2': _L1_ffn_in['b2']}

def reference(x, ctx_1024, mask_BxS2_bk0, mask_BxS_bk0, g_xattn, g_ffn, L0_xattn_Wq, L0_xattn_Wkv, L0_xattn_Wout, L0_xattn_bout, L0_ffn_input_ids, L0_ffn_gate_w, L0_ffn_gate_b, L0_ffn_w13, L0_ffn_w2, L0_ffn_w13_s, L0_ffn_w2_s, L1_xattn_Wq, L1_xattn_Wk, L1_xattn_Wv, L1_xattn_gru_wih, L1_xattn_gru_whh, L1_xattn_gru_bih, L1_xattn_gru_bhh, L1_xattn_slot_norm_w, L1_xattn_input_norm_w, L1_ffn_gate_w, L1_ffn_gate_b, L1_ffn_w1, L1_ffn_b1, L1_ffn_w2, L1_ffn_b2):
    import jax
    import jax.numpy as jnp

    def _L0_xattn_ref(txt, image, kv_mask, q_mask, Wq, Wkv, Wout, bout):
        import jax, jax.numpy as jnp
        import numpy as np
        B, N_TXT, N_IMG, DIM = (8, 64, 512, 128)
        HEADS, DIM_HEAD = (16, 64)
        INNER = HEADS * DIM_HEAD
        h, d = (HEADS, DIM_HEAD)
        scale = d ** (-0.5)
        b, n2, _ = txt.shape
        n1 = image.shape[1]
        q = (txt @ Wq).reshape(b, n2, h, d).transpose(0, 2, 1, 3)
        kv = image @ Wkv
        k, v = jnp.split(kv, 2, axis=-1)
        k = k.reshape(b, n1, h, d).transpose(0, 2, 1, 3)
        v = v.reshape(b, n1, h, d).transpose(0, 2, 1, 3)
        dots = jnp.einsum('bhid,bhjd->bhij', q, k) * scale
        mask_value = -jnp.finfo(dots.dtype).max
        mask = q_mask[:, None, :, None] & kv_mask[:, None, None, :]
        dots = jnp.where(mask, dots, mask_value)
        attn = jax.nn.softmax(dots, axis=-1)
        out = jnp.einsum('bhij,bhjd->bhid', attn, v)
        out = out.transpose(0, 2, 1, 3).reshape(b, n2, h * d)
        return out @ Wout + bout

    def _L0_ffn_ref(x, input_ids, gate_w, gate_b, w13, w2, w13_s, w2_s):
        import jax, jax.numpy as jnp
        import numpy as np
        from jax import lax
        DIM = 128
        INTER = 64
        N_EXPERTS = 16
        TOPK = 4
        ROUTE_SCALE = 2.5
        VOCAB = 4000

        def _silu_and_mul(gu):
            gate, up = jnp.split(gu, 2, axis=-1)
            return jax.nn.silu(gate) * up
        B, S, D = x.shape
        xt = x.reshape(-1, D)
        T = xt.shape[0]
        scores = jax.nn.sigmoid(xt.astype(jnp.float32) @ gate_w.T)
        biased = scores + gate_b
        _, idx = lax.top_k(biased, TOPK)
        w = jnp.take_along_axis(scores, idx, axis=-1)
        w = w / jnp.sum(w, axis=-1, keepdims=True)
        w = w * ROUTE_SCALE
        comb = jnp.zeros((T, N_EXPERTS), jnp.float32)
        comb = comb.at[jnp.arange(T)[:, None], idx].add(w)
        comb = comb.astype(x.dtype)

        def expert_body(y, args):
            w13_e, w2_e, c_e = args
            h = _silu_and_mul(xt @ w13_e.T)
            return (y + c_e[:, None] * (h @ w2_e.T), None)
        y, _ = lax.scan(expert_body, jnp.zeros_like(xt), (w13, w2, comb.T))
        y = y + _silu_and_mul(xt @ w13_s.T) @ w2_s.T
        return y.astype(x.dtype).reshape(B, S, D)

    def _L1_xattn_ref(slots, P, Wq, Wk, Wv, gru_wih, gru_whh, gru_bih, gru_bhh, slot_norm_w, input_norm_w):
        import jax, jax.numpy as jnp
        import numpy as np
        D = 128
        NUM_ITERS = 3
        EPS = 1e-06
        SCALE = D ** (-0.5)

        def rmsnorm(x, w, eps=EPS):
            return x * jax.lax.rsqrt(jnp.mean(x * x, axis=-1, keepdims=True) + eps) * w

        def gru_cell(x, h, wih, whh, bih, bhh):
            gx = x @ wih.T + bih
            gh = h @ whh.T + bhh
            xr, xz, xn = jnp.split(gx, 3, axis=-1)
            hr, hz, hn = jnp.split(gh, 3, axis=-1)
            r = jax.nn.sigmoid(xr + hr)
            z = jax.nn.sigmoid(xz + hz)
            n = jnp.tanh(xn + r * hn)
            return (1.0 - z) * n + z * h
        Pn = rmsnorm(P, input_norm_w)
        k_proj = Pn @ Wk.T
        v_proj = Pn @ Wv.T
        for _ in range(NUM_ITERS):
            sn = rmsnorm(slots, slot_norm_w)
            q_proj = sn @ Wq.T
            scores = jnp.einsum('bkd,bmd->bkm', q_proj, k_proj) * SCALE
            attn = jax.nn.softmax(scores, axis=-2)
            attn = attn / (jnp.sum(attn, axis=-1, keepdims=True) + EPS)
            updates = jnp.einsum('bkm,bmd->bkd', attn, v_proj)
            slots = gru_cell(updates, slots, gru_wih, gru_whh, gru_bih, gru_bhh)
        return slots

    def _L1_ffn_ref(x, gate_w, gate_b, w1, b1, w2, b2):
        import jax, jax.numpy as jnp
        import numpy as np
        import math
        E = 32
        K = 2
        CF = 1.2
        D = 128
        F = 512
        orig_shape = x.shape
        xt = x.reshape(-1, D)
        T = xt.shape[0]
        C = int(math.ceil(T * K / E * CF))
        logits = xt @ gate_w + gate_b
        probs = jax.nn.softmax(logits, axis=-1)
        top_w, top_i = jax.lax.top_k(probs, K)
        w = top_w / jnp.sum(top_w, axis=-1, keepdims=True)
        flat_e = top_i.reshape(-1)
        oh = jax.nn.one_hot(flat_e, E, dtype=jnp.int32)
        pos_all = jnp.cumsum(oh, axis=0) - 1
        pos = jnp.take_along_axis(pos_all, flat_e[:, None], axis=1)[:, 0]
        valid = pos < C
        pos_d = jnp.where(valid, pos, C)
        x_rep = jnp.repeat(xt, K, axis=0)
        xe = jnp.zeros((E, C, D), x.dtype).at[flat_e, pos_d].add(x_rep, mode='drop')
        he = jax.nn.gelu(jnp.einsum('ecd,edf->ecf', xe, w1) + b1[:, None, :], approximate=False)
        ye = jnp.einsum('ecf,efd->ecd', he, w2) + b2[:, None, :]
        y_flat = ye[flat_e, jnp.minimum(pos, C - 1)] * valid[:, None].astype(x.dtype)
        y = (y_flat.reshape(T, K, D) * w[..., None]).sum(axis=1)
        return y.reshape(orig_shape)
    x = x + jnp.tanh(g_xattn[0]) * _L0_xattn_ref(_layernorm(x, axis=-1), ctx_1024, mask_BxS2_bk0, mask_BxS_bk0, L0_xattn_Wq, L0_xattn_Wkv, L0_xattn_Wout, L0_xattn_bout)
    x = x + jnp.tanh(g_ffn[0]) * _L0_ffn_ref(_layernorm(x, axis=-1), L0_ffn_input_ids, L0_ffn_gate_w, L0_ffn_gate_b, L0_ffn_w13, L0_ffn_w2, L0_ffn_w13_s, L0_ffn_w2_s)
    x = x + jnp.tanh(g_xattn[1]) * _L1_xattn_ref(_layernorm(x, axis=-1), ctx_1024, L1_xattn_Wq, L1_xattn_Wk, L1_xattn_Wv, L1_xattn_gru_wih, L1_xattn_gru_whh, L1_xattn_gru_bih, L1_xattn_gru_bhh, L1_xattn_slot_norm_w, L1_xattn_input_norm_w)
    x = x + jnp.tanh(g_ffn[1]) * _L1_ffn_ref(_layernorm(x, axis=-1), L1_ffn_gate_w, L1_ffn_gate_b, L1_ffn_w1, L1_ffn_b1, L1_ffn_w2, L1_ffn_b2)
    return x

_drawn_inputs = setup_inputs


def setup_inputs(seed=0):
    import zlib

    import numpy as np

    out = dict(_drawn_inputs(seed))
    spreads = {'g_ffn': (-1.0, 0.6),
     'L0_xattn_bout': (0.0, 0.1),
     'L1_xattn_gru_bih': (0.0, 0.376),
     'L1_xattn_gru_bhh': (0.0, 0.587),
     'L1_xattn_slot_norm_w': (1.0, 0.6),
     'L1_xattn_input_norm_w': (1.0, 0.6),
     'L1_ffn_gate_b': (0.0, 0.1),
     'L1_ffn_b1': (0.0, 0.627),
     'L1_ffn_b2': (0.0, 0.453)}
    factors = {'L0_xattn_Wq': 24.594,
     'L0_ffn_gate_w': 8.0,
     'L0_ffn_gate_b': 8.0,
     'L0_ffn_w13': 8.0,
     'L0_ffn_w2': 8.0,
     'L0_ffn_w13_s': 8.0,
     'L0_ffn_w2_s': 8.0,
     'L1_ffn_w1': 5.038}
    for name, (base, spread) in spreads.items():
        noise = np.random.default_rng([zlib.crc32(name.encode()), seed]).standard_normal(out[name].shape)
        drawn = base * np.exp(spread * noise) if base else spread * noise
        out[name] = jnp.asarray(drawn.astype(out[name].dtype))
    for name, factor in factors.items():
        out[name] = (out[name] * factor).astype(out[name].dtype)
    return out
```

```python
from contextlib import ExitStack

import concourse.bass as bass
from concourse import mybir

F32 = mybir.dt.float32
BF16 = mybir.dt.bfloat16
I32 = mybir.dt.int32
U32 = mybir.dt.uint32
U8 = mybir.dt.uint8
ALU = mybir.AluOpType
ACT = mybir.ActivationFunctionType
AX = mybir.AxisListType

B, S, D, M = 16, 56, 128, 1500
T = B * S
HALF = T // 2
NT = T // 128
H, DH = 16, 64
QT = 128 // H
TILES = S // QT
BT = B * TILES
KB, KN = 4, M // 4
KP, KC = 125, 3
ITEMS = BT * KB
BIG = 1e30
E0, F0, TOP0, ROUTE = 16, 64, 4, 2.5
PAIRS = E0 // 2
CP, CC = 125, 12
GB = 8
GROUPS = B // GB
ITERS = 3
E1, F1, TOP1, CAP = 32, 512, 2, 68
FC = F1 // 128
SLOTS = E1 * CAP
ST = SLOTS // 128
TRASH = SLOTS
EARLY = 8


def build_program(nc, t):
    with ExitStack() as ctx:
        def sb(name, shape, dt=F32):
            return ctx.enter_context(nc.sbuf_tensor(name, shape, dt))

        def sem(name):
            return ctx.enter_context(nc.semaphore(name))

        mean_w = sb("mean_w", [128, 128])
        ones = sb("ones", [128, 128])
        ones_b = sb("ones_b", [128, 128], BF16)
        ident = sb("ident", [128, 128])
        before = sb("before", [128, 128])
        before_b = sb("before_b", [128, 128], BF16)
        iota_e = sb("iota_e", [128, E1])
        eps_ln = sb("eps_ln", [128, 1])
        eps_rms = sb("eps_rms", [128, 1])
        key_w = sb("key_w", [CP, 1])
        gates_in = sb("gates_in", [128, 4])
        gates = sb("gates", [128, 4])
        bout = sb("bout", [128, 1])
        xT = sb("xT", [128, T])
        xln_p = sb("xln_p", [128, T + QT])
        xln = xln_p[:, 0:T]
        ln_tiles = sb("ln_tiles", [128, 3 * T])
        cen, sq, rstd = (ln_tiles[:, k * T:(k + 1) * T] for k in range(3))
        folded = sb("folded", [128, 2 * H * 128])
        G = folded[:, 0:H * 128].rearrange("p (h j) -> p h j", h=H)
        MO = folded[:, H * 128:].rearrange("p (h j) -> p h j", h=H)
        MS = sb("MS", [128, 128])
        ymean = sb("ymean", [128, B])
        meanT = sb("meanT", [128, B])
        sumsq = sb("sumsq", [CP, B, CC])
        rkey = sb("rkey", [CP, B, CC])
        qm8 = sb("qm8", [BT, QT], U8)
        keepq = sb("keepq", [BT, QT])
        act_q = sb("act_q", [BT, 1])
        act_k = sb("act_k", [BT, KB])
        any_k = sb("any_k", [BT, 1])
        active = sb("active", [BT, KB])
        prefix = sb("prefix", [BT, KB])
        rowsum = sb("rowsum", [BT, 1])
        rank = sb("rank", [BT, KB])
        firstc = sb("firstc", [BT, KB])
        bstep = sb("bstep", [BT, TILES - 1])
        bidx = sb("bidx", [BT, 1])
        btidx = sb("btidx", [BT, 1])
        lists_w = sb("lists_w", [BT, KB, 2], BF16)
        first_w = sb("first_w", [BT, KB, 128], BF16)
        item_n = sb("item_n", [1, 1], I32)
        stat = sb("stat", [128, 8])
        gw0 = sb("gw0", [128, E0])
        gb0 = sb("gb0", [128, E0])
        ws = sb("ws", [128, 2 * F0])
        w2s = sb("w2s", [F0, 128])
        sc0 = sb("sc0", [128, NT, E0])
        bi0 = sb("bi0", [128, NT, E0])
        hot = sb("hot", [128, NT, E0])
        msk = sb("msk", [128, NT, E0])
        den = sb("den", [128, NT])
        top8 = sb("top8", [128, NT, 8])
        idx8 = sb("idx8", [128, NT, 8], U32)
        idxf = sb("idxf", [128, NT, 8])
        wq1 = sb("wq1", [128, 128])
        wk1 = sb("wk1", [128, 128])
        wv1 = sb("wv1", [128, 128])
        wih = sb("wih", [128, 3 * D])
        whh = sb("whh", [128, 3 * D])
        G1 = sb("G1", [128, 128])
        F1w = sb("F1w", [128, 3 * D])
        bih = sb("bih", [128, 3])
        bhh = sb("bhh", [128, 3])
        hb = sb("hb", [128, 3])
        wslot = sb("wslot", [128, 1])
        wkey = sb("wkey", [128, 1])
        wkey_s = sb("wkey_s", [128, 1])
        mx = sb("mx", [CP, 2, CC])
        sm = sb("sm", [CP, 2, CC])
        gw1 = sb("gw1", [128, E1])
        gb1 = sb("gb1", [128, E1])
        b1T = sb("b1T", [128, E1, FC])
        b2T = sb("b2T", [128, E1])
        r1 = sb("r1", [128, NT])
        r2 = sb("r2", [128, NT])
        valid = sb("valid", [128, TOP1, NT])
        posk = sb("posk", [128, TOP1, NT])
        gidx = sb("gidx", [128, TOP1, NT], I32)
        sidx = sb("sidx", [128, TOP1, NT], I32)
        wk = sb("wk", [128, TOP1, NT])
        trash = sb("trash", [128, TOP1, NT])
        hT = [sb(f"hT{k}", [128, FC, CAP]) for k in range(2)]
        hx = [sb(f"hx{k}", [128, FC, CAP]) for k in range(2)]
        early_w = sb("early_w", [128, EARLY, 2 * F1])
        region = sb("region", [128, GB * CC * 128 * 2])
        work = sb("work", [128, 4 * CC * S + 7 * HALF])
        used = {"region": 0, "work": 0}

        def carve(n, where="region"):
            tile = {"region": region, "work": work}[where]
            used[where] += n
            assert used[where] <= tile.shape[1]
            return tile[:, used[where] - n:used[where]]

        wqT, wkT, wvT, wo = (carve(H // 2 * 128).rearrange("p (h i) -> p h i", i=128) for _ in range(4))
        mctx = [carve(CC * 128) for _ in range(2)]
        msq = [carve(CC * 128) for _ in range(2)]
        ictx = [carve(KC * 128).rearrange("p (c d) -> p c d", c=KC) for _ in range(2)]
        ictxT = [carve(KN) for _ in range(2)]
        hot_r = [carve(ITEMS // 2).bitcast(BF16) for _ in range(KB)]
        iota_r = carve(ITEMS)
        keep_d = carve(BT * QT)
        imask = [carve(96).bitcast(U8) for _ in range(2)]
        km8 = carve(376).bitcast(U8)
        item_bt = carve(ITEMS + 2).bitcast(I32)
        item_blk = carve(ITEMS + 2).bitcast(I32)
        w13 = carve(2 * E0 * F0).rearrange("p (g n) -> p g n", g=2)
        w2p = carve(PAIRS * 128).rearrange("p (e d) -> p e d", e=PAIRS)
        pair_sel = carve(PAIRS * 128).rearrange("p (e d) -> p e d", e=PAIRS)
        combT = carve(T)
        sg = [carve(HALF) for _ in range(2)]
        hh = [carve(HALF) for _ in range(2)]
        Qk = [carve(128, "work") for _ in range(2)]
        maskb = [carve(KN, "work") for _ in range(2)]
        Sm = carve(KN, "work")
        P = carve(KN, "work")
        PT = carve(KC * 128, "work").rearrange("p (c r) -> p c r", c=KC)
        acc = carve(128, "work")
        On = carve(128, "work")
        OT = carve(128, "work")
        ybuf = carve((BT + 1) * QT, "work")
        not_first = carve(ITEMS, "work")
        first_neg = carve(ITEMS, "work")
        keys = region[:CP, 0:GB * CC * 128].rearrange("p (s c) -> p s c", s=GB)
        keysT = region[:, GB * CC * 128:GB * CC * 128 + GB * M].rearrange("p (s c) -> p s c", s=GB)
        used["work"] = 0
        SB = [carve(CC * S, "work").rearrange("p (c s) -> p c s", c=CC) for _ in range(2)]
        AT = [carve(CC * S, "work").rearrange("p (c s) -> p c s", c=CC) for _ in range(2)]
        slots_x, qT, Un, rt, zt, nt, tmp = (carve(HALF, "work") for _ in range(7))
        late_w = region[:, :].rearrange("p (e c) -> p e c", c=2 * F1)
        xtok = folded[:, 0:T].rearrange("p (n d) -> p n d", n=NT)
        rtok = folded[:, T:2 * T].rearrange("p (n d) -> p n d", n=NT)
        ysr = folded[:, 2 * T:2 * T + SLOTS].rearrange("p (n d) -> p n d", n=ST)
        xeT = ln_tiles[:, 0:SLOTS]
        used["work"] = 0
        xe = carve(SLOTS, "work").rearrange("p (n d) -> p n d", n=ST)
        ysT = carve(SLOTS, "work")
        lg, pr, posx = (carve(NT * E1, "work").rearrange("p (n e) -> p n e", n=NT) for _ in range(3))
        oh = [carve(NT * E1, "work").rearrange("p (n e) -> p n e", n=NT) for _ in range(TOP1)]
        ohb = carve(NT * E1 // 2, "work").bitcast(BF16).rearrange("p (n e) -> p n e", n=NT)
        yg = early_w[:, 0:2, 0:T]
        zero = early_w[:, 0:3, :].rearrange("p e c -> p (e c)")[:, 0:SLOTS]

        ps = ctx.enter_context(nc.psum_tensor("ps", [128, 8, 512], F32))

        ld_x = sem("ld_x")
        ld_attn = sem("ld_attn")
        ld_small = sem("ld_small")
        ld_mask = sem("ld_mask")
        ld_mctx = [sem(f"ld_mctx{k}") for k in range(2)]
        ld_item = [sem(f"ld_item{k}") for k in range(2)]
        ld_ffn0 = sem("ld_ffn0")
        ld_keys = [sem(f"ld_keys{s}") for s in range(GB)]
        ld_early = sem("ld_early")
        ld_late = [sem(f"ld_late{n}") for n in range((E1 - EARLY) // 4)]
        st_zero = sem("st_zero")
        st_xe = sem("st_xe")
        ld_xe = sem("ld_xe")
        st_ys = sem("st_ys")
        ld_yg = sem("ld_yg")
        st_out = sem("st_out")
        const = sem("const")
        cstep = sem("cstep")
        gates_ok = sem("gates_ok")
        ln_mean = sem("ln_mean")
        ln_cent = sem("ln_cent")
        ln_sq = sem("ln_sq")
        ln_var = sem("ln_var")
        ln_sd = sem("ln_sd")
        ln_rec = sem("ln_rec")
        ln_out = sem("ln_out")
        x_new = sem("x_new")
        fold_mm = sem("fold_mm")
        fold_ev = sem("fold_ev")
        fold_sum = sem("fold_sum")
        key_sq = sem("key_sq")
        key_ss = sem("key_ss")
        key_sum = sem("key_sum")
        mean_ev = sem("mean_ev")
        ymean_mm = sem("ymean_mm")
        ymean_ev = sem("ymean_ev")
        rk_sd = sem("rk_sd")
        rk_ok = sem("rk_ok")
        plan = sem("plan")
        plan_rs = sem("plan_rs")
        plan_rank = sem("plan_rank")
        plan_hot = sem("plan_hot")
        plan_list = sem("plan_list")
        items_ok = sem("items_ok")
        qk_mm = sem("qk_mm")
        qk_ev = sem("qk_ev")
        s_mm = sem("s_mm")
        mask_ok = sem("mask_ok")
        s_max = sem("s_max")
        m_prev = sem("m_prev")
        m_new = sem("m_new")
        m_neg = sem("m_neg")
        alpha_ok = sem("alpha_ok")
        p_exp = sem("p_exp")
        pt_mm = sem("pt_mm")
        pt_ev = sem("pt_ev")
        o_mm = sem("o_mm")
        l_ok = sem("l_ok")
        acc_ok = sem("acc_ok")
        rl_ok = sem("rl_ok")
        on_ok = sem("on_ok")
        ot_mm = sem("ot_mm")
        ot_ev = sem("ot_ev")
        y_mm = sem("y_mm")
        y_ok = sem("y_ok")
        keep_mm = sem("keep_mm")
        res0 = sem("res0")
        lg0_mm = sem("lg0_mm")
        sc0_ok = sem("sc0_ok")
        rt0 = sem("rt0")
        comb_ok = sem("comb_ok")
        combT_mm = sem("combT_mm")
        combT_ok = sem("combT_ok")
        e0_mm = sem("e0_mm")
        e0_act = sem("e0_act")
        e0_up = sem("e0_up")
        e0_h = sem("e0_h")
        e0_y = sem("e0_y")
        res1 = sem("res1")
        g1_mm = sem("g1_mm")
        g1_ev = sem("g1_ev")
        hb_ok = sem("hb_ok")
        key_n = sem("key_n")
        kt_mm = sem("kt_mm")
        kt_ev = sem("kt_ev")
        sl_ok = sem("sl_ok")
        q_sq = sem("q_sq")
        q_var = sem("q_var")
        q_sd = sem("q_sd")
        q_rec = sem("q_rec")
        q_sn = sem("q_sn")
        q_mm = sem("q_mm")
        q_ok = sem("q_ok")
        a_mm = sem("a_mm")
        a_max = sem("a_max")
        a_sub = sem("a_sub")
        a_exp = sem("a_exp")
        a_sum = sem("a_sum")
        a_rec = sem("a_rec")
        a_att = sem("a_att")
        u_mm = sem("u_mm")
        z_add = sem("z_add")
        z_rec = sem("z_rec")
        u_ok = sem("u_ok")
        gru_mm = sem("gru_mm")
        gru_t = sem("gru_t")
        gru_hn = sem("gru_hn")
        gru_v = sem("gru_v")
        gru_n = sem("gru_n")
        res2 = sem("res2")
        lg1_mm = sem("lg1_mm")
        rt1 = sem("rt1")
        rt1_exp = sem("rt1_exp")
        rt1_hot = sem("rt1_hot")
        pos_mm = sem("pos_mm")
        slot_ok = sem("slot_ok")
        tok_mm = sem("tok_mm")
        tok_ev = sem("tok_ev")
        xe_mm = sem("xe_mm")
        xe_ev = sem("xe_ev")
        h_mm = sem("h_mm")
        h_b = sem("h_b")
        h_ok = sem("h_ok")
        ye_mm = sem("ye_mm")
        ye_ok = sem("ye_ok")
        yt_mm = sem("yt_mm")
        yt_ev = sem("yt_ev")
        out_s = sem("out_s")

        xe_dram = t["xe_scratch"]
        ys_dram = t["ys_scratch"]
        block = ctx.enter_context(nc.Block())

        def half(h):
            return slice(h * HALF, (h + 1) * HALF)

        def bcast(ap, n):
            return ap.unsqueeze(len(ap.shape)).to_broadcast([*ap.shape, n])

        def over_tiles(ap):
            return ap.unsqueeze(1).to_broadcast([ap.shape[0], NT, ap.shape[1]])

        @block.sync
        def _(sp):
            sp.dma_start(xT[:, :], t["xT"]).then_inc(ld_x, 16)
            for r in range(TILES):
                sp.dma_start(km8[r * B:(r + 1) * B, 0:M], t["kv_mask"]).then_inc(ld_mask, 16)
            sp.dma_start(qm8[:, :], t["q_mask"]).then_inc(ld_mask, 16)
            for dst, name in ((wqT, "wqT"), (wkT, "wkT"), (wvT, "wvT"), (wo, "wo")):
                sp.dma_start(dst, t[name]).then_inc(ld_attn, 16)
            ctx_b = t["ctx"].rearrange("b (p c) d -> b p (c d)", p=CP)

            def load_batch(dst, b, done):
                for p0, p1 in ((0, 112), (112, CP)):
                    sp.dma_start(dst[p0:p1, :], ctx_b[bass.ds(b, 1), p0:p1, :].rearrange("a p c -> (a p) c")).then_inc(done, 16)

            for k in range(2):
                load_batch(mctx[k], k, ld_mctx[k])
            with sp.Fori(1, B // 2) as i:
                for k in range(2):
                    sp.wait_ge(mean_ev, i * 2 + k - 1)
                    load_batch(mctx[k], i * 2 + k, ld_mctx[k])
            sp.wait_ge(items_ok, 1)
            n = sp.value_load(item_n[0:1, 0:1], min_val=1, max_val=ITEMS)
            with sp.Fori(0, (n + 1) // 2) as i:
                for k in range(2):
                    sp.wait_ge(y_ok, i * 2 + k + 1)
                    blk = sp.value_load(item_blk[0:1, bass.ds(i * 2 + k, 1)], min_val=0, max_val=B * KB - 1)
                    sp.dma_start(ictx[k][:KP, :, :], t["ctx_blk"][bass.ds(blk, 1), :, :].rearrange("a (p c) d -> (a p) c d", c=KC)).then_inc(ld_item[k], 16)
                    sp.dma_start(ictxT[k], t["ctxT_blk"][bass.ds(blk, 1), :, :].rearrange("a p c -> (a p) c")).then_inc(ld_item[k], 16)
                    sp.dma_start(imask[k][:, 0:KN], t["kv_blk"][bass.ds(blk, 1), :].to_broadcast([128, KN])).then_inc(ld_item[k], 16)
            sp.wait_ge(x_new, 4)
            for g in range(GROUPS):
                for s in range(GB):
                    if g:
                        sp.wait_ge(u_mm, (g * ITERS - 1) * GB + s + 1)
                    load_batch(keys[:, s, :], g * GB + s, ld_keys[s])
            sp.wait_ge(u_mm, GROUPS * ITERS * GB)
            for e in range(0, E1 - EARLY, 4):
                sp.dma_start(late_w[:, e:e + 4, :], t["w12"][:, EARLY + e:EARLY + e + 4, :]).then_inc(ld_late[e // 4], 16)
            sp.wait_ge(st_xe, 16 * TOP1 * NT)
            for j0, j1 in ((0, 8), (8, ST)):
                sp.dma_start(xe[:, j0:j1, :], xe_dram[j0 * 128:j1 * 128, :].rearrange("(n p) d -> p n d", p=128)).then_inc(ld_xe, 16)
            sp.wait_ge(yt_ev, 5)
            sp.dma_start(ys_dram.rearrange("(n p) d -> p n d", p=128), ysr).then_inc(st_ys, 16)
            sp.wait_ge(out_s, 2 * NT)
            sp.dma_start(t["out"].rearrange("(n p) d -> p n d", p=128), xtok).then_inc(st_out, 16)
            sp.wait_ge(st_out, 16)

        @block.gpsimd
        def _(gp):
            gp.memset(mean_w[:, :], 1.0 / D).then_inc(const, 1)
            gp.memset(ones[:, :], 1.0).then_inc(const, 1)
            gp.memset(ones_b[:, :], 1.0).then_inc(const, 1)
            gp.memset(eps_ln[:, :], 1e-5).then_inc(const, 1)
            gp.memset(eps_rms[:, :], 1e-6).then_inc(const, 1)
            gp.memset(key_w[:, :], 1.0 / M).then_inc(const, 1)
            gp.memset(pair_sel, 0.0).then_inc(const, 1)
            gp.memset(ident[:, :], 0.0).then_inc(const, 1)
            gp.wait_ge(const, 8)
            gp.affine_select(out=ident[:, :], in_=ident[:, :], compare_op=ALU.not_equal, fill=1.0, base=0,
                             pattern=[[-1, 128]], channel_multiplier=1).then_inc(const, 1)
            gp.affine_select(out=before[:, :], in_=ones[:, :], compare_op=ALU.is_gt, fill=0.0, base=0,
                             pattern=[[1, 128]], channel_multiplier=-1).then_inc(const, 1)
            gp.affine_select(out=bstep[:, :], in_=ones[:BT, 0:TILES - 1], compare_op=ALU.is_ge, fill=0.0,
                             base=-B, pattern=[[-B, TILES - 1]], channel_multiplier=1).then_inc(const, 1)
            gp.affine_select(out=pair_sel[:E0].rearrange("p e (a i) -> p e a i", a=2),
                             in_=pair_sel[:E0].rearrange("p e (a i) -> p e a i", a=2),
                             compare_op=ALU.not_equal, fill=1.0, base=0,
                             pattern=[[-2, PAIRS], [-1, 2], [0, F0]], channel_multiplier=1).then_inc(const, 1)
            gp.iota(iota_e[:, :], pattern=[[1, E1]], base=0, channel_multiplier=0,
                    allow_small_or_imprecise_dtypes=True).then_inc(const, 1)
            gp.iota(iota_r, pattern=[[1, ITEMS]], base=0, channel_multiplier=0,
                    allow_small_or_imprecise_dtypes=True).then_inc(const, 1)
            gp.iota(btidx[:, :], pattern=[[0, 1]], base=0, channel_multiplier=1,
                    allow_small_or_imprecise_dtypes=True).then_inc(const, 1)
            gp.iota(trash[:, :, :], pattern=[[NT * 128, TOP1], [128, NT]], base=TRASH, channel_multiplier=1,
                    allow_small_or_imprecise_dtypes=True).then_inc(const, 1)
            gp.memset(item_bt[0:1, :], BT).then_inc(const, 1)
            gp.memset(item_blk[0:1, :], 0).then_inc(const, 1)
            gp.wait_ge(const, 18)
            gp.tensor_copy(before_b[:, :], before[:, :]).then_inc(const, 1)
            gp.memset(ybuf, 0.0).then_inc(const, 1)
            gp.memset(acc, 0.0).then_inc(const, 1)
            gp.memset(stat[:, :], 0.0).then_inc(const, 1)
            gp.memset(zero, 0.0).then_inc(const, 1)
            gp.memset(xln_p[:, T:T + QT], 0.0).then_inc(const, 1)
            gp.wait_ge(const, CONSTS)
            gp.dma_start(xe_dram[0:SLOTS, :].rearrange("(p n) d -> p (n d)", p=128), zero).then_inc(st_zero, 16)
            small = [(gates_in[:, 0:2], t["g_xattn"].to_broadcast([128, 2])),
                     (gates_in[:, 2:4], t["g_ffn"].to_broadcast([128, 2])),
                     (bout[:, :], t["bout"]), (gw0[:, :], t["gw0"]), (gb0[:, :], t["gb0"].to_broadcast([128, E0])),
                     (ws[:, :], t["ws"]), (w2s[:, :], t["w2s"]), (wq1[:, :], t["wq1"]), (wk1[:, :], t["wk1"]),
                     (wv1[:, :], t["wv1"]), (wih[:, :], t["wih"]), (whh[:, :], t["whh"]), (bih[:, :], t["bih"]),
                     (bhh[:, :], t["bhh"]), (wslot[:, :], t["wslot"]), (wkey[:, :], t["wkey"]), (gw1[:, :], t["gw1"]),
                     (gb1[:, :], t["gb1"].to_broadcast([128, E1])), (b1T[:, :, :], t["b1T"]), (b2T[:, :], t["b2T"])]
            assert len(small) == SMALL
            for dst, src in small:
                gp.dma_start(dst, src).then_inc(ld_small, 16)
            gp.dma_start(w13, t["w13"]).then_inc(ld_ffn0, 16)
            gp.dma_start(w2p, t["w2p"]).then_inc(ld_ffn0, 16)
            gp.wait_ge(st_zero, 16)
            gp.dma_start(early_w[:, :, :], t["w12"][:, 0:EARLY, :]).then_inc(ld_early, 16)

            with gp.Fori(0, GROUPS * ITERS) as r:
                for s in range(GB):
                    gp.wait_ge(a_rec, r * GB + s + 1)
                    if s >= 2:
                        gp.wait_ge(u_mm, r * GB + s - 1)
                    gp.tensor_tensor(AT[s % 2][:CP], SB[s % 2][:CP], bcast(sm[:, s % 2, :], S), ALU.mult).then_inc(a_att, 1)

            gp.wait_ge(slot_ok, 2)
            gp.wait_ge(tok_ev, 4)
            for k in range(TOP1):
                for j in range(NT):
                    gp.indirect_dma_start(xe_dram, bass.IndirectOffsetOnAxis(ap=sidx[:, k, j:j + 1].bitcast(U32), axis=0),
                                          xtok[:, j, :], None).then_inc(st_xe, 16)
            gp.wait_ge(st_ys, 16)
            for k in range(TOP1):
                for j in range(NT):
                    gp.indirect_dma_start(yg[:, k, j * 128:(j + 1) * 128], None, ys_dram,
                                          bass.IndirectOffsetOnAxis(ap=gidx[:, k, j:j + 1].bitcast(U32), axis=0)).then_inc(ld_yg, 16)

        @block.scalar
        def _(act):
            def ln(k):
                for h in range(2):
                    act.wait_ge(ln_cent, 2 * k + h + 1)
                    act.activation(sq[:, half(h)], cen[:, half(h)], ACT.Square).then_inc(ln_sq, 1)
                for h in range(2):
                    act.wait_ge(ln_var, 2 * k + h + 1)
                    act.activation(rstd[:, half(h)], ps[:, 2 + h, 0:HALF], ACT.Sqrt, bias=eps_ln[:, :]).then_inc(ln_sd, 1)

            act.wait_ge(const, CONSTS)
            ln(0)
            for f in range(2):
                for q in range(4):
                    act.wait_ge(fold_mm, 4 * f + q + 1)
                    dst = (G, MO)[f].rearrange("p (m a) j -> p a m j", a=2)[:, q % 2, 4 * (q // 2):4 * (q // 2) + 4, :]
                    act.activation(dst, ps[:, 4 + q, :].rearrange("p (m j) -> p m j", m=4), ACT.Copy, scale=(DH ** -0.5 if f == 0 else 1.0)).then_inc(fold_ev, 1)

            def square(k, loaded):
                act.wait_ge(ld_mctx[k], loaded)
                act.activation(msq[k][:CP, :], mctx[k][:CP, :], ACT.Square).then_inc(key_sq, 1)

            for k in range(2):
                square(k, 32)
            with act.Fori(1, B // 2) as i:
                for k in range(2):
                    act.wait_ge(key_ss, i * 2 + k - 1)
                    square(k, i * 32 + 32)
            act.wait_ge(key_ss, B)
            act.activation(rkey[:, :, :], sumsq[:, :, :], ACT.Sqrt, bias=eps_rms[:CP, :], scale=1.0 / D).then_inc(rk_sd, 1)
            act.wait_ge(ld_small, 16 * SMALL)
            act.activation(gates[:, :], gates_in[:, :], ACT.Tanh).then_inc(gates_ok, 1)
            act.wait_ge(items_ok, 1)
            n = act.value_load(item_n[0:1, 0:1], min_val=1, max_val=ITEMS)
            with act.Fori(0, (n + 1) // 2) as i:
                for k in range(2):
                    act.wait_ge(qk_mm, i * 2 + k + 1)
                    act.copy(Qk[k], ps[:, 0, 0:128]).then_inc(qk_ev, 1)
                    act.wait_ge(m_neg, i * 2 + k + 1)
                    act.activation(stat[:, 4:5], stat[:, 3:4], ACT.Exp, bias=stat[:, 2:3]).then_inc(alpha_ok, 1)
                    act.activation(P, Sm, ACT.Exp, bias=stat[:, 2:3], accum_out=stat[:, 5:6]).then_inc(p_exp, 1)
                    act.wait_ge(pt_mm, i * 2 + k + 1)
                    act.copy(PT[:KP].rearrange("p c r -> p (c r)"), ps[:KP, 2, 0:KC * 128]).then_inc(pt_ev, 1)
                    act.wait_ge(ot_mm, i * 2 + k + 1)
                    act.copy(OT, ps[:, 4, 0:128]).then_inc(ot_ev, 1)
            ln(1)
            act.wait_ge(lg0_mm, 1)
            act.activation(sc0[:, :, :].rearrange("p n e -> p (n e)"), ps[:, 4, 0:NT * E0], ACT.Sigmoid).then_inc(sc0_ok, 1)
            for j in range(2 * (PAIRS + 1)):
                p = 128 if j // 2 < PAIRS else F0
                act.wait_ge(e0_mm, j + 1)
                if j >= 2:
                    act.wait_ge(e0_up, j - 1)
                act.activation(sg[j % 2][:p, :], ps[:p, 2 * (j % 2), 0:HALF], ACT.Silu).then_inc(e0_act, 1)
            ln(2)
            act.wait_ge(g1_mm, 2)
            act.copy(G1[:, :], ps[:, 4, 0:128]).then_inc(g1_ev, 1)
            act.copy(F1w[:, :], ps[:, 5, 0:3 * D]).then_inc(g1_ev, 1)
            with act.Fori(0, GROUPS) as g:
                for s in range(GB):
                    for c in range(3):
                        act.wait_ge(kt_mm, g * (3 * GB) + 3 * s + c + 1)
                        act.copy(keysT[:, s, 4 * CP * c:4 * CP * (c + 1)], ps[:, 1 + c, 0:4 * CP]).then_inc(kt_ev, 1)
                with act.Fori(0, ITERS) as it:
                    r = act.snap(g * ITERS + it)
                    act.wait_ge(sl_ok, g * (ITERS + 1) + it + 1)
                    act.activation(sq[:, 0:HALF], slots_x, ACT.Square).then_inc(q_sq, 1)
                    act.wait_ge(q_var, r + 1)
                    act.activation(rstd[:, 0:HALF], ps[:, 6, 0:HALF], ACT.Sqrt, bias=eps_rms[:, :]).then_inc(q_sd, 1)
                    act.wait_ge(q_mm, r + 1)
                    act.activation(qT, ps[:, 7, 0:HALF], ACT.Copy, scale=wkey_s[:, :]).then_inc(q_ok, 1)
                    for s in range(GB):
                        act.wait_ge(a_sub, r * GB + s + 1)
                        act.activation(SB[s % 2][:CP], SB[s % 2][:CP], ACT.Exp).then_inc(a_exp, 1)
                    act.wait_ge(gru_mm, r * 2 + 1)
                    act.activation(nt, ps[:, 3, 0:HALF], ACT.Identity, bias=bhh[:, 2:3]).then_inc(gru_hn, 1)
                    act.wait_ge(gru_mm, r * 2 + 2)
                    act.activation(rt, ps[:, 0, 0:HALF], ACT.Tanh, bias=hb[:, 0:1], scale=0.5).then_inc(gru_t, 1)
                    act.activation(zt, ps[:, 1, 0:HALF], ACT.Tanh, bias=hb[:, 1:2], scale=0.5).then_inc(gru_t, 1)
                    act.wait_ge(gru_v, r * 4 + 2)
                    act.activation(nt, tmp, ACT.Tanh, bias=bih[:, 2:3]).then_inc(gru_n, 1)
            ln(3)
            act.wait_ge(rt1, 3)
            act.activation(pr, lg, ACT.Exp).then_inc(rt1_exp, 1)
            for c in range(4):
                act.wait_ge(tok_mm, c + 1)
                j0, j1 = ((0, 4), (4, NT))[c % 2]
                dst = (xtok, rtok)[c // 2][:, j0:j1, :].rearrange("p n d -> p (n d)")
                act.copy(dst, ps[:, 4 + c, 0:(j1 - j0) * 128]).then_inc(tok_ev, 1)
            for c in range(5):
                w = min(512, SLOTS - 512 * c)
                act.wait_ge(xe_mm, c + 1)
                act.copy(xeT[:, 512 * c:512 * c + w], ps[:, 4 + c % 2, 0:w]).then_inc(xe_ev, 1)
            for e in range(E1):
                act.wait_ge(h_b, e + 1)
                if e >= 2:
                    act.wait_ge(ye_mm, e - 1)
                act.activation(hT[e % 2][:, :, :], hx[e % 2][:, :, :], ACT.Gelu).then_inc(h_ok, 1)
            for c in range(5):
                j0, j1 = 4 * c, min(4 * c + 4, ST)
                act.wait_ge(yt_mm, c + 1)
                act.copy(ysr[:, j0:j1, :].rearrange("p n d -> p (n d)"), ps[:, 6 + c % 2, 0:(j1 - j0) * 128]).then_inc(yt_ev, 1)

        @block.vector
        def _(v):
            def ln(k):
                for h in range(2):
                    v.wait_ge(ln_mean, 2 * k + h + 1)
                    v.tensor_tensor(cen[:, half(h)], xT[:, half(h)], ps[:, h, 0:HALF], ALU.subtract).then_inc(ln_cent, 1)
                for h in range(2):
                    v.wait_ge(ln_sd, 2 * k + h + 1)
                    v.reciprocal(rstd[:, half(h)], rstd[:, half(h)]).then_inc(ln_rec, 1)
                for h in range(2):
                    v.wait_ge(ln_rec, 2 * k + h + 1)
                    v.tensor_tensor(xln[:, half(h)], cen[:, half(h)], rstd[:, half(h)], ALU.mult).then_inc(ln_out, 1)

            def chain(signal):
                count = [0]

                def step(ins, wait=True):
                    count[0] += 1
                    ins.then_inc(signal, 1)
                    if wait:
                        v.wait_ge(signal, count[0])

                return step

            v.wait_ge(const, CONSTS)
            v.wait_ge(ld_x, 16)
            ln(0)
            step = chain(plan)
            v.wait_ge(ld_mask, 16 * (TILES + 1))
            step(v.tensor_copy(keepq[:, :], qm8[:, :]))
            step(v.tensor_reduce(act_q[:, :], keepq[:, :], AX.X, ALU.max))
            step(v.tensor_reduce(act_k[:, :], km8[:BT, 0:M].rearrange("p (k m) -> p k m", k=KB), AX.X, ALU.max))
            step(v.tensor_reduce(any_k[:, :], act_k[:, :], AX.X, ALU.max))
            step(v.tensor_scalar(keepq[:, :], keepq[:, :], any_k[:, 0:1], None, ALU.mult))
            step(v.tensor_scalar(active[:, :], act_k[:, :], act_q[:, 0:1], None, ALU.mult))
            step(v.memset(prefix[:, 0:1], 0.0))
            for b in range(1, KB):
                step(v.tensor_tensor(prefix[:, b:b + 1], prefix[:, b - 1:b], active[:, b - 1:b], ALU.add))
            v.tensor_reduce(rowsum[:, :], active[:, :], AX.X, ALU.add).then_inc(plan_rs, 1)
            step(v.tensor_scalar(firstc[:, :], prefix[:, :], 0.0, None, ALU.is_equal))
            step(v.tensor_tensor(firstc[:, :], firstc[:, :], active[:, :], ALU.mult))
            step(v.tensor_reduce(bidx[:, :], bstep[:, :], AX.X, ALU.add))
            step(v.scalar_tensor_tensor(btidx[:, :], bidx[:, :], -float(B), btidx[:, :], ALU.mult, ALU.add))
            for b in range(KB):
                step(v.tensor_scalar(lists_w[:, b, 1:2], btidx[:, :], float(KB), float(b), ALU.mult, ALU.add), wait=False)
                step(v.tensor_copy(first_w[:, b, :], firstc[:, b:b + 1].to_broadcast([BT, 128])), wait=False)
            step(v.scalar_tensor_tensor(btidx[:, :], btidx[:, :], float(TILES), bidx[:, :], ALU.mult, ALU.add))
            for b in range(KB):
                step(v.tensor_scalar(lists_w[:, b, 0:1], btidx[:, :], float(-BT), None, ALU.add))
            v.wait_ge(plan_rank, 2)
            step(v.tensor_scalar(rank[:, :], prefix[:, :], ps[:BT, 2, 0:1], None, ALU.add))
            for b in range(KB):
                v.tensor_scalar(hot_r[b][:BT, :], iota_r[:BT, :], rank[:, b:b + 1], active[:, b:b + 1],
                                ALU.is_equal, ALU.mult).then_inc(plan_hot, 1)
            v.tensor_tensor(keep_d[:BT, :].rearrange("p (b t q) -> p t b q", t=TILES, q=QT),
                            bcast(ident[:BT, 0:BT].rearrange("p (t b) -> p t b", t=TILES), QT),
                            keepq[:, :].unsqueeze(1).unsqueeze(1).to_broadcast([BT, TILES, B, QT]), ALU.mult).then_inc(plan_hot, 1)
            v.wait_ge(plan_list, 1)
            step(v.tensor_scalar(item_bt[0:1, 0:ITEMS], ps[0:1, 4, 0:ITEMS], float(BT), None, ALU.add))
            step(v.tensor_copy(item_blk[0:1, 0:ITEMS], ps[0:1, 5, 0:ITEMS]))
            step(v.tensor_scalar(not_first, ps[:, 6, 0:ITEMS], -1.0, 1.0, ALU.mult, ALU.add))
            step(v.tensor_scalar(first_neg, ps[:, 6, 0:ITEMS], -BIG, None, ALU.mult))
            v.tensor_scalar(item_n[:, :], ps[0:1, 2, 1:2], 1.0, None, ALU.max).then_inc(items_ok, 1)

            def key_sums(k, b):
                v.wait_ge(key_sq, b + 1)
                v.tensor_reduce(sumsq[:, bass.ds(b, 1), :], msq[k][:CP, :].rearrange("p (a c d) -> p a c d", a=1, d=D),
                                AX.X, ALU.add).then_inc(key_ss, 1)
                v.wait_ge(key_sum, b + 1)
                v.tensor_copy(meanT[:, bass.ds(b, 1)], ps[:, (3, 1)[k], 0:1]).then_inc(mean_ev, 1)

            with v.Fori(0, B // 2) as i:
                for k in range(2):
                    key_sums(k, v.snap(i * 2 + k))
            v.wait_ge(rk_sd, 1)
            v.reciprocal(rkey[:, :, :], rkey[:, :, :]).then_inc(rk_ok, 1)
            v.wait_ge(fold_ev, 8)
            v.tensor_reduce(MS[:, :], MO.rearrange("p h j -> p j h"), AX.X, ALU.add).then_inc(fold_sum, 1)
            v.wait_ge(ymean_mm, 1)
            v.tensor_copy(ymean[:, :], ps[:, 7, 0:B]).then_inc(ymean_ev, 1)

            n = v.value_load(item_n[0:1, 0:1], min_val=1, max_val=ITEMS)
            v.sem_inc(y_ok, 2)
            with v.Fori(0, (n + 1) // 2) as i:
                for k in range(2):
                    j = v.snap(i * 2 + k)
                    bt = v.value_load(item_bt[0:1, bass.ds(j, 1)], min_val=0, max_val=BT)
                    v.wait_ge(ld_item[k], i * 48 + 48)
                    v.tensor_scalar(maskb[k], imask[k][:, 0:KN], -1.0, BIG, ALU.add, ALU.mult).then_inc(mask_ok, 1)
                    v.wait_ge(mask_ok, j + 1)
                    v.wait_ge(s_mm, j + 1)
                    v.scalar_tensor_tensor(stat[:, 3:4], stat[:, 0:1], not_first[:, bass.ds(j, 1)],
                                           first_neg[:, bass.ds(j, 1)], ALU.mult, ALU.add).then_inc(m_prev, 1)
                    v.tensor_tensor_reduce(Sm, ps[:, 1, 0:KN], maskb[k], 1.0, -3e38, ALU.add, ALU.max,
                                           stat[:, 7:8]).then_inc(s_max, 1)
                    v.wait_ge(m_prev, j + 1)
                    v.wait_ge(s_max, j + 1)
                    v.tensor_tensor(stat[:, 0:1], stat[:, 7:8], stat[:, 3:4], ALU.max).then_inc(m_new, 1)
                    v.wait_ge(m_new, j + 1)
                    v.tensor_scalar(stat[:, 2:3], stat[:, 0:1], -1.0, None, ALU.mult).then_inc(m_neg, 1)
                    v.wait_ge(alpha_ok, j + 1)
                    v.wait_ge(p_exp, j + 1)
                    v.scalar_tensor_tensor(stat[:, 1:2], stat[:, 1:2], stat[:, 4:5], stat[:, 5:6],
                                           ALU.mult, ALU.add).then_inc(l_ok, 1)
                    v.wait_ge(l_ok, j + 1)
                    v.reciprocal(stat[:, 6:7], stat[:, 1:2]).then_inc(rl_ok, 1)
                    v.wait_ge(o_mm, j + 1)
                    v.scalar_tensor_tensor(acc, acc, stat[:, 4:5], ps[:, 3, 0:128],
                                           ALU.mult, ALU.add).then_inc(acc_ok, 1)
                    v.wait_ge(acc_ok, j + 1)
                    v.wait_ge(rl_ok, j + 1)
                    v.tensor_scalar(On, acc, stat[:, 6:7], None, ALU.mult).then_inc(on_ok, 1)
                    v.wait_ge(y_mm, j + 1)
                    v.tensor_copy(ybuf[:, bass.ds(bt * QT, QT)], ps[:, 5, 0:QT]).then_inc(y_ok, 1)
            v.wait_ge(y_ok, ((n + 1) // 2) * 2 + 2)
            v.wait_ge(gates_ok, 1)
            v.wait_ge(ymean_ev, 1)
            v.wait_ge(keep_mm, 1)
            y = ybuf[:, 0:T]
            y3 = y.rearrange("p (b s) -> p b s", b=B)
            step = chain(res0)
            step(v.tensor_tensor(y3, y3, bcast(ymean[:, :], S), ALU.subtract))
            step(v.tensor_tensor(y[:, half(0)], y[:, half(0)], ps[:, 6, 0:HALF], ALU.mult), wait=False)
            step(v.tensor_tensor(y[:, half(1)], y[:, half(1)], ps[:, 7, 0:HALF], ALU.mult))
            step(v.tensor_tensor(y3, y3, bcast(ymean[:, :], S), ALU.add))
            step(v.tensor_scalar(y, y, bout[:, 0:1], gates[:, 0:1], ALU.add, ALU.mult))
            for h in range(2):
                v.tensor_tensor(xT[:, half(h)], xT[:, half(h)], y[:, half(h)], ALU.add).then_inc(x_new, 1)
            v.wait_ge(x_new, 2)
            ln(1)

            step = chain(rt0)
            v.wait_ge(sc0_ok, 1)
            step(v.tensor_tensor(bi0[:, :, :], sc0[:, :, :], over_tiles(gb0[:, :]), ALU.add))
            for j in range(NT):
                step(v.max(top8[:, j, :], bi0[:, j, :]), wait=j == NT - 1)
            for j in range(NT):
                step(v.max_index(idx8[:, j, :], top8[:, j, :], bi0[:, j, :]), wait=j == NT - 1)
            step(v.tensor_copy(idxf[:, :, :], idx8[:, :, :]))
            step(v.tensor_tensor(msk[:, :, :], over_tiles(iota_e[:, 0:E0]), bcast(idxf[:, :, 0], E0), ALU.is_equal))
            for k in range(1, TOP0):
                step(v.tensor_tensor(hot[:, :, :], over_tiles(iota_e[:, 0:E0]), bcast(idxf[:, :, k], E0), ALU.is_equal))
                step(v.tensor_tensor(msk[:, :, :], msk[:, :, :], hot[:, :, :], ALU.add))
            step(v.tensor_tensor(msk[:, :, :], msk[:, :, :], sc0[:, :, :], ALU.mult))
            step(v.tensor_reduce(den[:, :], msk[:, :, :], AX.X, ALU.add))
            step(v.reciprocal(den[:, :], den[:, :]))
            step(v.tensor_scalar(den[:, :], den[:, :], ROUTE, None, ALU.mult))
            v.tensor_tensor(msk[:, :, :], msk[:, :, :], bcast(den[:, :], E0), ALU.mult).then_inc(comb_ok, 1)
            v.wait_ge(combT_mm, 1)
            for h in range(2):
                v.tensor_copy(combT[:E0, half(h)], ps[:E0, 4 + h, 0:HALF]).then_inc(combT_ok, 1)
            for j in range(2 * (PAIRS + 1)):
                p = 128 if j // 2 < PAIRS else F0
                v.wait_ge(e0_act, j + 1)
                if j >= 2:
                    v.wait_ge(e0_y, j - 1)
                v.tensor_tensor(hh[j % 2][:p, :], sg[j % 2][:p, :], ps[:p, 2 * (j % 2) + 1, 0:HALF], ALU.mult).then_inc(e0_up, 1)
                v.wait_ge(e0_up, j + 1)
                if j // 2 < PAIRS:
                    v.tensor_tensor(hh[j % 2], hh[j % 2], ps[:, 6 + j % 2, 0:HALF], ALU.mult).then_inc(e0_h, 1)
            v.wait_ge(e0_y, 2 * (PAIRS + 1))
            for h in range(2):
                v.scalar_tensor_tensor(xT[:, half(h)], ps[:, 4 + h, 0:HALF], gates[:, 2:3], xT[:, half(h)],
                                       ALU.mult, ALU.add).then_inc(x_new, 1)
            v.wait_ge(x_new, 4)
            ln(2)

            v.tensor_scalar(hb[:, :], bih[:, :], 0.5, None, ALU.mult).then_inc(hb_ok, 1)
            v.wait_ge(hb_ok, 1)
            v.scalar_tensor_tensor(hb[:, :], bhh[:, :], 0.5, hb[:, :], ALU.mult, ALU.add).then_inc(hb_ok, 1)
            v.tensor_scalar(wkey_s[:, :], wkey[:, :], float(D) ** -0.5, None, ALU.mult).then_inc(hb_ok, 1)
            v.wait_ge(rk_ok, 1)
            v.wait_ge(ln_out, 6)
            with v.Fori(0, GROUPS) as g:
                for s in range(GB):
                    v.wait_ge(ld_keys[s], g * 32 + 32)
                    k4 = keys[:, s, :].rearrange("p (a c d) -> p a c d", a=1, d=D)
                    v.tensor_tensor(k4, k4, bcast(rkey[:, bass.ds(g * GB + s, 1), :], D), ALU.mult).then_inc(key_n, 1)
                v.tensor_copy(slots_x, xln[:, bass.ds(g * HALF, HALF)]).then_inc(sl_ok, 1)
                with v.Fori(0, ITERS) as it:
                    r = v.snap(g * ITERS + it)
                    v.wait_ge(q_sd, r + 1)
                    v.reciprocal(rstd[:, 0:HALF], rstd[:, 0:HALF]).then_inc(q_rec, 1)
                    v.wait_ge(q_rec, r + 1)
                    v.scalar_tensor_tensor(cen[:, 0:HALF], slots_x, wslot[:, 0:1], rstd[:, 0:HALF],
                                           ALU.mult, ALU.mult).then_inc(q_sn, 1)
                    for s in range(GB):
                        bank = 2 + 2 * (s % 2)
                        scores = ps[:CP, bank:bank + 2, 0:CC // 2 * S].rearrange("p a (c s) -> p a c s", s=S)
                        top = mx[:, s % 2, :].rearrange("p (a c) -> p a c", a=2)
                        v.wait_ge(a_mm, r * GB + s + 1)
                        v.tensor_reduce(top, scores, AX.X, ALU.max).then_inc(a_max, 1)
                        v.wait_ge(a_max, r * GB + s + 1)
                        if s >= 2:
                            v.wait_ge(a_att, r * GB + s - 1)
                        v.tensor_tensor(SB[s % 2][:CP].rearrange("p (a c) s -> p a c s", a=2), scores, bcast(top, S),
                                        ALU.subtract).then_inc(a_sub, 1)
                        v.wait_ge(a_exp, r * GB + s + 1)
                        v.tensor_reduce(sm[:, s % 2, :], SB[s % 2][:CP], AX.X, ALU.add).then_inc(a_sum, 1)
                        v.wait_ge(a_sum, r * GB + s + 1)
                        v.reciprocal(sm[:, s % 2, :], sm[:, s % 2, :]).then_inc(a_rec, 1)
                    v.wait_ge(u_mm, r * GB + GB)
                    v.tensor_scalar(tmp, ps[:, 7, 0:HALF], 1e-6, None, ALU.add).then_inc(z_add, 1)
                    v.wait_ge(z_add, r + 1)
                    v.reciprocal(tmp, tmp).then_inc(z_rec, 1)
                    v.wait_ge(z_rec, r + 1)
                    v.scalar_tensor_tensor(Un, ps[:, 6, 0:HALF], wkey[:, 0:1], tmp, ALU.mult, ALU.mult).then_inc(u_ok, 1)
                    v.wait_ge(gru_hn, r + 1)
                    v.wait_ge(gru_t, r * 2 + 2)
                    v.scalar_tensor_tensor(tmp, rt, 1.0, nt, ALU.add, ALU.mult).then_inc(gru_v, 1)
                    v.wait_ge(gru_v, r * 4 + 1)
                    v.scalar_tensor_tensor(tmp, tmp, 0.5, ps[:, 2, 0:HALF], ALU.mult, ALU.add).then_inc(gru_v, 1)
                    v.wait_ge(gru_n, r + 1)
                    v.tensor_tensor(rt, slots_x, nt, ALU.subtract).then_inc(gru_v, 1)
                    v.wait_ge(gru_v, r * 4 + 3)
                    v.scalar_tensor_tensor(rt, zt, 1.0, rt, ALU.add, ALU.mult).then_inc(gru_v, 1)
                    v.wait_ge(gru_v, r * 4 + 4)
                    v.scalar_tensor_tensor(slots_x, rt, 0.5, nt, ALU.mult, ALU.add).then_inc(sl_ok, 1)
                v.wait_ge(sl_ok, g * (ITERS + 1) + ITERS + 1)
                v.scalar_tensor_tensor(xT[:, bass.ds(g * HALF, HALF)], slots_x, gates[:, 1:2],
                                       xT[:, bass.ds(g * HALF, HALF)], ALU.mult, ALU.add).then_inc(x_new, 1)
                v.wait_ge(x_new, g + 5)
            ln(3)

            step = chain(rt1)
            v.wait_ge(lg1_mm, 1)
            logits = ps[:, 0, 0:NT * E1].rearrange("p (n e) -> p n e", n=NT)
            step(v.tensor_tensor(lg, logits, over_tiles(gb1[:, :]), ALU.add))
            step(v.tensor_reduce(r1[:, :], lg, AX.X, ALU.max))
            step(v.tensor_tensor(lg, lg, bcast(r1[:, :], E1), ALU.subtract))
            v.wait_ge(rt1_exp, 1)
            step(v.tensor_reduce(r2[:, :], pr, AX.X, ALU.add))
            step(v.reciprocal(r2[:, :], r2[:, :]))
            step(v.tensor_tensor(pr, pr, bcast(r2[:, :], E1), ALU.mult))
            for j in range(NT):
                step(v.max(top8[:, j, :], pr[:, j, :]), wait=j == NT - 1)
            for j in range(NT):
                step(v.max_index(idx8[:, j, :], top8[:, j, :], pr[:, j, :]), wait=j == NT - 1)
            step(v.tensor_copy(idxf[:, :, :], idx8[:, :, :]))
            for k in range(TOP1):
                step(v.tensor_tensor(oh[k], over_tiles(iota_e[:, :]), bcast(idxf[:, :, k], E1), ALU.is_equal))
            v.tensor_tensor(ohb, oh[0], oh[1], ALU.add).then_inc(rt1_hot, 1)
            v.wait_ge(pos_mm, 1)
            places = ps[:, 1, 0:NT * E1].rearrange("p (n e) -> p n e", n=NT)
            for k in range(TOP1):
                step(v.tensor_tensor(posx, oh[k], places, ALU.mult))
                step(v.tensor_reduce(posk[:, k, :], posx, AX.X, ALU.add))
            step(v.tensor_scalar(valid[:, :, :], posk[:, :, :], float(CAP), None, ALU.is_lt))
            for k in range(TOP1):
                step(v.scalar_tensor_tensor(posk[:, k, :], idxf[:, :, k], float(CAP), posk[:, k, :], ALU.mult, ALU.add))
            step(v.tensor_tensor(posk[:, :, :], posk[:, :, :], valid[:, :, :], ALU.mult))
            v.tensor_copy(gidx[:, :, :], posk[:, :, :]).then_inc(slot_ok, 1)
            step(v.tensor_tensor(wk[:, :, :], trash[:, :, :], valid[:, :, :], ALU.mult))
            step(v.tensor_tensor(wk[:, :, :], trash[:, :, :], wk[:, :, :], ALU.subtract))
            v.tensor_tensor(sidx[:, :, :], posk[:, :, :], wk[:, :, :], ALU.add).then_inc(slot_ok, 1)
            step(v.tensor_tensor(r1[:, :], top8[:, :, 0], top8[:, :, 1], ALU.add))
            step(v.reciprocal(r1[:, :], r1[:, :]))
            v.wait_ge(slot_ok, 2)
            for k in range(TOP1):
                step(v.scalar_tensor_tensor(wk[:, k, :], top8[:, :, k], gates[:, 3:4], r1[:, :], ALU.mult, ALU.mult))
            step(v.tensor_tensor(wk[:, :, :], wk[:, :, :], valid[:, :, :], ALU.mult))
            for e in range(E1):
                v.wait_ge(h_mm, e + 1)
                if e >= 2:
                    v.wait_ge(h_ok, e - 1)
                v.tensor_tensor(hx[e % 2][:, :, :], ps[:, e % 2, 0:FC * CAP].rearrange("p (c n) -> p c n", c=FC),
                                bcast(b1T[:, e, :], CAP), ALU.add).then_inc(h_b, 1)
                if e % 4 == 3:
                    g = e // 4
                    v.wait_ge(ye_mm, e + 1)
                    v.tensor_tensor(ysT[:, 4 * g * CAP:4 * (g + 1) * CAP].rearrange("p (c n) -> p c n", c=4),
                                    ps[:, 2 + g % 2, 0:4 * CAP].rearrange("p (c n) -> p c n", c=4),
                                    bcast(b2T[:, 4 * g:4 * g + 4], CAP), ALU.add).then_inc(ye_ok, 1)
            v.wait_ge(ld_yg, 16 * TOP1 * NT)
            v.wait_ge(st_xe, 16 * TOP1 * NT)
            for j in range(NT):
                v.scalar_tensor_tensor(xtok[:, j, :], yg[:, 0, j * 128:(j + 1) * 128], wk[:, 0, j:j + 1], rtok[:, j, :],
                                       ALU.mult, ALU.add).then_inc(out_s, 1)
            v.wait_ge(out_s, NT)
            for j in range(NT):
                v.scalar_tensor_tensor(xtok[:, j, :], yg[:, 1, j * 128:(j + 1) * 128], wk[:, 1, j:j + 1], xtok[:, j, :],
                                       ALU.mult, ALU.add).then_inc(out_s, 1)

        @block.tensor
        def _(pe):
            def ln(k):
                for h in range(2):
                    if k:
                        pe.wait_ge(x_new, 6 if k == 3 else 2 * k - 1 + h)
                    pe.matmul(ps[:, h, 0:HALF], mean_w[:, :], xT[:, half(h)], start=True, stop=True).then_inc(ln_mean, 1)
                for h in range(2):
                    pe.wait_ge(ln_sq, 2 * k + h + 1)
                    pe.matmul(ps[:, 2 + h, 0:HALF], mean_w[:, :], sq[:, half(h)], start=True, stop=True).then_inc(ln_var, 1)

            pe.wait_ge(const, CONSTS)
            pe.wait_ge(ld_x, 16)
            ln(0)
            pe.wait_ge(ld_attn, 64)
            for f, (left, right) in enumerate(((wqT, wkT), (wvT, wo))):
                for q in range(4):
                    if f:
                        pe.wait_ge(fold_ev, q + 1)
                    r0 = DH * (q % 2)
                    for m in range(4):
                        pair = 4 * (q // 2) + m
                        mm = pe.matmul(ps[:, 4 + q, m * 128:(m + 1) * 128], left[r0:r0 + DH, pair, :],
                                       right[r0:r0 + DH, pair, :], start=True, stop=True)
                    mm.then_inc(fold_mm, 1)
            pe.wait_ge(plan_rs, 1)
            pe.wait_ge(ln_sd, 1)
            pe.matmul(ps[:BT, 2, 0:1], before[:BT, 0:BT], rowsum[:, :], start=True, stop=True).then_inc(plan_rank, 1)
            pe.matmul(ps[0:1, 2, 1:2], ones[:BT, 0:1], rowsum[:, :], start=True, stop=True).then_inc(plan_rank, 1)
            pe.wait_ge(plan_hot, KB)
            pe.wait_ge(plan, PLAN_LISTS)
            pe.wait_ge(fold_ev, 8)
            for bank, left in ((4, lambda b: lists_w[:, b, 0:1]), (5, lambda b: lists_w[:, b, 1:2]), (6, lambda b: first_w[:, b, :])):
                rows = 128 if bank == 6 else 1
                for b in range(KB):
                    mm = pe.matmul(ps[:rows, bank, 0:ITEMS], left(b), hot_r[b][:BT, :], start=(b == 0), stop=(b == KB - 1))
            mm.then_inc(plan_list, 1)

            def key_mean(k, loaded):
                pe.wait_ge(ld_mctx[k], loaded)
                for c in range(CC):
                    mm = pe.matmul(ps[:, (3, 1)[k], 0:1], mctx[k][:CP, c * 128:(c + 1) * 128], key_w[:, :],
                                   start=(c == 0), stop=(c == CC - 1))
                mm.then_inc(key_sum, 1)

            pe.wait_ge(ln_sd, 2)
            for k in range(2):
                key_mean(k, 32)
            with pe.Fori(1, B // 2) as i:
                for k in range(2):
                    pe.wait_ge(mean_ev, i * 2 + k - 1)
                    key_mean(k, i * 32 + 32)
            pe.wait_ge(mean_ev, B)
            pe.wait_ge(fold_sum, 1)
            pe.matmul(ps[:, 7, 0:B], MS[:, :], meanT[:, :], start=True, stop=True).then_inc(ymean_mm, 1)

            pe.wait_ge(items_ok, 1)
            pe.wait_ge(ln_out, 2)
            n = pe.value_load(item_n[0:1, 0:1], min_val=1, max_val=ITEMS)
            with pe.Fori(0, (n + 1) // 2) as i:
                for k in range(2):
                    j = pe.snap(i * 2 + k)
                    bt = pe.value_load(item_bt[0:1, bass.ds(j, 1)], min_val=0, max_val=BT)
                    pe.wait_ge(y_ok, j + 2)
                    for h in range(H):
                        mm = pe.matmul(ps[:, 0, h * QT:(h + 1) * QT], G[:, h, :],
                                       xln_p[:, bass.ds(bt * QT, QT)], start=True, stop=True)
                    mm.then_inc(qk_mm, 1)
                    pe.wait_ge(qk_ev, j + 1)
                    pe.wait_ge(ld_item[k], i * 48 + 48)
                    pe.matmul(ps[:, 1, 0:KN], Qk[k], ictxT[k], start=True, stop=True).then_inc(s_mm, 1)
                    pe.wait_ge(p_exp, j + 1)
                    for c in range(KC):
                        mm = pe.transpose(ps[:KP, 2, c * 128:(c + 1) * 128],
                                          P.rearrange("p (m c) -> p c m", c=KC)[:, c, :], ident[:, :])
                    mm.then_inc(pt_mm, 1)
                    pe.wait_ge(pt_ev, j + 1)
                    for c in range(KC):
                        mm = pe.matmul(ps[:, 3, 0:128], PT[:KP, c, :], ictx[k][:KP, c, :], start=(c == 0), stop=(c == KC - 1))
                    mm.then_inc(o_mm, 1)
                    pe.wait_ge(on_ok, j + 1)
                    pe.transpose(ps[:, 4, 0:128], On, ident[:, :]).then_inc(ot_mm, 1)
                    pe.wait_ge(ot_ev, j + 1)
                    for h in range(H):
                        mm = pe.matmul(ps[:, 5, 0:QT], MO[:, h, :], OT[:, h * QT:(h + 1) * QT], start=(h == 0), stop=(h == H - 1))
                    mm.then_inc(y_mm, 1)
            pe.wait_ge(plan_hot, KB + 1)
            pe.wait_ge(ymean_ev, 1)
            for h in range(2):
                mm = pe.matmul(ps[:, 6 + h, 0:HALF], ones[:BT, :], keep_d[:BT, half(h)], start=True, stop=True)
            mm.then_inc(keep_mm, 1)
            ln(1)

            pe.wait_ge(ld_small, 16 * SMALL)
            pe.wait_ge(ln_out, 4)
            for j in range(NT):
                mm = pe.matmul(ps[:, 4, j * E0:(j + 1) * E0], xln[:, j * 128:(j + 1) * 128], gw0[:, :], start=True, stop=True)
            mm.then_inc(lg0_mm, 1)
            pe.wait_ge(comb_ok, 1)
            for j in range(NT):
                c = j * 128
                for c0, c1 in ((c, min(c + 128, max(c, HALF))), (max(c, min(HALF, c + 128)), c + 128)):
                    if c1 > c0:
                        mm = pe.transpose(ps[:E0, 4 + c0 // HALF, c0 % HALF:c0 % HALF + c1 - c0],
                                          msk[c0 - c:c1 - c, j, :], ident[c0 - c:c1 - c, c0 - c:c1 - c])
            mm.then_inc(combT_mm, 1)
            pe.wait_ge(ld_ffn0, 32)

            def shares(j):
                pair, h = divmod(j, 2)
                p = 128 if pair < PAIRS else F0
                if j >= 2:
                    pe.wait_ge(e0_up, j - 1)
                    if j - 2 < 2 * PAIRS:
                        pe.wait_ge(e0_h, j - 1)
                for g in range(2):
                    w = w13[:, g, pair * 2 * F0:(pair + 1) * 2 * F0] if pair < PAIRS else ws[:, g * F0:(g + 1) * F0]
                    mm = pe.matmul(ps[:p, 2 * (j % 2) + g, 0:HALF], w, xln[:, half(h)], start=True, stop=True)
                if pair < PAIRS:
                    pe.wait_ge(combT_ok, 2)
                    mm = pe.matmul(ps[:, 6 + j % 2, 0:HALF], pair_sel[:E0, pair, :], combT[:E0, half(h)], start=True, stop=True)
                mm.then_inc(e0_mm, 1)

            def down(j):
                pair, h = divmod(j, 2)
                if pair < PAIRS:
                    pe.wait_ge(e0_h, j + 1)
                else:
                    pe.wait_ge(e0_up, j + 1)
                w, x = (w2p[:, pair, :], hh[j % 2]) if pair < PAIRS else (w2s[:, :], hh[j % 2][:F0, :])
                pe.matmul(ps[:, 4 + h, 0:HALF], w, x, start=(pair == 0), stop=(pair == PAIRS),
                          skip_group_check=True).then_inc(e0_y, 1)

            last = 2 * (PAIRS + 1)
            shares(0)
            for j in range(last):
                if j + 1 < last:
                    shares(j + 1)
                down(j)
            ln(2)

            pe.matmul(ps[:, 4, 0:128], wq1[:, :], wk1[:, :], start=True, stop=True).then_inc(g1_mm, 1)
            pe.matmul(ps[:, 5, 0:3 * D], wv1[:, :], wih[:, :], start=True, stop=True).then_inc(g1_mm, 1)
            pe.wait_ge(g1_ev, 2)
            with pe.Fori(0, GROUPS) as g:
                for s in range(GB):
                    pe.wait_ge(key_n, g * GB + s + 1)
                    for c in range(3):
                        if s:
                            pe.wait_ge(kt_ev, g * (3 * GB) + 3 * s + c - 2)
                        for a in range(4):
                            q = 4 * c + a
                            mm = pe.transpose(ps[:, 1 + c, a * CP:(a + 1) * CP], keys[:, s, q * 128:(q + 1) * 128],
                                              ident[:CP, 0:CP])
                        mm.then_inc(kt_mm, 1)
                with pe.Fori(0, ITERS) as it:
                    r = pe.snap(g * ITERS + it)
                    pe.wait_ge(q_sq, r + 1)
                    pe.matmul(ps[:, 6, 0:HALF], mean_w[:, :], sq[:, 0:HALF], start=True, stop=True).then_inc(q_var, 1)
                    pe.wait_ge(q_sn, r + 1)
                    pe.matmul(ps[:, 7, 0:HALF], G1[:, :], cen[:, 0:HALF], start=True, stop=True).then_inc(q_mm, 1)
                    for gate in range(2):
                        pe.matmul(ps[:, gate, 0:HALF], whh[:, gate * D:(gate + 1) * D], slots_x, start=True, stop=False)

                    def scores(s):
                        if s >= 2:
                            pe.wait_ge(a_sub, r * GB + s - 1)
                        for c in range(CC):
                            bank = 2 + 2 * (s % 2) + c // (CC // 2)
                            col = c % (CC // 2) * S
                            mm = pe.matmul(ps[:CP, bank, col:col + S], keysT[:, s, c * CP:(c + 1) * CP],
                                           qT[:, s * S:(s + 1) * S], start=True, stop=True)
                        mm.then_inc(a_mm, 1)

                    pe.wait_ge(q_ok, r + 1)
                    pe.wait_ge(kt_ev, g * (3 * GB) + 3 * GB)
                    scores(0)
                    scores(1)
                    for s in range(GB):
                        pe.wait_ge(a_att, r * GB + s + 1)
                        for bank in (6, 7):
                            for c in range(CC):
                                w = keys[:, s, c * 128:(c + 1) * 128] if bank == 6 else ones[:CP, :]
                                mm = pe.matmul(ps[:, bank, s * S:(s + 1) * S], w, AT[s % 2][:CP, c, :],
                                               start=(c == 0), stop=(c == CC - 1))
                        mm.then_inc(u_mm, 1)
                        if s + 2 < GB:
                            scores(s + 2)
                    pe.matmul(ps[:, 3, 0:HALF], whh[:, 2 * D:3 * D], slots_x, start=True, stop=True).then_inc(gru_mm, 1)
                    pe.wait_ge(u_ok, r + 1)
                    for gate in range(3):
                        mm = pe.matmul(ps[:, gate, 0:HALF], F1w[:, gate * D:(gate + 1) * D], Un, start=(gate == 2), stop=True)
                    mm.then_inc(gru_mm, 1)
            ln(3)

            pe.wait_ge(ln_out, 8)
            for j in range(NT):
                mm = pe.matmul(ps[:, 0, j * E1:(j + 1) * E1], xln[:, j * 128:(j + 1) * 128], gw1[:, :], start=True, stop=True)
            mm.then_inc(lg1_mm, 1)
            for c in range(4):
                src = (xln, xT)[c // 2]
                j0, j1 = ((0, 4), (4, NT))[c % 2]
                for j in range(j0, j1):
                    mm = pe.transpose(ps[:, 4 + c, (j - j0) * 128:(j - j0 + 1) * 128], src[:, j * 128:(j + 1) * 128], ident[:, :])
                mm.then_inc(tok_mm, 1)
            pe.wait_ge(rt1_hot, 1)
            for j in range(NT):
                for i in range(j + 1):
                    mm = pe.matmul(ps[:, 1, j * E1:(j + 1) * E1], before_b[:, :] if i == j else ones_b[:, :],
                                   ohb[:, i, :], start=(i == 0), stop=(i == j))
            mm.then_inc(pos_mm, 1)
            pe.wait_ge(ld_xe, 32)
            pe.wait_ge(tok_ev, 4)
            for c in range(5):
                if c >= 2:
                    pe.wait_ge(xe_ev, c - 1)
                for j in range(4 * c, min(4 * c + 4, ST)):
                    mm = pe.transpose(ps[:, 4 + c % 2, j % 4 * 128:(j % 4 + 1) * 128], xe[:, j, :], ident[:, :])
                mm.then_inc(xe_mm, 1)

            def weights(e):
                return early_w[:, e, :] if e < EARLY else late_w[:, e - EARLY, :]

            def hidden(e):
                if e == 0:
                    pe.wait_ge(ld_early, 16)
                if e >= EARLY and (e - EARLY) % 4 == 0:
                    pe.wait_ge(ld_late[(e - EARLY) // 4], 16)
                pe.wait_ge(xe_ev, min(5, ((e + 1) * CAP - 1) // 512 + 1))
                if e >= 2:
                    pe.wait_ge(h_b, e - 1)
                for c in range(FC):
                    mm = pe.matmul(ps[:, e % 2, c * CAP:(c + 1) * CAP], weights(e)[:, c * 128:(c + 1) * 128],
                                   xeT[:, e * CAP:(e + 1) * CAP], start=True, stop=True)
                mm.then_inc(h_mm, 1)

            def result(e):
                g = e // 4
                if e % 4 == 0 and g >= 2:
                    pe.wait_ge(ye_ok, g - 1)
                pe.wait_ge(h_ok, e + 1)
                for c in range(FC):
                    mm = pe.matmul(ps[:, 2 + g % 2, e % 4 * CAP:(e % 4 + 1) * CAP], weights(e)[:, F1 + c * 128:F1 + (c + 1) * 128],
                                   hT[e % 2][:, c, :], start=(c == 0), stop=(c == FC - 1))
                mm.then_inc(ye_mm, 1)

            hidden(0)
            for e in range(E1):
                if e + 1 < E1 and e % 4 != 3:
                    hidden(e + 1)
                result(e)
                if e + 1 < E1 and e % 4 == 3:
                    hidden(e + 1)
            pe.wait_ge(ye_ok, E1 // 4)
            for c in range(5):
                if c >= 2:
                    pe.wait_ge(yt_ev, c - 1)
                for j in range(4 * c, min(4 * c + 4, ST)):
                    mm = pe.transpose(ps[:, 6 + c % 2, j % 4 * 128:(j % 4 + 1) * 128], ysT[:, j * 128:(j + 1) * 128], ident[:, :])
                mm.then_inc(yt_mm, 1)


SMALL = 20
CONSTS = 24
PLAN_LISTS = 27


def kernel(**inputs):
    import numpy as np
    import concourse.bacc as _bacc
    from concourse import mybir as _mybir
    from concourse.bass_utils import run_bass_kernel_spmd as _run

    a = {k: np.asarray(v) for k, v in inputs.items()}

    def heads(w):
        return w.T.reshape(H // 2, 2 * DH, D).transpose(1, 0, 2)

    ctx = a["ctx_1024"]
    wkv = a["L0_xattn_Wkv"]
    w13 = a["L0_ffn_w13"]
    arrays = {
        "xT": a["x"].reshape(T, D).T,
        "ctx": ctx,
        "ctx_blk": ctx.reshape(B * KB, KN, D),
        "ctxT_blk": ctx.reshape(B * KB, KN, D).transpose(0, 2, 1),
        "kv_mask": a["mask_BxS2_bk0"],
        "kv_blk": a["mask_BxS2_bk0"].reshape(B * KB, KN),
        "q_mask": a["mask_BxS_bk0"].reshape(B, TILES, QT).transpose(1, 0, 2).reshape(BT, QT),
        "wqT": heads(a["L0_xattn_Wq"]),
        "wkT": heads(wkv[:, 0:H * DH]),
        "wvT": heads(wkv[:, H * DH:]),
        "wo": a["L0_xattn_Wout"].reshape(H // 2, 2 * DH, D).transpose(1, 0, 2),
        "bout": a["L0_xattn_bout"].reshape(D, 1),
        "g_xattn": a["g_xattn"].reshape(1, 2),
        "g_ffn": a["g_ffn"].reshape(1, 2),
        "gw0": a["L0_ffn_gate_w"].T,
        "gb0": a["L0_ffn_gate_b"].reshape(1, E0),
        "w13": w13.reshape(E0, 2, F0, D).transpose(3, 1, 0, 2).reshape(D, 2, E0 * F0),
        "w2p": a["L0_ffn_w2"].transpose(0, 2, 1).reshape(PAIRS, 2 * F0, D).transpose(1, 0, 2),
        "ws": a["L0_ffn_w13_s"].T,
        "w2s": a["L0_ffn_w2_s"].T,
        "wq1": a["L1_xattn_Wq"],
        "wk1": a["L1_xattn_Wk"],
        "wv1": a["L1_xattn_Wv"],
        "wih": a["L1_xattn_gru_wih"].T,
        "whh": a["L1_xattn_gru_whh"].T,
        "bih": a["L1_xattn_gru_bih"].reshape(3, D).T,
        "bhh": a["L1_xattn_gru_bhh"].reshape(3, D).T,
        "wslot": a["L1_xattn_slot_norm_w"].reshape(D, 1),
        "wkey": a["L1_xattn_input_norm_w"].reshape(D, 1),
        "gw1": a["L1_ffn_gate_w"],
        "gb1": a["L1_ffn_gate_b"].reshape(1, E1),
        "b1T": a["L1_ffn_b1"].reshape(E1, FC, 128).transpose(2, 0, 1),
        "b2T": a["L1_ffn_b2"].T,
        "w12": np.concatenate([a["L1_ffn_w1"].transpose(1, 0, 2),
                               a["L1_ffn_w2"].reshape(E1, FC, 128, D).transpose(2, 0, 1, 3).reshape(128, E1, F1)], axis=2),
    }
    arrays = {k: np.ascontiguousarray(v) for k, v in arrays.items()}
    nc = _bacc.Bacc("TRN2", target_bir_lowering=False, num_devices=1)
    tensors = {k: nc.dram_tensor(f"in_{k}", v.shape, U8 if v.dtype == bool else _mybir.dt.from_np(v.dtype),
                                 kind="ExternalInput").ap()
               for k, v in arrays.items()}
    tensors["xe_scratch"] = nc.dram_tensor("xe_scratch", (SLOTS + TOP1 * T, D), _mybir.dt.float32).ap()
    tensors["ys_scratch"] = nc.dram_tensor("ys_scratch", (SLOTS, D), _mybir.dt.float32).ap()
    tensors["out"] = nc.dram_tensor("out_x", (T, D), _mybir.dt.float32, kind="ExternalOutput").ap()
    build_program(nc, tensors)
    r = _run(nc, [{f"in_{k}": v for k, v in arrays.items()}], core_ids=[0])
    return r.results[0]["out_x"].reshape(B, S, D)
```

```python
from contextlib import ExitStack

import concourse.bass as bass
from concourse import mybir

F32 = mybir.dt.float32
BF16 = mybir.dt.bfloat16
I32 = mybir.dt.int32
U32 = mybir.dt.uint32
U8 = mybir.dt.uint8
ALU = mybir.AluOpType
ACT = mybir.ActivationFunctionType
AX = mybir.AxisListType

B, S, D, M = 16, 56, 128, 1500
T = B * S
HALF = T // 2
NT = T // 128
H, DH = 16, 64
QT = 128 // H
TILES = S // QT
BT = B * TILES
KB, KN = 4, M // 4
KP, KC = 125, 3
ITEMS = BT * KB
BIG = 1e30
NOTHING = BT
UNUSED = BT + 1
KEY_BUFS = 4
E0, F0, TOP0, ROUTE = 16, 64, 4, 2.5
PAIRS = E0 // 2
CP, CC = 125, 12
GB = 8
GROUPS = B // GB
QB = GB // 2
QS = QB * S
ITERS = 3
HB = 2 * QB
CH = CC // 2
PHASES = 2 * ITERS
KW = 129
WIDE = 96
E1, F1, TOP1, CAP = 32, 512, 2, 68
FC = F1 // 128
SLOTS = E1 * CAP
ST = SLOTS // 128
TRASH = SLOTS
EARLY = 8


def build_program(nc, t):
    with ExitStack() as ctx:
        def sb(name, shape, dt=F32):
            return ctx.enter_context(nc.sbuf_tensor(name, shape, dt))

        def sem(name):
            return ctx.enter_context(nc.semaphore(name))

        mean_w = sb("mean_w", [128, 128])
        ones = sb("ones", [128, 128])
        ones_b = sb("ones_b", [128, 128], BF16)
        ident = sb("ident", [128, 128])
        before = sb("before", [128, 128])
        before_b = sb("before_b", [128, 128], BF16)
        iota_e = sb("iota_e", [128, E1])
        eps_ln = sb("eps_ln", [128, 1])
        eps_rms = sb("eps_rms", [128, 1])
        mean_rows = sb("mean_rows", [B, 128])
        gates_in = sb("gates_in", [128, 4])
        gates = sb("gates", [128, 4])
        bout = sb("bout", [128, 1])
        xT = sb("xT", [128, T])
        xln = sb("xln", [128, T])
        ln_tiles = sb("ln_tiles", [128, 3 * T])
        cen, sq, rstd = (ln_tiles[:, k * T:(k + 1) * T] for k in range(3))
        folded = sb("folded", [128, 2 * H * 128])
        G = folded[:, 0:H * 128].rearrange("p (h j) -> p h j", h=H)
        MO = folded[:, H * 128:].rearrange("p (h j) -> p h j", h=H)
        MS = sb("MS", [128, 128])
        ymean = sb("ymean", [128, B])
        meanT = sb("meanT", [128, B])
        sumsq = sb("sumsq", [CP, B, CC])
        rms = sb("rms", [CP, B, CC])
        rkey = sb("rkey", [CP, B, CC])
        qm8 = sb("qm8", [BT, QT], U8)
        keepq = sb("keepq", [BT, QT])
        act_q = sb("act_q", [BT, 1])
        act_k = sb("act_k", [BT, KB])
        any_k = sb("any_k", [BT, 1])
        active = sb("active", [BT, KB])
        prefix = sb("prefix", [BT, KB])
        rowsum = sb("rowsum", [BT, 1])
        rank = sb("rank", [BT, KB])
        firstc = sb("firstc", [BT, KB])
        lastc = sb("lastc", [BT, KB])
        bstep = sb("bstep", [BT, TILES - 1])
        bidx = sb("bidx", [BT, 1])
        btidx = sb("btidx", [BT, 1])
        lists_w = sb("lists_w", [BT, KB, 3], BF16)
        first_w = sb("first_w", [BT, KB, 128], BF16)
        item_n = sb("item_n", [1, 1], I32)
        m_run = sb("m_run", [128, 1])
        l_run = sb("l_run", [128, 1])
        l_inv = sb("l_inv", [128, 1])
        m_before = sb("m_before", [128, 2])
        m_block = sb("m_block", [128, 2])
        m_minus = sb("m_minus", [128, 2])
        rescale = sb("rescale", [128, 2])
        l_block = sb("l_block", [128, 2])
        gate_bout = sb("gate_bout", [128, 1])
        gw0 = sb("gw0", [128, E0])
        gb0 = sb("gb0", [128, E0])
        ws = sb("ws", [128, 2 * F0])
        w2s = sb("w2s", [F0, 128])
        sc0 = sb("sc0", [128, NT, E0])
        bi0 = sb("bi0", [128, NT, E0])
        hot = sb("hot", [128, NT, E0])
        msk = sb("msk", [128, NT, E0])
        den = sb("den", [128, NT])
        top8 = sb("top8", [128, NT, 8])
        idx8 = sb("idx8", [128, NT, 8], U32)
        idxf = sb("idxf", [128, NT, 8])
        wq1 = sb("wq1", [128, 128])
        wk1 = sb("wk1", [128, 128])
        wv1 = sb("wv1", [128, 128])
        wih = sb("wih", [128, 3 * D])
        whh = sb("whh", [128, 3 * D])
        G1 = sb("G1", [128, 128])
        F1w = sb("F1w", [128, 3 * D])
        bih = sb("bih", [128, 3])
        bhh = sb("bhh", [128, 3])
        hb = sb("hb", [128, 3])
        wslot = sb("wslot", [128, 1])
        wkey = sb("wkey", [128, 1])
        wkey_s = sb("wkey_s", [128, 1])
        mx = sb("mx", [CP, 2, CC])
        nb = sb("nb", [CP, 2, CC])
        sm = sb("sm", [CP, 2, CC])
        rs = sb("rs", [CP, 2, CC])
        zr = sb("zr", [S, 2, 1])
        gw1 = sb("gw1", [128, E1])
        gb1 = sb("gb1", [128, E1])
        b1T = sb("b1T", [128, E1, FC])
        b2T = sb("b2T", [128, E1])
        r1 = sb("r1", [128, NT])
        r2 = sb("r2", [128, NT])
        valid = sb("valid", [128, TOP1, NT])
        posk = sb("posk", [128, TOP1, NT])
        gidx = sb("gidx", [128, TOP1, NT], I32)
        sidx = sb("sidx", [128, TOP1, NT], I32)
        wk = sb("wk", [128, TOP1, NT])
        trash = sb("trash", [128, TOP1, NT])
        hT = [sb(f"hT{k}", [128, FC * CAP + WIDE - CAP]) for k in range(2)]
        hx1 = sb("hx1", [128, FC, CAP])
        early_w = sb("early_w", [128, EARLY, 2 * F1])
        region = sb("region", [128, 24 * 2 * F1])
        work = sb("work", [128, 4 * CC * S + 7 * HALF])
        used = {"region": 0, "work": 0, "early": 0}
        early = early_w[:, :, :].rearrange("p e c -> p (e c)")

        def carve(n, where="region"):
            tile = {"region": region, "work": work, "early": early}[where]
            used[where] += n
            assert used[where] <= tile.shape[1]
            return tile[:, used[where] - n:used[where]]

        tilesT = carve(H * (T + 2 * QT)).rearrange("p (h s) -> p h s", h=H)
        wqT, wkT, wvT, wo = (carve(H // 2 * 128).rearrange("p (h i) -> p h i", i=128) for _ in range(4))
        msq2 = carve(2 * CC * 128)
        msq = [msq2[:, k * CC * 128:(k + 1) * CC * 128] for k in range(2)]
        zero = msq2[:, 0:SLOTS]
        padd6 = carve(CC // 2 * 128)
        padd = [carve(CC // 4 * 128, "work") for _ in range(2)]
        item_bt = carve(ITEMS + 2).bitcast(I32)
        item_blk = carve(ITEMS + 2).bitcast(I32)
        item_dst = carve(ITEMS + 2).bitcast(I32)
        mctx = [carve(CC * 128, "early") for _ in range(KEY_BUFS)]
        hot_r = [carve(ITEMS // 2, "early").bitcast(BF16) for _ in range(KB)]
        iota_r = carve(ITEMS, "early")
        km8 = carve(376, "early").bitcast(U8)
        key_sel = carve(B * B, "early")[:CP, :].rearrange("p (b j) -> p b j", b=B)
        keep_d = carve(BT * QT, "work")
        not_first = carve(ITEMS + 1, "work")
        first_neg = carve(ITEMS + 1, "work")
        mask_row = [carve(96, "work").bitcast(U8) for _ in range(2)]
        mask_b = [carve(188, "work").bitcast(BF16) for _ in range(2)]
        Qk = [carve(128, "work") for _ in range(2)]
        P = carve(KN, "work")
        PT = carve(KC * 128, "work").rearrange("p (c r) -> p c r", c=KC)
        acc = carve(128, "work")
        On = carve(128, "work")
        ictx = [carve(KC * 128, w).rearrange("p (c d) -> p c d", c=KC) for w in ("region", "work")]
        ictxT = [carve(KN, "work") for _ in range(2)]
        used["early"] = 0
        w13 = carve(2 * E0 * F0, "early").rearrange("p (g n) -> p g n", g=2)
        w2p = carve(PAIRS * 128, "early").rearrange("p (e d) -> p e d", e=PAIRS)
        pair_sel = carve(PAIRS * 128, "early").rearrange("p (e d) -> p e d", e=PAIRS)
        combT = carve(T, "early")
        sg = [carve(HALF, "early") for _ in range(2)]
        hh = [carve(HALF, "early") for _ in range(2)]
        keys = region[:CP, 0:GB * CC * KW].rearrange("p (s c d) -> p s c d", s=GB, d=KW)
        keysT = region[:, GB * CC * KW:GB * CC * KW + GB * M].rearrange("p (s m) -> p s m", s=GB)
        used["work"] = 0
        A = [carve(CC * S, "work").rearrange("p (c s) -> p c s", c=CC) for _ in range(2)]
        UnN = carve(QB * 128, "work").rearrange("p (s d) -> p s d", s=QB)
        slots_x = carve(2 * QS, "work").rearrange("p (a s) -> p a s", a=2)
        qT_all = carve(2 * (QS + WIDE - S), "work")
        qT = qT_all.rearrange("p (a s) -> p a s", a=2)
        Un, rt, zt, nt, hn, tmp, sn, sq1, rstd1 = (carve(QS, "work") for _ in range(9))
        late_w = region[:, :].rearrange("p (e c) -> p e c", c=2 * F1)
        xtok = folded[:, 0:T].rearrange("p (n d) -> p n d", n=NT)
        rtok = folded[:, T:2 * T].rearrange("p (n d) -> p n d", n=NT)
        ysr = folded[:, 2 * T:2 * T + SLOTS].rearrange("p (n d) -> p n d", n=ST)
        xeT = ln_tiles[:, 0:SLOTS + WIDE - CAP]
        hx = [ln_tiles[:, SLOTS + WIDE - CAP:SLOTS + WIDE - CAP + FC * CAP].rearrange("p (c n) -> p c n", c=FC), hx1]
        used["work"] = 0
        xe = carve(SLOTS, "work").rearrange("p (n d) -> p n d", n=ST)
        ysT = carve(SLOTS, "work")
        lg, pr, posx = (carve(NT * E1, "work").rearrange("p (n e) -> p n e", n=NT) for _ in range(3))
        oh = [carve(NT * E1, "work").rearrange("p (n e) -> p n e", n=NT) for _ in range(TOP1)]
        ohb = carve(NT * E1 // 2, "work").bitcast(BF16).rearrange("p (n e) -> p n e", n=NT)
        yg = early_w[:, 0:2, 0:T]

        ps = ctx.enter_context(nc.psum_tensor("ps", [128, 8, 512], F32))

        ld_x = sem("ld_x")
        ld_attn = sem("ld_attn")
        ld_small = sem("ld_small")
        ld_mask = sem("ld_mask")
        ld_mctx = [sem(f"ld_mctx{k}") for k in range(KEY_BUFS)]
        ld_itemT = [sem(f"ld_itemT{k}") for k in range(2)]
        ld_item = [sem(f"ld_item{k}") for k in range(2)]
        ld_ffn0 = sem("ld_ffn0")
        ld_keys = [sem(f"ld_keys{s}") for s in range(GB)]
        ld_early = sem("ld_early")
        ld_late = [sem(f"ld_late{n}") for n in range((E1 - EARLY) // 4)]
        st_zero = sem("st_zero")
        st_xe = sem("st_xe")
        ld_xe = sem("ld_xe")
        st_ys = sem("st_ys")
        ld_yg = sem("ld_yg")
        st_out = sem("st_out")
        const = sem("const")
        cstep = sem("cstep")
        gates_ok = sem("gates_ok")
        ln_mean = sem("ln_mean")
        ln_cent = sem("ln_cent")
        ln_sq = sem("ln_sq")
        ln_var = sem("ln_var")
        ln_sd = sem("ln_sd")
        ln_rec = sem("ln_rec")
        ln_out = sem("ln_out")
        x_new = sem("x_new")
        fold_mm = sem("fold_mm")
        fold_ev = sem("fold_ev")
        fold_sum = sem("fold_sum")
        key_sq = sem("key_sq")
        key_ss = sem("key_ss")
        key_add = sem("key_add")
        key_add3 = sem("key_add3")
        key_sum = sem("key_sum")
        mean_mm = sem("mean_mm")
        mean_ev = sem("mean_ev")
        ymean_mm = sem("ymean_mm")
        ymean_ev = sem("ymean_ev")
        rk_sd = sem("rk_sd")
        rk_ok = sem("rk_ok")
        qa_mm = sem("qa_mm")
        qa_ev = sem("qa_ev")
        plan = sem("plan")
        plan_rs = sem("plan_rs")
        plan_rank = sem("plan_rank")
        plan_hot = sem("plan_hot")
        plan_list = sem("plan_list")
        items_ok = sem("items_ok")
        q_tile = sem("q_tile")
        s_mm = sem("s_mm")
        s_max = sem("s_max")
        m_prev = sem("m_prev")
        m_new = sem("m_new")
        m_neg = sem("m_neg")
        p_exp = sem("p_exp")
        pt_mm = sem("pt_mm")
        pt_ev = sem("pt_ev")
        o_mm = sem("o_mm")
        l_ok = sem("l_ok")
        acc_ok = sem("acc_ok")
        rl_ok = sem("rl_ok")
        on_ok = sem("on_ok")
        ot_mm = sem("ot_mm")
        ot_ev = sem("ot_ev")
        y_mm = sem("y_mm")
        pair_ok = sem("pair_ok")
        y_keep = sem("y_keep")
        keep_mm = sem("keep_mm")
        res0 = sem("res0")
        lg0_mm = sem("lg0_mm")
        sc0_ok = sem("sc0_ok")
        rt0 = sem("rt0")
        comb_ok = sem("comb_ok")
        combT_mm = sem("combT_mm")
        combT_ok = sem("combT_ok")
        e0_mm = sem("e0_mm")
        e0_act = sem("e0_act")
        e0_up = sem("e0_up")
        e0_h = sem("e0_h")
        e0_y = sem("e0_y")
        res1 = sem("res1")
        g1_mm = sem("g1_mm")
        g1_ev = sem("g1_ev")
        hb_ok = sem("hb_ok")
        q_pad = sem("q_pad")
        key_col = sem("key_col")
        sl_ok = sem("sl_ok")
        q_sq = sem("q_sq")
        q_var = sem("q_var")
        q_sd = sem("q_sd")
        q_rec = sem("q_rec")
        q_sn = sem("q_sn")
        q_mm = sem("q_mm")
        q_ok = sem("q_ok")
        a_mm = sem("a_mm")
        a_max = sem("a_max")
        a_neg = sem("a_neg")
        a_exp = sem("a_exp")
        a_rec = sem("a_rec")
        a_w = sem("a_w")
        a_att = sem("a_att")
        u_mm = sem("u_mm")
        z_add = sem("z_add")
        z_rec = sem("z_rec")
        un_ok = sem("un_ok")
        gru_slots = sem("gru_slots")
        ut_mm = sem("ut_mm")
        u_ok = sem("u_ok")
        hn_ok = sem("hn_ok")
        gate_mm = sem("gate_mm")
        gru_t = sem("gru_t")
        gru_v = sem("gru_v")
        gru_n = sem("gru_n")
        gru_new = sem("gru_new")
        gru_last = sem("gru_last")
        lg1_mm = sem("lg1_mm")
        rt1 = sem("rt1")
        rt1_exp = sem("rt1_exp")
        rt1_hot = sem("rt1_hot")
        pos_mm = sem("pos_mm")
        slot_ok = sem("slot_ok")
        tok_mm = sem("tok_mm")
        tok_ev = sem("tok_ev")
        wide_ok = sem("wide_ok")
        xe_mm = sem("xe_mm")
        xe_ev = sem("xe_ev")
        h_mm = sem("h_mm")
        h_b = sem("h_b")
        h_ok = sem("h_ok")
        ye_mm = sem("ye_mm")
        ye_ok = sem("ye_ok")
        yt_mm = sem("yt_mm")
        yt_ev = sem("yt_ev")
        out_s = sem("out_s")

        xe_dram = t["xe_scratch"]
        ys_dram = t["ys_scratch"]
        block = ctx.enter_context(nc.Block())

        def half(h):
            return slice(h * HALF, (h + 1) * HALF)

        def bcast(ap, n):
            return ap.unsqueeze(len(ap.shape)).to_broadcast([*ap.shape, n])

        def over_tiles(ap):
            return ap.unsqueeze(1).to_broadcast([ap.shape[0], NT, ap.shape[1]])

        def phases(eng, phase):
            for g in range(GROUPS):
                phase(g, 0, g * PHASES)
                with eng.Fori(0, ITERS - 1) as it:
                    for w in (1, 2):
                        phase(g, w, eng.snap(it * 2 + (g * PHASES + w)))
                phase(g, PHASES - 1, g * PHASES + PHASES - 1)

        def quad(g, k):
            return slice((g * 2 + k) * QS, (g * 2 + k + 1) * QS)

        def loads_next(g, w):
            return w == 0 or (w == PHASES - 1 and g + 1 < GROUPS)

        def prepares(g, w):
            return w < PHASES - 1 or g + 1 < GROUPS

        @block.sync
        def _(sp):
            sp.dma_start(xT[:, :], t["xT"]).then_inc(ld_x, 16)
            for r in range(TILES):
                sp.dma_start(km8[r * B:(r + 1) * B, 0:M], t["kv_mask"]).then_inc(ld_mask, 16)
            sp.dma_start(qm8[:, :], t["q_mask"]).then_inc(ld_mask, 16)
            for dst, name in ((wqT, "wqT"), (wkT, "wkT"), (wvT, "wvT"), (wo, "wo")):
                sp.dma_start(dst, t[name]).then_inc(ld_attn, 16)
            ctx_b = t["ctx"].rearrange("b (p c) d -> b p (c d)", p=CP)

            def load_batch(dst, b, done):
                for p0, p1 in ((0, 112), (112, CP)):
                    sp.dma_start(dst[p0:p1, :], ctx_b[bass.ds(b, 1), p0:p1, :].rearrange("a p c -> (a p) c")).then_inc(done, 16)

            for k in range(KEY_BUFS):
                load_batch(mctx[k], k, ld_mctx[k])
            with sp.Fori(1, B // KEY_BUFS) as i:
                for k in range(KEY_BUFS):
                    sp.wait_ge(key_sq, i * KEY_BUFS + (k - KEY_BUFS + 1))
                    sp.wait_ge(key_add, i * KEY_BUFS + (k - KEY_BUFS + 1))
                    load_batch(mctx[k], i * KEY_BUFS + k, ld_mctx[k])
            sp.wait_ge(items_ok, 1)
            n = sp.value_load(item_n[0:1, 0:1], min_val=1, max_val=ITEMS)

            def load_item(j, k, values=True):
                blk = sp.value_load(item_blk[0:1, bass.ds(j, 1)], min_val=0, max_val=B * KB - 1)
                sp.wait_ge(s_mm, j + 1)
                sp.dma_start(ictxT[k], t["ctxT_blk"][bass.ds(blk, 1), :, :].rearrange("a p c -> (a p) c")).then_inc(ld_itemT[k], 16)
                sp.dma_start(mask_row[k][0:1, 0:KN], t["kv_blk"][bass.ds(blk, 1), :]).then_inc(ld_itemT[k], 16)
                if not values:
                    return
                sp.wait_ge(o_mm, j + 1)
                sp.dma_start(ictx[k][:KP, :, :], t["ctx_blk"][bass.ds(blk, 1), :, :].rearrange("a (p c) d -> (a p) c d", c=KC)).then_inc(ld_item[k], 16)

            with sp.Fori(0, (n + 1) // 2) as i:
                for k in range(2):
                    load_item(sp.snap(i * 2 + k), k)
            load_item(sp.snap((n + 1) // 2 * 2), 0, values=False)
            sp.wait_ge(y_mm, 2)
            for g in range(GROUPS):
                for s in range(GB):
                    if g:
                        sp.wait_ge(u_mm, (g * PHASES - 2) * QB + s + 1)
                    for p0, p1 in ((0, 112), (112, CP)):
                        sp.dma_start(keys[p0:p1, s, :, 0:128],
                                     ctx_b[g * GB + s, p0:p1, :].rearrange("p (c d) -> p c d", c=CC)).then_inc(ld_keys[s], 16)
                    sp.dma_start(keysT[:, s, :], t["ctxT"][g * GB + s]).then_inc(ld_keys[s], 16)
            sp.wait_ge(u_mm, GROUPS * PHASES * QB)
            for e in range(0, E1 - EARLY, 4):
                sp.dma_start(late_w[:, e:e + 4, :], t["w12"][:, EARLY + e:EARLY + e + 4, :]).then_inc(ld_late[e // 4], 16)
            sp.wait_ge(st_xe, 16 * TOP1 * NT)
            for j0, j1 in ((0, 8), (8, ST)):
                sp.dma_start(xe[:, j0:j1, :], xe_dram[j0 * 128:j1 * 128, :].rearrange("(n p) d -> p n d", p=128)).then_inc(ld_xe, 16)
            sp.wait_ge(yt_ev, 5)
            sp.dma_start(ys_dram.rearrange("(n p) d -> p n d", p=128), ysr).then_inc(st_ys, 16)
            sp.wait_ge(out_s, 2 * NT)
            sp.dma_start(t["out"].rearrange("(n p) d -> p n d", p=128), xtok).then_inc(st_out, 16)
            sp.wait_ge(st_out, 16)

        @block.gpsimd
        def _(gp):
            gp.memset(mean_w[:, :], 1.0 / D).then_inc(const, 1)
            gp.memset(ones[:, :], 1.0).then_inc(const, 1)
            gp.memset(ones_b[:, :], 1.0).then_inc(const, 1)
            gp.memset(eps_ln[:, :], 1e-5).then_inc(const, 1)
            gp.memset(eps_rms[:, :], 1e-6).then_inc(const, 1)
            gp.memset(key_sel[:, :, :], 0.0).then_inc(const, 1)
            gp.memset(ident[:, :], 0.0).then_inc(const, 1)
            gp.wait_ge(const, 7)
            gp.affine_select(out=ident[:, :], in_=ident[:, :], compare_op=ALU.not_equal, fill=1.0, base=0,
                             pattern=[[-1, 128]], channel_multiplier=1).then_inc(const, 1)
            gp.affine_select(out=before[:, :], in_=ones[:, :], compare_op=ALU.is_gt, fill=0.0, base=0,
                             pattern=[[1, 128]], channel_multiplier=-1).then_inc(const, 1)
            gp.affine_select(out=bstep[:, :], in_=ones[:BT, 0:TILES - 1], compare_op=ALU.is_ge, fill=0.0,
                             base=-B, pattern=[[-B, TILES - 1]], channel_multiplier=1).then_inc(const, 1)
            gp.affine_select(out=key_sel[:, :, :], in_=key_sel[:, :, :], compare_op=ALU.not_equal, fill=1.0 / M,
                             base=0, pattern=[[1, B], [-1, B]], channel_multiplier=0).then_inc(const, 1)
            gp.iota(iota_e[:, :], pattern=[[1, E1]], base=0, channel_multiplier=0,
                    allow_small_or_imprecise_dtypes=True).then_inc(const, 1)
            gp.iota(iota_r, pattern=[[1, ITEMS]], base=0, channel_multiplier=0,
                    allow_small_or_imprecise_dtypes=True).then_inc(const, 1)
            gp.iota(btidx[:, :], pattern=[[0, 1]], base=0, channel_multiplier=1,
                    allow_small_or_imprecise_dtypes=True).then_inc(const, 1)
            gp.iota(trash[:, :, :], pattern=[[NT * 128, TOP1], [128, NT]], base=TRASH, channel_multiplier=1,
                    allow_small_or_imprecise_dtypes=True).then_inc(const, 1)
            gp.memset(item_bt[0:1, :], NOTHING).then_inc(const, 1)
            gp.memset(item_blk[0:1, :], 0).then_inc(const, 1)
            gp.memset(item_dst[0:1, :], UNUSED).then_inc(const, 1)
            gp.memset(not_first, 0.0).then_inc(const, 1)
            gp.memset(first_neg, 0.0).then_inc(const, 1)
            gp.memset(acc, 0.0).then_inc(const, 1)
            gp.memset(On, 0.0).then_inc(const, 1)
            gp.memset(m_run[:, :], 0.0).then_inc(const, 1)
            gp.memset(l_run[:, :], 1.0).then_inc(const, 1)
            gp.memset(zero, 0.0).then_inc(const, 1)
            gp.memset(tilesT[:, :, T:T + 2 * QT], 0.0).then_inc(const, 1)
            gp.wait_ge(const, CONSTS - 1)
            gp.tensor_copy(before_b[:, :], before[:, :]).then_inc(const, 1)
            gp.wait_ge(const, CONSTS)
            gp.dma_start(xe_dram[0:SLOTS, :].rearrange("(p n) d -> p (n d)", p=128), zero).then_inc(st_zero, 16)
            small = [(gates_in[:, 0:2], t["g_xattn"].to_broadcast([128, 2])),
                     (gates_in[:, 2:4], t["g_ffn"].to_broadcast([128, 2])),
                     (bout[:, :], t["bout"]), (gw0[:, :], t["gw0"]), (gb0[:, :], t["gb0"].to_broadcast([128, E0])),
                     (ws[:, :], t["ws"]), (w2s[:, :], t["w2s"]), (wq1[:, :], t["wq1"]), (wk1[:, :], t["wk1"]),
                     (wv1[:, :], t["wv1"]), (wih[:, :], t["wih"]), (whh[:, :], t["whh"]), (bih[:, :], t["bih"]),
                     (bhh[:, :], t["bhh"]), (wslot[:, :], t["wslot"]), (wkey[:, :], t["wkey"]), (gw1[:, :], t["gw1"]),
                     (gb1[:, :], t["gb1"].to_broadcast([128, E1])), (b1T[:, :, :], t["b1T"]), (b2T[:, :], t["b2T"])]
            assert len(small) == SMALL
            for dst, src in small:
                gp.dma_start(dst, src).then_inc(ld_small, 16)

            with gp.Fori(0, B // KEY_BUFS) as i:
                for k in range(KEY_BUFS):
                    gp.wait_ge(ld_mctx[k], i * 32 + 32)
                    gp.wait_ge(key_add3, i * KEY_BUFS + (k + 1))
                    gp.tensor_tensor(padd6[:CP, :], mctx[k][:CP, 0:CC // 2 * 128], mctx[k][:CP, CC // 2 * 128:], ALU.add).then_inc(key_add, 1)
                    gp.wait_ge(key_add, i * KEY_BUFS + (k + 1))
                    gp.wait_ge(key_sum, i * KEY_BUFS + (k + 1))
                    gp.tensor_tensor(padd[k % 2][:CP, :], padd6[:CP, 0:CC // 4 * 128], padd6[:CP, CC // 4 * 128:], ALU.add).then_inc(key_add3, 1)
            gp.wait_ge(key_sq, B)
            gp.wait_ge(key_sum, B + 2)
            gp.wait_ge(plan_list, 1)
            gp.dma_start(w13, t["w13"]).then_inc(ld_ffn0, 16)
            gp.dma_start(w2p, t["w2p"]).then_inc(ld_ffn0, 16)
            gp.memset(pair_sel, 0.0).then_inc(pair_ok, 1)
            gp.wait_ge(pair_ok, 1)
            gp.affine_select(out=pair_sel[:E0].rearrange("p e (a i) -> p e a i", a=2),
                             in_=pair_sel[:E0].rearrange("p e (a i) -> p e a i", a=2),
                             compare_op=ALU.not_equal, fill=1.0, base=0,
                             pattern=[[-2, PAIRS], [-1, 2], [0, F0]], channel_multiplier=1).then_inc(pair_ok, 1)
            gp.wait_ge(items_ok, 1)
            gp.wait_ge(qa_ev, 2 * H)
            n = gp.value_load(item_n[0:1, 0:1], min_val=1, max_val=ITEMS)

            def item_queries(j, k, loads):
                bt = gp.value_load(item_bt[0:1, bass.ds(j, 1)], min_val=0, max_val=BT)
                gp.wait_ge(ld_itemT[k], loads)
                gp.wait_ge(s_mm, j + 1)
                gp.tensor_copy(Qk[k].rearrange("p (h q) -> p h q", h=H), tilesT[:, :, bass.ds(bt * QT, QT)])
                gp.tensor_scalar(mask_b[k][0:1, 0:KN], mask_row[k][0:1, 0:KN], -1.0, BIG, ALU.add, ALU.mult).then_inc(q_tile, 1)

            item_queries(0, 0, 32)
            with gp.Fori(0, (n + 1) // 2) as i:
                item_queries(gp.snap(i * 2 + 1), 1, i * 32 + 32)
                item_queries(gp.snap(i * 2 + 2), 0, i * 32 + 64)

            gp.wait_ge(y_mm, 2)
            gp.memset(qT_all, 0.0).then_inc(q_pad, 1)
            gp.wait_ge(rk_sd, 1)

            def key_rms(g):
                for s in range(GB):
                    if g:
                        gp.wait_ge(u_mm, (g * PHASES - 2) * QB + s + 1)
                    gp.tensor_copy(keys[:, s, :, 128:KW], rms[:, g * GB + s, :].unsqueeze(2)).then_inc(key_col, 1)

            def slot_squares(u, k):
                gp.wait_ge(sl_ok, u + 1)
                gp.tensor_tensor(sq1, slots_x[:, k, :], slots_x[:, k, :], ALU.mult).then_inc(q_sq, 1)

            key_rms(0)
            gp.wait_ge(x_new, 4)
            gp.dma_start(early_w[:, :, :], t["w12"][:, 0:EARLY, :]).then_inc(ld_early, 16)
            slot_squares(0, 0)

            def phase(g, w, u):
                if prepares(g, w):
                    slot_squares(u + 1, 1 - w % 2)
                if w == PHASES - 1 and g + 1 < GROUPS:
                    key_rms(g + 1)

            phases(gp, phase)

            gp.wait_ge(ln_out, 8)
            gp.memset(xeT[:, SLOTS:], 0.0).then_inc(wide_ok, 1)
            for k in range(2):
                gp.memset(hT[k][:, FC * CAP:], 0.0).then_inc(wide_ok, 1)
            gp.wait_ge(slot_ok, 2)
            gp.wait_ge(tok_ev, 4)
            for k in range(TOP1):
                for j in range(NT):
                    gp.indirect_dma_start(xe_dram, bass.IndirectOffsetOnAxis(ap=sidx[:, k, j:j + 1].bitcast(U32), axis=0),
                                          xtok[:, j, :], None).then_inc(st_xe, 16)
            gp.wait_ge(st_ys, 16)
            for k in range(TOP1):
                for j in range(NT):
                    gp.indirect_dma_start(yg[:, k, j * 128:(j + 1) * 128], None, ys_dram,
                                          bass.IndirectOffsetOnAxis(ap=gidx[:, k, j:j + 1].bitcast(U32), axis=0)).then_inc(ld_yg, 16)

        @block.scalar
        def _(act):
            def ln(k):
                for h in range(2):
                    act.wait_ge(ln_cent, 2 * k + h + 1)
                    act.activation(sq[:, half(h)], cen[:, half(h)], ACT.Square).then_inc(ln_sq, 1)
                for h in range(2):
                    act.wait_ge(ln_var, 2 * k + h + 1)
                    act.activation(rstd[:, half(h)], ps[:, 2 + h, 0:HALF], ACT.Sqrt, bias=eps_ln[:, :]).then_inc(ln_sd, 1)

            act.wait_ge(const, CONSTS)
            ln(0)
            for f in range(2):
                for q in range(4):
                    act.wait_ge(fold_mm, 4 * f + q + 1)
                    dst = (G, MO)[f].rearrange("p (m a) j -> p a m j", a=2)[:, q % 2, 4 * (q // 2):4 * (q // 2) + 4, :]
                    act.activation(dst, ps[:, 4 + q, :].rearrange("p (m j) -> p m j", m=4), ACT.Copy, scale=(DH ** -0.5 if f == 0 else 1.0)).then_inc(fold_ev, 1)

            act.wait_ge(st_zero, 16)
            with act.Fori(0, B // KEY_BUFS) as i:
                for k in range(KEY_BUFS):
                    b = act.snap(i * KEY_BUFS + k)
                    for h in range(2):
                        act.wait_ge(qa_mm, b * 2 + (h + 1))
                        act.copy(tilesT[:, bass.ds(b, 1), half(h)], ps[:, h, 0:HALF].unsqueeze(1)).then_inc(qa_ev, 1)
                for k in range(KEY_BUFS):
                    act.wait_ge(ld_mctx[k], i * 32 + 32)
                    act.wait_ge(key_ss, i * KEY_BUFS + (k + 1))
                    act.activation(msq[k % 2][:CP, :], mctx[k][:CP, :], ACT.Square).then_inc(key_sq, 1)
            act.wait_ge(ld_small, 16 * SMALL)
            act.activation(gates[:, :], gates_in[:, :], ACT.Tanh).then_inc(gates_ok, 1)

            def probabilities(j, k):
                act.wait_ge(m_neg, j + 1)
                act.activation(rescale[:, k:k + 1], m_before[:, k:k + 1], ACT.Exp, bias=m_minus[:, k:k + 1])
                act.activation(P, ps[:, k, 0:KN], ACT.Exp, bias=m_minus[:, k:k + 1],
                               accum_out=l_block[:, k:k + 1]).then_inc(p_exp, 1)

            def keep_result(j):
                dst = act.value_load(item_dst[0:1, bass.ds(j, 1)], min_val=0, max_val=UNUSED)
                act.wait_ge(ot_mm, j + 1)
                act.copy(tilesT[:, :, bass.ds(dst * QT, QT)], ps[:, 4, 0:128].rearrange("p (h q) -> p h q", h=H)).then_inc(ot_ev, 1)

            act.wait_ge(items_ok, 1)
            n = act.value_load(item_n[0:1, 0:1], min_val=1, max_val=ITEMS)
            probabilities(0, 0)
            with act.Fori(0, (n + 1) // 2) as i:
                for k in range(2):
                    j = act.snap(i * 2 + k)
                    act.wait_ge(pt_mm, j + 1)
                    act.wait_ge(o_mm, j + 2)
                    act.copy(PT[:KP].rearrange("p c r -> p (c r)"), ps[:KP, 2, 0:KC * 128]).then_inc(pt_ev, 1)
                    probabilities(j + 1, 1 - k)
                    keep_result(j)
            keep_result(act.snap((n + 1) // 2 * 2))
            act.wait_ge(key_ss, B + 2)
            act.activation(rms[:, :, :], sumsq[:, :, :], ACT.Sqrt, bias=eps_rms[:CP, :], scale=1.0 / D).then_inc(rk_sd, 1)
            ln(1)
            act.wait_ge(lg0_mm, 1)
            act.activation(sc0[:, :, :].rearrange("p n e -> p (n e)"), ps[:, 4, 0:NT * E0], ACT.Sigmoid).then_inc(sc0_ok, 1)
            for j in range(2 * (PAIRS + 1)):
                p = 128 if j // 2 < PAIRS else F0
                act.wait_ge(e0_mm, j + 1)
                if j >= 2:
                    act.wait_ge(e0_up, j - 1)
                act.activation(sg[j % 2][:p, :], ps[:p, 2 * (j % 2), 0:HALF], ACT.Silu).then_inc(e0_act, 1)
            ln(2)
            act.wait_ge(g1_mm, 2)
            act.copy(G1[:, :], ps[:, 4, 0:128]).then_inc(g1_ev, 1)
            act.copy(F1w[:, :], ps[:, 5, 0:3 * D]).then_inc(g1_ev, 1)

            def exponentials(g, k, u, m):
                (s, h), a, b = divmod(m, 2), m // 2 % 2, g * GB + k * QB + m // 2
                act.wait_ge(a_neg, u * HB + (m + 1))
                if not isinstance(u, int) or u * QB + s >= 2:
                    act.wait_ge(u_mm, u * QB + (s - 1))
                for c in range(CH):
                    q = h * CH + c
                    i = act.activation(A[a][:CP, q, :], ps[:CP, 2 + 2 * a + h, c * S:(c + 1) * S], ACT.Exp,
                                       bias=nb[:, a, q:q + 1], scale=rkey[:, b, q:q + 1], accum_out=sm[:, a, q:q + 1])
                i.then_inc(a_exp, 1)

            def gates_of(v):
                act.wait_ge(gate_mm, v + 1)
                act.activation(rt, ps[:, 0, 0:QS], ACT.Tanh, bias=hb[:, 0:1], scale=0.5).then_inc(gru_t, 1)
                act.activation(zt, ps[:, 0, QS:2 * QS], ACT.Tanh, bias=hb[:, 1:2], scale=0.5).then_inc(gru_t, 1)
                act.wait_ge(gru_v, v * 2 + 2)
                act.activation(nt, tmp, ACT.Tanh, bias=bih[:, 2:3]).then_inc(gru_n, 1)

            def slot_rms(u):
                act.wait_ge(q_var, u + 1)
                act.activation(rstd1, ps[:, 0, 0:QS], ACT.Sqrt, bias=eps_rms[:, :]).then_inc(q_sd, 1)

            slot_rms(0)
            exponentials(0, 0, 0, 0)
            exponentials(0, 0, 0, 1)

            def phase(g, w, u):
                k = w % 2
                for m in range(HB):
                    if m + 2 < HB:
                        exponentials(g, k, u, m + 2)
                    elif prepares(g, w):
                        exponentials(g + w // (PHASES - 1), 1 - k, u + 1, m + 2 - HB)
                    if m == 0 and (g, w) != (0, 0):
                        gates_of(u - 1)
                    if m == 2 and prepares(g, w):
                        slot_rms(u + 1)

            phases(act, phase)
            gates_of(GROUPS * PHASES - 1)
            ln(3)
            act.wait_ge(rt1, 3)
            act.activation(pr, lg, ACT.Exp).then_inc(rt1_exp, 1)
            for c in range(4):
                act.wait_ge(tok_mm, c + 1)
                j0, j1 = ((0, 4), (4, NT))[c % 2]
                dst = (xtok, rtok)[c // 2][:, j0:j1, :].rearrange("p n d -> p (n d)")
                act.copy(dst, ps[:, 4 + c, 0:(j1 - j0) * 128]).then_inc(tok_ev, 1)
            for c in range(5):
                w = min(512, SLOTS - 512 * c)
                act.wait_ge(xe_mm, c + 1)
                act.copy(xeT[:, 512 * c:512 * c + w], ps[:, 4 + c % 2, 0:w]).then_inc(xe_ev, 1)
            for e in range(E1):
                act.wait_ge(h_b, e + 1)
                if e >= 2:
                    act.wait_ge(ye_mm, e - 1)
                act.activation(hT[e % 2][:, 0:FC * CAP], hx[e % 2].rearrange("p c n -> p (c n)"), ACT.Gelu).then_inc(h_ok, 1)
            for c in range(5):
                j0, j1 = 4 * c, min(4 * c + 4, ST)
                act.wait_ge(yt_mm, c + 1)
                act.copy(ysr[:, j0:j1, :].rearrange("p n d -> p (n d)"), ps[:, 6 + c % 2, 0:(j1 - j0) * 128]).then_inc(yt_ev, 1)

        @block.vector
        def _(v):
            def ln(k):
                for h in range(2):
                    v.wait_ge(ln_mean, 2 * k + h + 1)
                    v.tensor_tensor(cen[:, half(h)], xT[:, half(h)], ps[:, h, 0:HALF], ALU.subtract).then_inc(ln_cent, 1)
                for h in range(2):
                    v.wait_ge(ln_sd, 2 * k + h + 1)
                    v.reciprocal(rstd[:, half(h)], rstd[:, half(h)]).then_inc(ln_rec, 1)
                for h in range(2):
                    v.wait_ge(ln_rec, 2 * k + h + 1)
                    v.tensor_tensor(xln[:, half(h)], cen[:, half(h)], rstd[:, half(h)], ALU.mult).then_inc(ln_out, 1)

            def chain(signal):
                count = [0]

                def step(ins, wait=True):
                    count[0] += 1
                    ins.then_inc(signal, 1)
                    if wait:
                        v.wait_ge(signal, count[0])

                step.count = count
                return step

            v.wait_ge(const, CONSTS)
            v.wait_ge(ld_x, 16)
            ln(0)
            v.sem_inc(key_ss, 2)
            v.sem_inc(key_sum, 2)
            v.sem_inc(key_add3, 1)
            v.sem_inc(s_mm, 2)
            v.sem_inc(o_mm, 2)
            v.sem_inc(on_ok, 1)
            v.sem_inc(ot_ev, 1)
            step = chain(plan)
            v.wait_ge(ld_mask, 16 * (TILES + 1))
            step(v.tensor_copy(keepq[:, :], qm8[:, :]))
            step(v.tensor_reduce(act_q[:, :], keepq[:, :], AX.X, ALU.max))
            step(v.tensor_reduce(act_k[:, :], km8[:BT, 0:M].rearrange("p (k m) -> p k m", k=KB), AX.X, ALU.max))
            step(v.tensor_reduce(any_k[:, :], act_k[:, :], AX.X, ALU.max))
            step(v.tensor_scalar(keepq[:, :], keepq[:, :], any_k[:, 0:1], None, ALU.mult))
            step(v.tensor_scalar(active[:, :], act_k[:, :], act_q[:, 0:1], None, ALU.mult))
            step(v.memset(prefix[:, 0:1], 0.0))
            for b in range(1, KB):
                step(v.tensor_tensor(prefix[:, b:b + 1], prefix[:, b - 1:b], active[:, b - 1:b], ALU.add))
            v.tensor_reduce(rowsum[:, :], active[:, :], AX.X, ALU.add).then_inc(plan_rs, 1)
            step(v.tensor_scalar(firstc[:, :], prefix[:, :], 0.0, None, ALU.is_equal))
            step(v.tensor_tensor(firstc[:, :], firstc[:, :], active[:, :], ALU.mult))
            step(v.tensor_tensor(lastc[:, :], prefix[:, :], active[:, :], ALU.add))
            v.wait_ge(plan_rs, 1)
            step(v.tensor_scalar(lastc[:, :], lastc[:, :], rowsum[:, 0:1], None, ALU.is_equal))
            step(v.tensor_tensor(lastc[:, :], lastc[:, :], active[:, :], ALU.mult))
            step(v.tensor_reduce(bidx[:, :], bstep[:, :], AX.X, ALU.add))
            step(v.scalar_tensor_tensor(btidx[:, :], bidx[:, :], -float(B), btidx[:, :], ALU.mult, ALU.add))
            for b in range(KB):
                step(v.tensor_scalar(lists_w[:, b, 1:2], btidx[:, :], float(KB), float(b), ALU.mult, ALU.add), wait=False)
                step(v.tensor_copy(first_w[:, b, :], firstc[:, b:b + 1].to_broadcast([BT, 128])), wait=False)
            step(v.scalar_tensor_tensor(btidx[:, :], btidx[:, :], float(TILES), bidx[:, :], ALU.mult, ALU.add))
            for b in range(KB):
                step(v.tensor_scalar(lists_w[:, b, 0:1], btidx[:, :], -float(NOTHING), None, ALU.add), wait=False)
                step(v.tensor_scalar(lists_w[:, b, 2:3], btidx[:, :], -float(UNUSED), lastc[:, b:b + 1], ALU.add, ALU.mult))
            assert step.count[0] == PLAN_LISTS
            v.wait_ge(plan_rank, 2)
            step(v.tensor_scalar(rank[:, :], prefix[:, :], ps[:BT, 2, 0:1], None, ALU.add))
            for b in range(KB):
                v.tensor_scalar(hot_r[b][:BT, :], iota_r[:BT, :], rank[:, b:b + 1], active[:, b:b + 1],
                                ALU.is_equal, ALU.mult).then_inc(plan_hot, 1)
            v.tensor_tensor(keep_d[:BT, :].rearrange("p (b t q) -> p t b q", t=TILES, q=QT),
                            bcast(ident[:BT, 0:BT].rearrange("p (t b) -> p t b", t=TILES), QT),
                            keepq[:, :].unsqueeze(1).unsqueeze(1).to_broadcast([BT, TILES, B, QT]), ALU.mult).then_inc(plan_hot, 1)
            v.wait_ge(fold_ev, 8)
            v.tensor_reduce(MS[:, :], MO.rearrange("p h j -> p j h"), AX.X, ALU.add).then_inc(fold_sum, 1)

            def key_squares(b, k):
                v.wait_ge(key_sq, b + 1)
                v.tensor_reduce(sumsq[:, bass.ds(b, 1), :], msq[k][:CP, :].rearrange("p (a c d) -> p a c d", a=1, d=D),
                                AX.X, ALU.add).then_inc(key_ss, 1)

            for b in range(KEY_BUFS):
                key_squares(b, b % 2)
            v.wait_ge(plan_list, 1)
            step(v.tensor_scalar(item_bt[0:1, 0:ITEMS], ps[0:1, 4, 0:ITEMS], float(NOTHING), None, ALU.add))
            step(v.tensor_scalar(item_dst[0:1, 1:ITEMS + 1], ps[0:1, 2, 8:8 + ITEMS], float(UNUSED), None, ALU.add))
            step(v.tensor_copy(item_blk[0:1, 0:ITEMS], ps[0:1, 5, 0:ITEMS]))
            step(v.tensor_scalar(not_first[:, 0:ITEMS], ps[:, 6, 0:ITEMS], -1.0, 1.0, ALU.mult, ALU.add))
            step(v.tensor_scalar(first_neg[:, 0:ITEMS], ps[:, 6, 0:ITEMS], -BIG, None, ALU.mult))
            v.tensor_scalar(item_n[:, :], ps[0:1, 2, 1:2], 1.0, None, ALU.max).then_inc(items_ok, 1)

            with v.Fori(KEY_BUFS // 2, B // 2) as i:
                for k in range(2):
                    key_squares(v.snap(i * 2 + k), k)
            v.wait_ge(key_sum, B + 2)
            v.tensor_reduce(mean_rows[:, :], ps[:B, 3, 0:CC // 4 * 128].rearrange("p (c d) -> p d c", d=D), AX.X, ALU.add).then_inc(mean_ev, 1)

            def block_maximum(j, k):
                v.wait_ge(s_mm, j + 3)
                v.scalar_tensor_tensor(m_before[:, k:k + 1], m_run[:, :], not_first[:, bass.ds(j, 1)],
                                       first_neg[:, bass.ds(j, 1)], ALU.mult, ALU.add).then_inc(m_prev, 1)
                v.tensor_reduce(m_block[:, k:k + 1], ps[:, k, 0:KN], AX.X, ALU.max).then_inc(s_max, 1)
                v.wait_ge(m_prev, j + 1)
                v.wait_ge(s_max, j + 1)
                v.tensor_tensor(m_run[:, :], m_block[:, k:k + 1], m_before[:, k:k + 1], ALU.max).then_inc(m_new, 1)
                v.wait_ge(m_new, j + 1)
                v.tensor_scalar(m_minus[:, k:k + 1], m_run[:, :], -1.0, None, ALU.mult).then_inc(m_neg, 1)

            def accumulate(j, k):
                v.wait_ge(p_exp, j + 1)
                v.scalar_tensor_tensor(l_run[:, :], l_run[:, :], rescale[:, k:k + 1], l_block[:, k:k + 1],
                                       ALU.mult, ALU.add).then_inc(l_ok, 1)
                v.wait_ge(l_ok, j + 1)
                v.reciprocal(l_inv[:, :], l_run[:, :]).then_inc(rl_ok, 1)
                v.wait_ge(o_mm, j + 3)
                v.scalar_tensor_tensor(acc, acc, rescale[:, k:k + 1], ps[:, 3, 0:128],
                                       ALU.mult, ALU.add).then_inc(acc_ok, 1)
                v.wait_ge(acc_ok, j + 1)
                v.wait_ge(rl_ok, j + 1)
                v.tensor_scalar(On, acc, l_inv[:, :], None, ALU.mult).then_inc(on_ok, 1)

            n = v.value_load(item_n[0:1, 0:1], min_val=1, max_val=ITEMS)
            block_maximum(0, 0)
            with v.Fori(0, (n + 1) // 2) as i:
                for k in range(2):
                    j = v.snap(i * 2 + k)
                    block_maximum(j + 1, 1 - k)
                    accumulate(j, k)
            keep, base, part = cen, sq, rstd
            v.wait_ge(mean_mm, 1)
            v.tensor_copy(meanT[:, :], ps[:, 7, 0:B]).then_inc(mean_ev, 1)
            v.wait_ge(gates_ok, 1)
            step = chain(y_keep)
            step(v.tensor_tensor(gate_bout[:, :], bout[:, :], gates[:, 0:1], ALU.mult), wait=False)
            v.wait_ge(keep_mm, 1)
            for h in range(2):
                step(v.tensor_scalar(keep[:, half(h)], ps[:, h, 0:HALF], gates[:, 0:1], None, ALU.mult), wait=(h == 1))
            step(v.tensor_scalar(base, keep, -1.0, gates[:, 0:1], ALU.mult, ALU.add))
            base3 = base.rearrange("p (b s) -> p b s", b=B)
            v.wait_ge(ymean_mm, 1)
            step(v.tensor_copy(ymean[:, :], ps[:, 7, 0:B]))
            step(v.tensor_tensor(base3, base3, bcast(ymean[:, :], S), ALU.mult))
            step(v.scalar_tensor_tensor(base, base, gate_bout[:, :], xT[:, :], ALU.add, ALU.add))
            v.wait_ge(rk_sd, 1)
            v.reciprocal(rkey[:, :, :], rms[:, :, :]).then_inc(rk_ok, 1)
            for h in range(2):
                v.wait_ge(y_mm, h + 1)
                step(v.tensor_tensor(part[:, half(h)], ps[:, 5 + h, 0:HALF], keep[:, half(h)], ALU.mult))
                v.tensor_tensor(xT[:, half(h)], part[:, half(h)], base[:, half(h)], ALU.add).then_inc(x_new, 1)
            v.wait_ge(x_new, 2)
            ln(1)

            step = chain(rt0)
            v.wait_ge(sc0_ok, 1)
            step(v.tensor_tensor(bi0[:, :, :], sc0[:, :, :], over_tiles(gb0[:, :]), ALU.add))
            for j in range(NT):
                step(v.max(top8[:, j, :], bi0[:, j, :]), wait=j == NT - 1)
            for j in range(NT):
                step(v.max_index(idx8[:, j, :], top8[:, j, :], bi0[:, j, :]), wait=j == NT - 1)
            step(v.tensor_copy(idxf[:, :, :], idx8[:, :, :]))
            step(v.tensor_tensor(msk[:, :, :], over_tiles(iota_e[:, 0:E0]), bcast(idxf[:, :, 0], E0), ALU.is_equal))
            for k in range(1, TOP0):
                step(v.tensor_tensor(hot[:, :, :], over_tiles(iota_e[:, 0:E0]), bcast(idxf[:, :, k], E0), ALU.is_equal))
                step(v.tensor_tensor(msk[:, :, :], msk[:, :, :], hot[:, :, :], ALU.add))
            step(v.tensor_tensor(msk[:, :, :], msk[:, :, :], sc0[:, :, :], ALU.mult))
            step(v.tensor_reduce(den[:, :], msk[:, :, :], AX.X, ALU.add))
            step(v.reciprocal(den[:, :], den[:, :]))
            step(v.tensor_scalar(den[:, :], den[:, :], ROUTE, None, ALU.mult))
            v.tensor_tensor(msk[:, :, :], msk[:, :, :], bcast(den[:, :], E0), ALU.mult).then_inc(comb_ok, 1)
            v.wait_ge(combT_mm, 1)
            for h in range(2):
                v.tensor_copy(combT[:E0, half(h)], ps[:E0, 4 + h, 0:HALF]).then_inc(combT_ok, 1)
            for j in range(2 * (PAIRS + 1)):
                p = 128 if j // 2 < PAIRS else F0
                v.wait_ge(e0_act, j + 1)
                if j >= 2:
                    v.wait_ge(e0_y, j - 1)
                v.tensor_tensor(hh[j % 2][:p, :], sg[j % 2][:p, :], ps[:p, 2 * (j % 2) + 1, 0:HALF], ALU.mult).then_inc(e0_up, 1)
                v.wait_ge(e0_up, j + 1)
                if j // 2 < PAIRS:
                    v.tensor_tensor(hh[j % 2], hh[j % 2], ps[:, 6 + j % 2, 0:HALF], ALU.mult).then_inc(e0_h, 1)
            v.wait_ge(e0_y, 2 * (PAIRS + 1))
            for h in range(2):
                v.scalar_tensor_tensor(xT[:, half(h)], ps[:, 4 + h, 0:HALF], gates[:, 2:3], xT[:, half(h)],
                                       ALU.mult, ALU.add).then_inc(x_new, 1)
            v.wait_ge(x_new, 4)
            ln(2)

            v.tensor_scalar(hb[:, :], bih[:, :], 0.5, None, ALU.mult).then_inc(hb_ok, 1)
            v.wait_ge(hb_ok, 1)
            v.scalar_tensor_tensor(hb[:, :], bhh[:, :], 0.5, hb[:, :], ALU.mult, ALU.add).then_inc(hb_ok, 1)
            v.tensor_scalar(wkey_s[:, :], wkey[:, :], float(D) ** -0.5, None, ALU.mult).then_inc(hb_ok, 1)
            v.wait_ge(rk_ok, 1)
            v.wait_ge(ln_out, 6)
            v.wait_ge(hb_ok, 3)

            def maxima(g, k, u, m):
                (s, h), a, b, n = divmod(m, 2), m // 2 % 2, g * GB + k * QB + m // 2, u * HB + m
                c = slice(h * CH, (h + 1) * CH)
                v.wait_ge(a_mm, n + 1)
                v.tensor_reduce(mx[:, a, c], ps[:CP, 2 + 2 * a + h, 0:CH * S].rearrange("p (c s) -> p c s", s=S),
                                AX.X, ALU.max).then_inc(a_max, 1)
                v.wait_ge(a_max, n + 1)
                v.scalar_tensor_tensor(nb[:, a, c], mx[:, a, c], -1.0, rkey[:, b, c], ALU.mult, ALU.mult).then_inc(a_neg, 1)

            def attention(g, k, u, m):
                (s, h), a, b, n = divmod(m, 2), m // 2 % 2, g * GB + k * QB + m // 2, u * HB + m
                c = slice(h * CH, (h + 1) * CH)
                v.wait_ge(a_exp, n + 1)
                v.reciprocal(rs[:, a, c], sm[:, a, c]).then_inc(a_rec, 1)
                v.wait_ge(a_rec, n + 1)
                v.tensor_tensor(rs[:, a, c], rs[:, a, c], rkey[:, b, c], ALU.mult).then_inc(a_w, 1)
                v.wait_ge(a_w, n + 1)
                v.tensor_tensor(A[a][:CP, c, :], A[a][:CP, c, :], bcast(rs[:, a, c], S), ALU.mult).then_inc(a_att, 1)

            def update(u, s):
                n, a = u * QB + s, s % 2
                v.wait_ge(u_mm, n + 1)
                v.tensor_scalar(zr[:, a, :], ps[:S, 6 + a, 128:KW], 1e-6, None, ALU.add).then_inc(z_add, 1)
                v.wait_ge(z_add, n + 1)
                v.reciprocal(zr[:, a, :], zr[:, a, :]).then_inc(z_rec, 1)
                v.wait_ge(z_rec, n + 1)
                v.tensor_scalar(UnN[:S, s, :], ps[:S, 6 + a, 0:128], zr[:, a, :], None, ALU.mult).then_inc(un_ok, 1)

            def gru_inputs(v_):
                v.wait_ge(ut_mm, v_ + 1)
                v.tensor_scalar(Un, ps[:, 1, 0:QS], wkey[:, 0:1], None, ALU.mult).then_inc(u_ok, 1)
                v.tensor_scalar(hn, ps[:, 1, QS:2 * QS], bhh[:, 2:3], None, ALU.add).then_inc(hn_ok, 1)

            def gru_candidate(v_):
                v.wait_ge(hn_ok, v_ + 1)
                v.wait_ge(gru_t, v_ * 2 + 2)
                v.scalar_tensor_tensor(tmp, rt, 1.0, hn, ALU.add, ALU.mult).then_inc(gru_v, 1)
                v.wait_ge(gru_v, v_ * 2 + 1)
                v.scalar_tensor_tensor(tmp, tmp, 0.5, ps[:, 1, 0:QS], ALU.mult, ALU.add).then_inc(gru_v, 1)

            def gru_slots_new(v_, k, dst):
                v.wait_ge(gru_n, v_ + 1)
                v.tensor_tensor(rt, slots_x[:, k, :], nt, ALU.subtract).then_inc(gru_new, 1)
                v.wait_ge(gru_new, v_ * 2 + 1)
                v.scalar_tensor_tensor(rt, zt, 1.0, rt, ALU.add, ALU.mult).then_inc(gru_new, 1)
                v.wait_ge(gru_new, v_ * 2 + 2)
                return v.scalar_tensor_tensor(dst, rt, 0.5, nt, ALU.mult, ALU.add)

            def finish(v_, g, k):
                gru_slots_new(v_, k, tmp).then_inc(gru_last, 1)
                v.wait_ge(gru_last, g * 2 + k + 1)
                v.scalar_tensor_tensor(xT[:, quad(g, k)], tmp, gates[:, 1:2], xT[:, quad(g, k)], ALU.mult, ALU.add).then_inc(x_new, 1)

            def slot_norm(u, k):
                v.wait_ge(q_sd, u + 1)
                v.reciprocal(rstd1, rstd1).then_inc(q_rec, 1)
                v.wait_ge(q_rec, u + 1)
                v.scalar_tensor_tensor(sn, slots_x[:, k, :], wslot[:, 0:1], rstd1, ALU.mult, ALU.mult).then_inc(q_sn, 1)

            def queries(u, k):
                v.wait_ge(q_mm, u + 1)
                v.tensor_scalar(qT[:, k, 0:QS], ps[:, 1, 0:QS], wkey_s[:, :], None, ALU.mult).then_inc(q_ok, 1)

            v.tensor_copy(slots_x[:, 0, :], xln[:, quad(0, 0)]).then_inc(sl_ok, 1)
            v.wait_ge(sl_ok, 1)
            slot_norm(0, 0)
            v.wait_ge(q_pad, 1)
            queries(0, 0)
            maxima(0, 0, 0, 0)
            maxima(0, 0, 0, 1)
            attention(0, 0, 0, 0)

            def phase(g, w, u):
                k = w % 2
                gru = (g, w) != (0, 0)
                for m in range(HB):
                    if m == 0 and gru:
                        update(u - 1, QB - 1)
                        gru_inputs(u - 1)
                    if m + 2 < HB:
                        maxima(g, k, u, m + 2)
                    elif prepares(g, w):
                        maxima(g + w // (PHASES - 1), 1 - k, u + 1, m + 2 - HB)
                    if m == 5 and prepares(g, w):
                        queries(u + 1, 1 - k)
                    if m + 1 < HB:
                        attention(g, k, u, m + 1)
                    elif prepares(g, w):
                        attention(g + w // (PHASES - 1), 1 - k, u + 1, 0)
                    if m == 0 and gru:
                        gru_candidate(u - 1)
                    if m == 1:
                        if w in (0, PHASES - 1):
                            if gru:
                                finish(u - 1, g - (w == 0), 1 - k)
                            if loads_next(g, w):
                                v.tensor_copy(slots_x[:, 1 - k, :], xln[:, quad(g + (w > 0), 1 - k)]).then_inc(sl_ok, 1)
                        else:
                            gru_slots_new(u - 1, 1 - k, slots_x[:, 1 - k, :]).then_inc(sl_ok, 1)
                    if m in (2, 4, 6):
                        update(u, m // 2 - 1)
                    if m == 3 and prepares(g, w):
                        v.wait_ge(sl_ok, u + 2)
                        slot_norm(u + 1, 1 - k)

            phases(v, phase)
            last = GROUPS * PHASES - 1
            update(last, QB - 1)
            gru_inputs(last)
            gru_candidate(last)
            finish(last, GROUPS - 1, 1)
            v.wait_ge(x_new, 4 + 2 * GROUPS)
            ln(3)

            step = chain(rt1)
            v.wait_ge(lg1_mm, 1)
            logits = ps[:, 0, 0:NT * E1].rearrange("p (n e) -> p n e", n=NT)
            step(v.tensor_tensor(lg, logits, over_tiles(gb1[:, :]), ALU.add))
            step(v.tensor_reduce(r1[:, :], lg, AX.X, ALU.max))
            step(v.tensor_tensor(lg, lg, bcast(r1[:, :], E1), ALU.subtract))
            v.wait_ge(rt1_exp, 1)
            step(v.tensor_reduce(r2[:, :], pr, AX.X, ALU.add))
            step(v.reciprocal(r2[:, :], r2[:, :]))
            step(v.tensor_tensor(pr, pr, bcast(r2[:, :], E1), ALU.mult))
            for j in range(NT):
                step(v.max(top8[:, j, :], pr[:, j, :]), wait=j == NT - 1)
            for j in range(NT):
                step(v.max_index(idx8[:, j, :], top8[:, j, :], pr[:, j, :]), wait=j == NT - 1)
            step(v.tensor_copy(idxf[:, :, :], idx8[:, :, :]))
            for k in range(TOP1):
                step(v.tensor_tensor(oh[k], over_tiles(iota_e[:, :]), bcast(idxf[:, :, k], E1), ALU.is_equal))
            v.tensor_tensor(ohb, oh[0], oh[1], ALU.add).then_inc(rt1_hot, 1)
            v.wait_ge(pos_mm, 1)
            places = ps[:, 1, 0:NT * E1].rearrange("p (n e) -> p n e", n=NT)
            for k in range(TOP1):
                step(v.tensor_tensor(posx, oh[k], places, ALU.mult))
                step(v.tensor_reduce(posk[:, k, :], posx, AX.X, ALU.add))
            step(v.tensor_scalar(valid[:, :, :], posk[:, :, :], float(CAP), None, ALU.is_lt))
            for k in range(TOP1):
                step(v.scalar_tensor_tensor(posk[:, k, :], idxf[:, :, k], float(CAP), posk[:, k, :], ALU.mult, ALU.add))
            step(v.tensor_tensor(posk[:, :, :], posk[:, :, :], valid[:, :, :], ALU.mult))
            v.tensor_copy(gidx[:, :, :], posk[:, :, :]).then_inc(slot_ok, 1)
            step(v.tensor_tensor(wk[:, :, :], trash[:, :, :], valid[:, :, :], ALU.mult))
            step(v.tensor_tensor(wk[:, :, :], trash[:, :, :], wk[:, :, :], ALU.subtract))
            v.tensor_tensor(sidx[:, :, :], posk[:, :, :], wk[:, :, :], ALU.add).then_inc(slot_ok, 1)
            step(v.tensor_tensor(r1[:, :], top8[:, :, 0], top8[:, :, 1], ALU.add))
            step(v.reciprocal(r1[:, :], r1[:, :]))
            v.wait_ge(slot_ok, 2)
            for k in range(TOP1):
                step(v.scalar_tensor_tensor(wk[:, k, :], top8[:, :, k], gates[:, 3:4], r1[:, :], ALU.mult, ALU.mult))
            step(v.tensor_tensor(wk[:, :, :], wk[:, :, :], valid[:, :, :], ALU.mult))
            for e in range(E1):
                v.wait_ge(h_mm, e + 1)
                if e >= 2:
                    v.wait_ge(h_ok, e - 1)
                v.tensor_tensor(hx[e % 2][:, :, :], ps[:, e % 2, 0:FC * CAP].rearrange("p (c n) -> p c n", c=FC),
                                bcast(b1T[:, e, :], CAP), ALU.add).then_inc(h_b, 1)
                if e % 4 == 3:
                    g = e // 4
                    v.wait_ge(ye_mm, e + 1)
                    v.tensor_tensor(ysT[:, 4 * g * CAP:4 * (g + 1) * CAP].rearrange("p (c n) -> p c n", c=4),
                                    ps[:, 2 + g % 2, 0:4 * CAP].rearrange("p (c n) -> p c n", c=4),
                                    bcast(b2T[:, 4 * g:4 * g + 4], CAP), ALU.add).then_inc(ye_ok, 1)
            v.wait_ge(ld_yg, 16 * TOP1 * NT)
            v.wait_ge(st_xe, 16 * TOP1 * NT)
            for j in range(NT):
                v.scalar_tensor_tensor(xtok[:, j, :], yg[:, 0, j * 128:(j + 1) * 128], wk[:, 0, j:j + 1], rtok[:, j, :],
                                       ALU.mult, ALU.add).then_inc(out_s, 1)
            v.wait_ge(out_s, NT)
            for j in range(NT):
                v.scalar_tensor_tensor(xtok[:, j, :], yg[:, 1, j * 128:(j + 1) * 128], wk[:, 1, j:j + 1], xtok[:, j, :],
                                       ALU.mult, ALU.add).then_inc(out_s, 1)

        @block.tensor
        def _(pe):
            def ln(k):
                for h in range(2):
                    if k:
                        pe.wait_ge(x_new, 4 + 2 * GROUPS if k == 3 else 2 * k - 1 + h)
                    pe.matmul(ps[:, h, 0:HALF], mean_w[:, :], xT[:, half(h)], start=True, stop=True).then_inc(ln_mean, 1)
                for h in range(2):
                    pe.wait_ge(ln_sq, 2 * k + h + 1)
                    pe.matmul(ps[:, 2 + h, 0:HALF], mean_w[:, :], sq[:, half(h)], start=True, stop=True).then_inc(ln_var, 1)

            pe.wait_ge(const, CONSTS)
            pe.wait_ge(ld_x, 16)
            ln(0)
            pe.wait_ge(ld_attn, 64)
            for f, (left, right) in enumerate(((wqT, wkT), (wvT, wo))):
                for q in range(4):
                    if f:
                        pe.wait_ge(fold_ev, q + 1)
                    r0 = DH * (q % 2)
                    for m in range(4):
                        pair = 4 * (q // 2) + m
                        mm = pe.matmul(ps[:, 4 + q, m * 128:(m + 1) * 128], left[r0:r0 + DH, pair, :],
                                       right[r0:r0 + DH, pair, :], start=True, stop=True)
                    mm.then_inc(fold_mm, 1)
            pe.wait_ge(fold_ev, 8)
            pe.wait_ge(ln_out, 2)
            pe.wait_ge(plan_rs, 1)
            pe.matmul(ps[:BT, 2, 0:1], before[:BT, 0:BT], rowsum[:, :], start=True, stop=True).then_inc(plan_rank, 1)
            pe.matmul(ps[0:1, 2, 1:2], ones[:BT, 0:1], rowsum[:, :], start=True, stop=True).then_inc(plan_rank, 1)
            for i in range(B // KEY_BUFS):
                for head in range(i * KEY_BUFS, (i + 1) * KEY_BUFS):
                    for h in range(2):
                        if head:
                            pe.wait_ge(qa_ev, 2 * head - 1 + h)
                        pe.matmul(ps[:, h, 0:HALF], G[:, head, :], xln[:, half(h)], start=True, stop=True).then_inc(qa_mm, 1)
                for b in range(i * KEY_BUFS, (i + 1) * KEY_BUFS):
                    pe.wait_ge(key_add3, b + 2)
                    pe.matmul(ps[:B, 3, 0:CC // 4 * 128], key_sel[:, b, :], padd[b % 2][:CP, :],
                              start=(b == 0), stop=(b == B - 1), skip_group_check=True).then_inc(key_sum, 1)
                if i == 0:
                    pe.wait_ge(plan_hot, KB)
                    pe.wait_ge(plan, PLAN_LISTS)
                    for bank, col, left in ((4, 0, lambda b: lists_w[:, b, 0:1]), (5, 0, lambda b: lists_w[:, b, 1:2]),
                                            (2, 8, lambda b: lists_w[:, b, 2:3]), (6, 0, lambda b: first_w[:, b, :])):
                        rows = 128 if bank == 6 else 1
                        for blk in range(KB):
                            mm = pe.matmul(ps[:rows, bank, col:col + ITEMS], left(blk), hot_r[blk][:BT, :],
                                           start=(blk == 0), stop=(blk == KB - 1))
                    mm.then_inc(plan_list, 1)
            pe.wait_ge(items_ok, 1)

            def item_scores(j, k, loads):
                pe.wait_ge(ld_itemT[k], loads)
                pe.wait_ge(q_tile, j + 1)
                pe.matmul(ps[:, k, 0:KN], Qk[k], ictxT[k], start=True, stop=False)
                pe.matmul(ps[:, k, 0:KN], ones_b[0:1, :], mask_b[k][0:1, 0:KN], start=False, stop=True).then_inc(s_mm, 1)

            def transpose_result(j):
                pe.wait_ge(on_ok, j + 1)
                pe.wait_ge(ot_ev, j + 1)
                pe.matmul(ps[:, 4, 0:128], On, ident[:, :], start=True, stop=True).then_inc(ot_mm, 1)

            n = pe.value_load(item_n[0:1, 0:1], min_val=1, max_val=ITEMS)
            item_scores(0, 0, 32)
            with pe.Fori(0, (n + 1) // 2) as i:
                for k in range(2):
                    j = pe.snap(i * 2 + k)
                    pe.wait_ge(p_exp, j + 1)
                    for c in range(KC):
                        mm = pe.transpose(ps[:KP, 2, c * 128:(c + 1) * 128],
                                          P.rearrange("p (m c) -> p c m", c=KC)[:, c, :], ident[:, :])
                    mm.then_inc(pt_mm, 1)
                    item_scores(j + 1, 1 - k, i * 32 + (32, 64)[k])
                    transpose_result(j)
                    pe.wait_ge(pt_ev, j + 1)
                    pe.wait_ge(ld_item[k], i * 16 + 16)
                    for c in range(KC):
                        mm = pe.matmul(ps[:, 3, 0:128], PT[:KP, c, :], ictx[k][:KP, c, :], start=(c == 0), stop=(c == KC - 1))
                    mm.then_inc(o_mm, 1)
            last = pe.snap((n + 1) // 2 * 2)
            transpose_result(last)
            pe.wait_ge(mean_ev, 1)
            pe.matmul(ps[:, 7, 0:B], mean_rows[:, :], ident[:B, 0:B], start=True, stop=True).then_inc(mean_mm, 1)
            pe.wait_ge(plan_hot, KB + 1)
            pe.wait_ge(p_exp, last + 1)
            for h in range(2):
                mm = pe.matmul(ps[:, h, 0:HALF], ones[:BT, :], keep_d[:BT, half(h)], start=True, stop=True)
            mm.then_inc(keep_mm, 1)
            pe.wait_ge(fold_sum, 1)
            pe.wait_ge(mean_ev, 2)
            pe.matmul(ps[:, 7, 0:B], MS[:, :], meanT[:, :], start=True, stop=True).then_inc(ymean_mm, 1)
            pe.wait_ge(ot_ev, last + 2)
            for h in range(2):
                for head in range(H):
                    mm = pe.matmul(ps[:, 5 + h, 0:HALF], MO[:, head, :], tilesT[:, head, half(h)],
                                   start=(head == 0), stop=(head == H - 1))
                mm.then_inc(y_mm, 1)
            ln(1)

            pe.wait_ge(ld_small, 16 * SMALL)
            pe.wait_ge(ln_out, 4)
            for j in range(NT):
                mm = pe.matmul(ps[:, 4, j * E0:(j + 1) * E0], xln[:, j * 128:(j + 1) * 128], gw0[:, :], start=True, stop=True)
            mm.then_inc(lg0_mm, 1)
            pe.wait_ge(comb_ok, 1)
            for j in range(NT):
                c = j * 128
                for c0, c1 in ((c, min(c + 128, max(c, HALF))), (max(c, min(HALF, c + 128)), c + 128)):
                    if c1 > c0:
                        mm = pe.transpose(ps[:E0, 4 + c0 // HALF, c0 % HALF:c0 % HALF + c1 - c0],
                                          msk[c0 - c:c1 - c, j, :], ident[c0 - c:c1 - c, c0 - c:c1 - c])
            mm.then_inc(combT_mm, 1)
            pe.wait_ge(ld_ffn0, 32)
            pe.wait_ge(pair_ok, 2)

            def shares(j):
                pair, h = divmod(j, 2)
                p = 128 if pair < PAIRS else F0
                if j >= 2:
                    pe.wait_ge(e0_up, j - 1)
                    if j - 2 < 2 * PAIRS:
                        pe.wait_ge(e0_h, j - 1)
                for g in range(2):
                    w = w13[:, g, pair * 2 * F0:(pair + 1) * 2 * F0] if pair < PAIRS else ws[:, g * F0:(g + 1) * F0]
                    mm = pe.matmul(ps[:p, 2 * (j % 2) + g, 0:HALF], w, xln[:, half(h)], start=True, stop=True)
                if pair < PAIRS:
                    pe.wait_ge(combT_ok, 2)
                    mm = pe.matmul(ps[:, 6 + j % 2, 0:HALF], pair_sel[:E0, pair, :], combT[:E0, half(h)], start=True, stop=True)
                mm.then_inc(e0_mm, 1)

            def down(j):
                pair, h = divmod(j, 2)
                if pair < PAIRS:
                    pe.wait_ge(e0_h, j + 1)
                else:
                    pe.wait_ge(e0_up, j + 1)
                w, x = (w2p[:, pair, :], hh[j % 2]) if pair < PAIRS else (w2s[:, :], hh[j % 2][:F0, :])
                pe.matmul(ps[:, 4 + h, 0:HALF], w, x, start=(pair == 0), stop=(pair == PAIRS),
                          skip_group_check=True).then_inc(e0_y, 1)

            last = 2 * (PAIRS + 1)
            shares(0)
            for j in range(last):
                if j + 1 < last:
                    shares(j + 1)
                down(j)
            ln(2)

            pe.matmul(ps[:, 4, 0:128], wq1[:, :], wk1[:, :], start=True, stop=True).then_inc(g1_mm, 1)
            pe.matmul(ps[:, 5, 0:3 * D], wv1[:, :], wih[:, :], start=True, stop=True).then_inc(g1_mm, 1)
            pe.wait_ge(g1_ev, 2)

            def scores(g, k, u, m):
                (s, h), a, n = divmod(m, 2), m // 2 % 2, u * HB + m
                pe.wait_ge(q_ok, u + 1)
                pe.wait_ge(ld_keys[k * QB + s], (g + 1) * 48)
                if not isinstance(n, int) or n >= 4:
                    pe.wait_ge(a_exp, n - 3)
                for c in range(CH):
                    mm = pe.matmul(ps[:CP, 2 + 2 * a + h, c * S:c * S + WIDE],
                                   keysT[:, k * QB + s, :].rearrange("p (m c) -> p c m", c=CC)[:, h * CH + c, :],
                                   qT[:, k, s * S:s * S + WIDE], start=True, stop=True)
                mm.then_inc(a_mm, 1)

            def update(g, k, u, m):
                (s, h), a, n = divmod(m, 2), m // 2 % 2, u * QB + m // 2
                pe.wait_ge(a_att, u * HB + (m + 1))
                if h == 0:
                    pe.wait_ge(key_col, g * GB + k * QB + s + 1)
                    if not isinstance(n, int) or n >= 2:
                        pe.wait_ge(un_ok, n - 1)
                for c in range(h * CH, (h + 1) * CH):
                    mm = pe.matmul(ps[:S, 6 + a, 0:KW], A[a][:CP, c, :], keys[:, k * QB + s, c, :],
                                   start=(c == 0), stop=(c == CC - 1), skip_group_check=True)
                if h == 1:
                    mm.then_inc(u_mm, 1)

            def gru_start(v_, k):
                if not isinstance(v_, int) or v_ > 0:
                    pe.wait_ge(gru_v, v_ * 2)
                for gate in range(2):
                    pe.matmul(ps[:, 0, gate * QS:(gate + 1) * QS], whh[:, gate * D:(gate + 1) * D],
                              slots_x[:, k, :], start=(gate == 0), stop=False, skip_group_check=True)
                pe.wait_ge(un_ok, (v_ + 1) * QB)
                pe.matmul(ps[:, 1, QS:2 * QS], whh[:, 2 * D:3 * D], slots_x[:, k, :], start=True, stop=True)
                for s in range(QB):
                    mm = pe.transpose(ps[:, 1, s * S:(s + 1) * S], UnN[:S, s, :], ident[:S, 0:S])
                mm.then_inc(ut_mm, 1)

            def gru_gates(v_):
                pe.wait_ge(u_ok, v_ + 1)
                for gate in range(2):
                    pe.matmul(ps[:, 0, gate * QS:(gate + 1) * QS], F1w[:, gate * D:(gate + 1) * D], Un,
                              start=False, stop=True, skip_group_check=True)
                pe.wait_ge(hn_ok, v_ + 1)
                pe.matmul(ps[:, 1, 0:QS], F1w[:, 2 * D:3 * D], Un, start=True, stop=True).then_inc(gate_mm, 1)

            def slot_var(u):
                pe.wait_ge(q_sq, u + 1)
                pe.matmul(ps[:, 0, 0:QS], mean_w[:, :], sq1, start=True, stop=True).then_inc(q_var, 1)

            def queries(u):
                pe.wait_ge(q_sn, u + 1)
                pe.matmul(ps[:, 1, 0:QS], G1[:, :], sn, start=True, stop=True).then_inc(q_mm, 1)

            slot_var(0)
            queries(0)
            scores(0, 0, 0, 0)
            scores(0, 0, 0, 1)

            def phase(g, w, u):
                k = w % 2
                gru = (g, w) != (0, 0)
                for m in range(HB):
                    if m == 0 and gru:
                        gru_start(u - 1, 1 - k)
                    if m == 3 and prepares(g, w):
                        slot_var(u + 1)
                    if m + 2 < HB:
                        scores(g, k, u, m + 2)
                    elif prepares(g, w):
                        scores(g + w // (PHASES - 1), 1 - k, u + 1, m + 2 - HB)
                    if m == 0 and gru:
                        gru_gates(u - 1)
                    if m == 5 and prepares(g, w):
                        queries(u + 1)
                    update(g, k, u, m)

            phases(pe, phase)
            gru_start(GROUPS * PHASES - 1, 1)
            gru_gates(GROUPS * PHASES - 1)
            ln(3)

            pe.wait_ge(ln_out, 8)
            for j in range(NT):
                mm = pe.matmul(ps[:, 0, j * E1:(j + 1) * E1], xln[:, j * 128:(j + 1) * 128], gw1[:, :], start=True, stop=True)
            mm.then_inc(lg1_mm, 1)
            for c in range(4):
                src = (xln, xT)[c // 2]
                j0, j1 = ((0, 4), (4, NT))[c % 2]
                for j in range(j0, j1):
                    mm = pe.transpose(ps[:, 4 + c, (j - j0) * 128:(j - j0 + 1) * 128], src[:, j * 128:(j + 1) * 128], ident[:, :])
                mm.then_inc(tok_mm, 1)
            pe.wait_ge(rt1_hot, 1)
            for j in range(NT):
                for i in range(j + 1):
                    mm = pe.matmul(ps[:, 1, j * E1:(j + 1) * E1], before_b[:, :] if i == j else ones_b[:, :],
                                   ohb[:, i, :], start=(i == 0), stop=(i == j))
            mm.then_inc(pos_mm, 1)
            pe.wait_ge(ld_xe, 32)
            pe.wait_ge(tok_ev, 4)
            for c in range(5):
                if c >= 2:
                    pe.wait_ge(xe_ev, c - 1)
                for j in range(4 * c, min(4 * c + 4, ST)):
                    mm = pe.transpose(ps[:, 4 + c % 2, j % 4 * 128:(j % 4 + 1) * 128], xe[:, j, :], ident[:, :])
                mm.then_inc(xe_mm, 1)

            def weights(e):
                return early_w[:, e, :] if e < EARLY else late_w[:, e - EARLY, :]

            def hidden(e):
                if e == 0:
                    pe.wait_ge(ld_early, 16)
                    pe.wait_ge(wide_ok, 3)
                if e >= EARLY and (e - EARLY) % 4 == 0:
                    pe.wait_ge(ld_late[(e - EARLY) // 4], 16)
                pe.wait_ge(xe_ev, min(5, ((e + 1) * CAP - 1) // 512 + 1))
                if e >= 2:
                    pe.wait_ge(h_b, e - 1)
                for c in range(FC):
                    mm = pe.matmul(ps[:, e % 2, c * CAP:c * CAP + WIDE], weights(e)[:, c * 128:(c + 1) * 128],
                                   xeT[:, e * CAP:e * CAP + WIDE], start=True, stop=True)
                mm.then_inc(h_mm, 1)

            def result(e):
                g = e // 4
                if e % 4 == 0 and g >= 2:
                    pe.wait_ge(ye_ok, g - 1)
                pe.wait_ge(h_ok, e + 1)
                for c in range(FC):
                    mm = pe.matmul(ps[:, 2 + g % 2, e % 4 * CAP:e % 4 * CAP + WIDE], weights(e)[:, F1 + c * 128:F1 + (c + 1) * 128],
                                   hT[e % 2][:, c * CAP:c * CAP + WIDE], start=(c == 0), stop=(c == FC - 1))
                mm.then_inc(ye_mm, 1)

            hidden(0)
            for e in range(E1):
                if e + 1 < E1 and e % 4 != 3:
                    hidden(e + 1)
                result(e)
                if e + 1 < E1 and e % 4 == 3:
                    hidden(e + 1)
            pe.wait_ge(ye_ok, E1 // 4)
            for c in range(5):
                if c >= 2:
                    pe.wait_ge(yt_ev, c - 1)
                for j in range(4 * c, min(4 * c + 4, ST)):
                    mm = pe.transpose(ps[:, 6 + c % 2, j % 4 * 128:(j % 4 + 1) * 128], ysT[:, j * 128:(j + 1) * 128], ident[:, :])
                mm.then_inc(yt_mm, 1)


SMALL = 20
CONSTS = 27
PLAN_LISTS = 34


def kernel(**inputs):
    import numpy as np
    import concourse.bacc as _bacc
    from concourse import mybir as _mybir
    from concourse.bass_utils import run_bass_kernel_spmd as _run

    a = {k: np.asarray(v) for k, v in inputs.items()}

    def heads(w):
        return w.T.reshape(H // 2, 2 * DH, D).transpose(1, 0, 2)

    ctx = a["ctx_1024"]
    wkv = a["L0_xattn_Wkv"]
    w13 = a["L0_ffn_w13"]
    arrays = {
        "xT": a["x"].reshape(T, D).T,
        "ctx": ctx,
        "ctxT": ctx.transpose(0, 2, 1),
        "ctx_blk": ctx.reshape(B * KB, KN, D),
        "ctxT_blk": ctx.reshape(B * KB, KN, D).transpose(0, 2, 1),
        "kv_mask": a["mask_BxS2_bk0"],
        "kv_blk": a["mask_BxS2_bk0"].reshape(B * KB, KN),
        "q_mask": a["mask_BxS_bk0"].reshape(B, TILES, QT).transpose(1, 0, 2).reshape(BT, QT),
        "wqT": heads(a["L0_xattn_Wq"]),
        "wkT": heads(wkv[:, 0:H * DH]),
        "wvT": heads(wkv[:, H * DH:]),
        "wo": a["L0_xattn_Wout"].reshape(H // 2, 2 * DH, D).transpose(1, 0, 2),
        "bout": a["L0_xattn_bout"].reshape(D, 1),
        "g_xattn": a["g_xattn"].reshape(1, 2),
        "g_ffn": a["g_ffn"].reshape(1, 2),
        "gw0": a["L0_ffn_gate_w"].T,
        "gb0": a["L0_ffn_gate_b"].reshape(1, E0),
        "w13": w13.reshape(E0, 2, F0, D).transpose(3, 1, 0, 2).reshape(D, 2, E0 * F0),
        "w2p": a["L0_ffn_w2"].transpose(0, 2, 1).reshape(PAIRS, 2 * F0, D).transpose(1, 0, 2),
        "ws": a["L0_ffn_w13_s"].T,
        "w2s": a["L0_ffn_w2_s"].T,
        "wq1": a["L1_xattn_Wq"],
        "wk1": a["L1_xattn_Wk"],
        "wv1": a["L1_xattn_Wv"],
        "wih": a["L1_xattn_gru_wih"].T,
        "whh": a["L1_xattn_gru_whh"].T,
        "bih": a["L1_xattn_gru_bih"].reshape(3, D).T,
        "bhh": a["L1_xattn_gru_bhh"].reshape(3, D).T,
        "wslot": a["L1_xattn_slot_norm_w"].reshape(D, 1),
        "wkey": a["L1_xattn_input_norm_w"].reshape(D, 1),
        "gw1": a["L1_ffn_gate_w"],
        "gb1": a["L1_ffn_gate_b"].reshape(1, E1),
        "b1T": a["L1_ffn_b1"].reshape(E1, FC, 128).transpose(2, 0, 1),
        "b2T": a["L1_ffn_b2"].T,
        "w12": np.concatenate([a["L1_ffn_w1"].transpose(1, 0, 2),
                               a["L1_ffn_w2"].reshape(E1, FC, 128, D).transpose(2, 0, 1, 3).reshape(128, E1, F1)], axis=2),
    }
    arrays = {k: np.ascontiguousarray(v) for k, v in arrays.items()}
    nc = _bacc.Bacc("TRN2", target_bir_lowering=False, num_devices=1)
    tensors = {k: nc.dram_tensor(f"in_{k}", v.shape, U8 if v.dtype == bool else _mybir.dt.from_np(v.dtype),
                                 kind="ExternalInput").ap()
               for k, v in arrays.items()}
    tensors["xe_scratch"] = nc.dram_tensor("xe_scratch", (SLOTS + TOP1 * T, D), _mybir.dt.float32).ap()
    tensors["ys_scratch"] = nc.dram_tensor("ys_scratch", (SLOTS, D), _mybir.dt.float32).ap()
    tensors["out"] = nc.dram_tensor("out_x", (T, D), _mybir.dt.float32, kind="ExternalOutput").ap()
    build_program(nc, tensors)
    r = _run(nc, [{f"in_{k}": v for k, v in arrays.items()}], core_ids=[0])
    return r.results[0]["out_x"].reshape(B, S, D)
```

```python
from contextlib import ExitStack

import concourse.bass as bass
from concourse import mybir

F32 = mybir.dt.float32
BF16 = mybir.dt.bfloat16
I32 = mybir.dt.int32
U32 = mybir.dt.uint32
U8 = mybir.dt.uint8
ALU = mybir.AluOpType
ACT = mybir.ActivationFunctionType
AX = mybir.AxisListType

B, S, D, M = 16, 56, 128, 1500
T = B * S
HALF = T // 2
NT = T // 128
H, DH = 16, 64
QT = 128 // H
TILES = S // QT
BT = B * TILES
KB, KN = 4, M // 4
KP, KC = 125, 3
ITEMS = BT * KB
BIG = 1e30
NOTHING = BT
UNUSED = BT + 1
KEY_BUFS = 4
AHEAD = 2
E0, F0, TOP0, ROUTE = 16, 64, 4, 2.5
PAIRS = E0 // 2
PARTS = 96
CP, CC = 125, 12
GB = 8
GROUPS = B // GB
QB = GB // 2
QS = QB * S
ITERS = 3
HB = 2 * QB
CH = CC // 2
LOOK = 3
PHASES = 2 * ITERS
KW = 129
WIDE = 96
E1, F1, TOP1, CAP = 32, 512, 2, 68
FC = F1 // 128
SLOTS = E1 * CAP
ST = SLOTS // 128
YC = (ST + 3) // 4
TRASH = SLOTS
EARLY = 8


def build_program(nc, t):
    with ExitStack() as ctx:
        def sb(name, shape, dt=F32):
            return ctx.enter_context(nc.sbuf_tensor(name, shape, dt))

        def sem(name):
            return ctx.enter_context(nc.semaphore(name))

        mean_w = sb("mean_w", [128, 128])
        ones = sb("ones", [128, 128])
        ones_b = sb("ones_b", [128, 128], BF16)
        ident = sb("ident", [128, 128])
        before = sb("before", [128, 128])
        before_b = sb("before_b", [128, 128], BF16)
        iota_e = sb("iota_e", [128, E1])
        eps_ln = sb("eps_ln", [128, 1])
        eps_rms = sb("eps_rms", [128, 1])
        mean_rows = sb("mean_rows", [B, 128])
        gates_in = sb("gates_in", [128, 4])
        gates = sb("gates", [128, 4])
        bout = sb("bout", [128, 1])
        xT = sb("xT", [128, T])
        xln = sb("xln", [128, T])
        ln_tiles = sb("ln_tiles", [128, 3 * T])
        cen, sq, rstd = (ln_tiles[:, k * T:(k + 1) * T] for k in range(3))
        ln_s = sb("ln_s", [128, NT])
        folded = sb("folded", [128, 2 * H * 128])
        G = folded[:, 0:H * 128].rearrange("p (h j) -> p h j", h=H)
        MO = folded[:, H * 128:].rearrange("p (h j) -> p h j", h=H)
        MS = sb("MS", [128, 128])
        ymean = sb("ymean", [128, B])
        meanT = sb("meanT", [128, B])
        sumsq = sb("sumsq", [CP, B, CC])
        rms = sb("rms", [CP, B, CC])
        rkey = sb("rkey", [CP, B, CC])
        qm8 = sb("qm8", [BT, QT], U8)
        keepq = sb("keepq", [BT, QT])
        act_q = sb("act_q", [BT, 1])
        act_k = sb("act_k", [BT, KB])
        any_k = sb("any_k", [BT, 1])
        active = sb("active", [BT, KB])
        prefix = sb("prefix", [BT, KB])
        rowsum = sb("rowsum", [BT, 1])
        rank = sb("rank", [BT, KB])
        firstc = sb("firstc", [BT, KB])
        lastc = sb("lastc", [BT, KB])
        bstep = sb("bstep", [BT, TILES - 1])
        bidx = sb("bidx", [BT, 1])
        btidx = sb("btidx", [BT, 1])
        lists_w = sb("lists_w", [BT, KB, 4], BF16)
        first_w = sb("first_w", [BT, KB, 128], BF16)
        item_n = sb("item_n", [1, 2], I32)
        m_run = sb("m_run", [128, 1])
        l_run = sb("l_run", [128, 1])
        l_inv = sb("l_inv", [128, 1])
        m_before = sb("m_before", [128, 2])
        m_block = sb("m_block", [128, 2])
        m_minus = sb("m_minus", [128, 2])
        gate_bout = sb("gate_bout", [128, 1])
        gw0 = sb("gw0", [128, E0])
        gb0 = sb("gb0", [128, E0])
        ws = sb("ws", [128, 2 * F0])
        w2s = sb("w2s", [F0, 128])
        sc0 = sb("sc0", [128, NT, E0])
        bi0 = sb("bi0", [128, NT, E0])
        hot = sb("hot", [128, NT, E0])
        msk = sb("msk", [128, NT, E0])
        den = sb("den", [128, NT])
        top8 = sb("top8", [128, NT, 8])
        idx8 = sb("idx8", [128, NT, 8], U32)
        idxf = sb("idxf", [128, NT, 8])
        wq1 = sb("wq1", [128, 128])
        wk1 = sb("wk1", [128, 128])
        wv1 = sb("wv1", [128, 128])
        wih = sb("wih", [128, 3 * D])
        whh = sb("whh", [128, 3 * D])
        G1 = sb("G1", [128, 128])
        F1w = sb("F1w", [128, 3 * D])
        bih = sb("bih", [128, 3])
        bhh = sb("bhh", [128, 3])
        hb = sb("hb", [128, 3])
        wslot = sb("wslot", [128, 1])
        wkey = sb("wkey", [128, 1])
        wkey_s = sb("wkey_s", [128, 1])
        mx = sb("mx", [CP, 2, CC])
        nb = sb("nb", [CP, 2, CC])
        sm = sb("sm", [CP, 2, CC])
        rs = sb("rs", [CP, 2, CC])
        zr = sb("zr", [S, 2, 1])
        gw1 = sb("gw1", [128, E1])
        gb1 = sb("gb1", [128, E1])
        b1T = sb("b1T", [128, E1, FC])
        b2T = sb("b2T", [128, E1])
        r1 = sb("r1", [128, NT])
        r2 = sb("r2", [128, NT])
        valid = sb("valid", [128, TOP1, NT])
        posk = sb("posk", [128, TOP1, NT])
        gidx = sb("gidx", [128, TOP1, NT], I32)
        sidx = sb("sidx", [128, TOP1, NT], I32)
        wk = sb("wk", [128, TOP1, NT])
        trash = sb("trash", [128, TOP1, NT])
        hT = [sb(f"hT{k}", [128, FC * CAP + WIDE - CAP]) for k in range(2)]
        hx1 = sb("hx1", [128, FC, CAP])
        early_w = sb("early_w", [128, EARLY, 2 * F1])
        region = sb("region", [128, 24 * 2 * F1])
        work = sb("work", [128, 4 * CC * S + 7 * HALF])
        used = {"region": 0, "work": 0, "early": 0, "early_rest": 0}
        early = early_w[:, :, :].rearrange("p e c -> p (e c)")
        early_rest = early[:, 6224:]

        def carve(n, where="region"):
            tile = {"region": region, "work": work, "early": early, "early_rest": early_rest}[where]
            used[where] += n
            assert used[where] <= tile.shape[1]
            return tile[:, used[where] - n:used[where]]

        tilesT = carve(H * (T + 2 * QT)).rearrange("p (h s) -> p h s", h=H)
        wqT, wkT, wvT, wo = (carve(H // 2 * 128).rearrange("p (h i) -> p h i", i=128) for _ in range(4))
        msq2 = carve(2 * CC * 128)
        msq = [msq2[:, k * CC * 128:(k + 1) * CC * 128] for k in range(2)]
        zero = msq2[:, 0:SLOTS]
        padd6 = carve(CC // 2 * 128)
        padd = [carve(CC // 4 * 128, "work") for _ in range(2)]
        item_bt = carve(ITEMS + AHEAD).bitcast(I32)
        item_blk = carve(ITEMS + AHEAD).bitcast(I32)
        item_dst = carve(ITEMS + AHEAD).bitcast(I32)
        mctx = [carve(CC * 128, "early") for _ in range(KEY_BUFS)]
        hot_r = [carve(ITEMS // 2, "early").bitcast(BF16) for _ in range(KB)]
        iota_r = carve(ITEMS, "early")
        km8 = carve(376, "early").bitcast(U8)
        key_sel = carve(B * B, "early")[:CP, :].rearrange("p (b j) -> p b j", b=B)
        keep_d = carve(BT * QT, "work")
        not_first = carve(ITEMS + AHEAD, "work")
        first_neg = carve(ITEMS + AHEAD, "work")
        rescale = carve(ITEMS + AHEAD, "early_rest")
        l_block = carve(ITEMS + AHEAD, "early_rest")
        mask_row = [carve(96, "work").bitcast(U8) for _ in range(2)]
        mask_b = [carve(188, "work").bitcast(BF16) for _ in range(2)]
        Qk = [carve(128, "work") for _ in range(2)]
        P = [carve(KN, "work") for _ in range(2)]
        PT = carve(KC * 128, "work").rearrange("p (c r) -> p c r", c=KC)
        acc = carve(128, "work")
        On = carve(128, "work")
        ictx = [carve(KC * 128, w).rearrange("p (c d) -> p c d", c=KC) for w in ("region", "early_rest")]
        ictxT = [carve(KN, "work") for _ in range(2)]
        used["early"] = 0
        w13 = carve(2 * E0 * F0, "early").rearrange("p (g n) -> p g n", g=2)
        w2p = carve(PAIRS * 128, "early").rearrange("p (e d) -> p e d", e=PAIRS)
        pair_sel = carve(PAIRS * 64, "early").bitcast(BF16).rearrange("p (e d) -> p e d", e=PAIRS)
        combT = carve(T // 2, "early").bitcast(BF16)
        parts = carve(NT * PARTS // 2, "early").bitcast(BF16).rearrange("p (n r) -> p n r", n=NT)
        ident_b = carve(64, "early").bitcast(BF16)
        sg = [carve(HALF, "early") for _ in range(2)]
        hh = [carve(HALF, "early") for _ in range(2)]
        keys = region[:CP, 0:GB * CC * KW].rearrange("p (s c d) -> p s c d", s=GB, d=KW)
        keysT = region[:, GB * CC * KW:GB * CC * KW + GB * M].rearrange("p (s m) -> p s m", s=GB)
        used["work"] = 0
        A = [carve(CC * S, "work").rearrange("p (c s) -> p c s", c=CC) for _ in range(2)]
        UnN = carve(QB * 128, "work").rearrange("p (s d) -> p s d", s=QB)
        slots_x = carve(2 * QS, "work").rearrange("p (a s) -> p a s", a=2)
        qT_all = carve(2 * (QS + WIDE - S), "work")
        qT = qT_all.rearrange("p (a s) -> p a s", a=2)
        Un, rt, zt, nt, hn, tmp, sn, sq1, rstd1 = (carve(QS, "work") for _ in range(9))
        late_w = region[:, :].rearrange("p (e c) -> p e c", c=2 * F1)
        xtok = folded[:, 0:T].rearrange("p (n d) -> p n d", n=NT)
        rtok = folded[:, T:2 * T].rearrange("p (n d) -> p n d", n=NT)
        ysr = folded[:, 2 * T:2 * T + SLOTS].rearrange("p (n d) -> p n d", n=ST)
        xeT = ln_tiles[:, 0:SLOTS + WIDE - CAP]
        hx = [ln_tiles[:, SLOTS + WIDE - CAP:SLOTS + WIDE - CAP + FC * CAP].rearrange("p (c n) -> p c n", c=FC), hx1]
        used["work"] = 0
        xe = carve(SLOTS, "work").rearrange("p (n d) -> p n d", n=ST)
        ysT = carve(SLOTS, "work")
        lg, pr, posx = (carve(NT * E1, "work").rearrange("p (n e) -> p n e", n=NT) for _ in range(3))
        oh = [carve(NT * E1, "work").rearrange("p (n e) -> p n e", n=NT) for _ in range(TOP1)]
        ohb = carve(NT * E1 // 2, "work").bitcast(BF16).rearrange("p (n e) -> p n e", n=NT)
        yg = early_w[:, 0:2, 0:T]

        ps = ctx.enter_context(nc.psum_tensor("ps", [128, 8, 512], F32))

        ld_x = sem("ld_x")
        ld_attn = sem("ld_attn")
        ld_small = sem("ld_small")
        ld_mask = sem("ld_mask")
        ld_mctx = [sem(f"ld_mctx{k}") for k in range(KEY_BUFS)]
        ld_itemT = [sem(f"ld_itemT{k}") for k in range(2)]
        ld_item = [sem(f"ld_item{k}") for k in range(2)]
        ld_ffn0 = sem("ld_ffn0")
        ld_keys = [sem(f"ld_keys{s}") for s in range(GB)]
        ld_early = sem("ld_early")
        ld_late = [sem(f"ld_late{n}") for n in range((E1 - EARLY) // 4)]
        st_zero = sem("st_zero")
        st_xe = sem("st_xe")
        ld_xe = [sem(f"ld_xe{k}") for k in range(2)]
        st_ys = sem("st_ys")
        ld_yg = [sem(f"ld_yg{j}") for j in range((NT + 1) // 2)]
        st_out = sem("st_out")
        const = sem("const")
        gates_ok = sem("gates_ok")
        ln_mean = sem("ln_mean")
        ln_cent = sem("ln_cent")
        ln_sq = sem("ln_sq")
        ln_var = sem("ln_var")
        ln_sd = sem("ln_sd")
        ln_rec = sem("ln_rec")
        ln_diag = sem("ln_diag")
        ln_bc = sem("ln_bc")
        ln_out = sem("ln_out")
        x_new = sem("x_new")
        fold_mm = sem("fold_mm")
        fold_ev = sem("fold_ev")
        fold_sum = sem("fold_sum")
        key_sq = sem("key_sq")
        key_ss = sem("key_ss")
        key_add = sem("key_add")
        key_add3 = sem("key_add3")
        key_sum = sem("key_sum")
        mean_mm = sem("mean_mm")
        mean_ev = sem("mean_ev")
        ymean_mm = sem("ymean_mm")
        rk_sd = sem("rk_sd")
        rk_ok = sem("rk_ok")
        qa_mm = sem("qa_mm")
        qa_ev = sem("qa_ev")
        plan = sem("plan")
        plan_rs = sem("plan_rs")
        plan_rank = sem("plan_rank")
        plan_hot = sem("plan_hot")
        plan_list = sem("plan_list")
        items_ok = sem("items_ok")
        q_tile = sem("q_tile")
        s_mm = sem("s_mm")
        s_max = sem("s_max")
        m_prev = sem("m_prev")
        m_new = sem("m_new")
        m_neg = sem("m_neg")
        p_exp = sem("p_exp")
        pt_mm = sem("pt_mm")
        pt_ev = sem("pt_ev")
        o_mm = sem("o_mm")
        l_ok = sem("l_ok")
        acc_ok = sem("acc_ok")
        rl_ok = sem("rl_ok")
        on_ok = sem("on_ok")
        ot_mm = sem("ot_mm")
        ot_ev = sem("ot_ev")
        y_mm = sem("y_mm")
        pair_ok = sem("pair_ok")
        y_keep = sem("y_keep")
        keep_mm = sem("keep_mm")
        lg0_mm = sem("lg0_mm")
        sc0_ok = sem("sc0_ok")
        rt0 = sem("rt0")
        comb_ok = sem("comb_ok")
        combT_mm = sem("combT_mm")
        combT_ok = sem("combT_ok")
        e0_mm = sem("e0_mm")
        e0_share = sem("e0_share")
        e0_act = sem("e0_act")
        e0_up = sem("e0_up")
        e0_h = sem("e0_h")
        e0_y = sem("e0_y")
        g1_mm = sem("g1_mm")
        g1_ev = sem("g1_ev")
        hb_ok = sem("hb_ok")
        q_pad = sem("q_pad")
        key_col = sem("key_col")
        sl_ok = sem("sl_ok")
        q_sq = sem("q_sq")
        q_var = sem("q_var")
        q_sd = sem("q_sd")
        q_rec = sem("q_rec")
        q_sn = sem("q_sn")
        q_mm = sem("q_mm")
        q_ok = sem("q_ok")
        a_mm = sem("a_mm")
        a_max = sem("a_max")
        a_neg = sem("a_neg")
        a_exp = sem("a_exp")
        a_rec = sem("a_rec")
        a_w = sem("a_w")
        a_att = sem("a_att")
        u_mm = sem("u_mm")
        z_add = sem("z_add")
        z_rec = sem("z_rec")
        un_ok = sem("un_ok")
        ut_mm = sem("ut_mm")
        u_ok = sem("u_ok")
        hn_ok = sem("hn_ok")
        gate_mm = sem("gate_mm")
        gru_t = sem("gru_t")
        gru_v = sem("gru_v")
        gru_n = sem("gru_n")
        gru_new = sem("gru_new")
        gru_last = sem("gru_last")
        lg1_mm = sem("lg1_mm")
        rt1 = sem("rt1")
        rt1_exp = sem("rt1_exp")
        rt1_hot = sem("rt1_hot")
        pos_mm = sem("pos_mm")
        slot_ok = sem("slot_ok")
        tok_mm = sem("tok_mm")
        tok_ev = sem("tok_ev")
        wide_ok = sem("wide_ok")
        xe_mm = sem("xe_mm")
        xe_ev = sem("xe_ev")
        h_mm = sem("h_mm")
        h_b = sem("h_b")
        h_ok = sem("h_ok")
        ye_mm = sem("ye_mm")
        ye_ok = sem("ye_ok")
        yt_mm = sem("yt_mm")
        yt_ev = sem("yt_ev")
        out_s = sem("out_s")

        xe_dram = t["xe_scratch"]
        ys_dram = t["ys_scratch"]
        block = ctx.enter_context(nc.Block())

        def half(h):
            return slice(h * HALF, (h + 1) * HALF)

        def bcast(ap, n):
            return ap.unsqueeze(len(ap.shape)).to_broadcast([*ap.shape, n])

        def by_tile(ap):
            return ap.rearrange("p (b t q) -> p t b q", t=TILES, q=QT)

        def over_tiles(ap):
            return ap.unsqueeze(1).to_broadcast([ap.shape[0], NT, ap.shape[1]])

        def phases(eng, phase):
            for g in range(GROUPS):
                phase(g, 0, g * PHASES)
                with eng.Fori(0, ITERS - 1) as it:
                    for w in (1, 2):
                        phase(g, w, eng.snap(it * 2 + (g * PHASES + w)))
                phase(g, PHASES - 1, g * PHASES + PHASES - 1)

        def quad(g, k):
            return slice((g * 2 + k) * QS, (g * 2 + k + 1) * QS)

        def slot_rows_after(c):
            return (min((c + 1) * 512, SLOTS) - 1) // (4 * CAP) * 4 + 3

        def expert_rows_after(c):
            return 4 * c - 6

        def loads_next(g, w):
            return w == 0 or (w == PHASES - 1 and g + 1 < GROUPS)

        def prepares(g, w):
            return w < PHASES - 1 or g + 1 < GROUPS

        @block.sync
        def _(sp):
            sp.dma_start(xT[:, :], t["xT"]).then_inc(ld_x, 16)
            ctx_b = t["ctx"].rearrange("b (p c) d -> b p (c d)", p=CP)

            def load_batch(dst, b, done):
                for p0, p1 in ((0, 112), (112, CP)):
                    sp.dma_start(dst[p0:p1, :], ctx_b[bass.ds(b, 1), p0:p1, :].rearrange("a p c -> (a p) c")).then_inc(done, 16)

            load_batch(mctx[0], 0, ld_mctx[0])
            for dst, name in ((wqT, "wqT"), (wkT, "wkT")):
                sp.dma_start(dst, t[name]).then_inc(ld_attn, 16)
            load_batch(mctx[1], 1, ld_mctx[1])
            for dst, name in ((wvT, "wvT"), (wo, "wo")):
                sp.dma_start(dst, t[name]).then_inc(ld_attn, 16)
            for r in range(TILES):
                sp.dma_start(km8[r * B:(r + 1) * B, 0:M], t["kv_mask"]).then_inc(ld_mask, 16)
            sp.dma_start(qm8[:, :], t["q_mask"]).then_inc(ld_mask, 16)
            for k in range(2, KEY_BUFS):
                load_batch(mctx[k], k, ld_mctx[k])
            small = [(gates_in[:, 0:2], t["g_xattn"].to_broadcast([128, 2])),
                     (gates_in[:, 2:4], t["g_ffn"].to_broadcast([128, 2])),
                     (bout[:, :], t["bout"]), (gw0[:, :], t["gw0"]), (gb0[:, :], t["gb0"].to_broadcast([128, E0])),
                     (ws[:, :], t["ws"]), (w2s[:, :], t["w2s"]), (wq1[:, :], t["wq1"]), (wk1[:, :], t["wk1"]),
                     (wv1[:, :], t["wv1"]), (wih[:, :], t["wih"]), (whh[:, :], t["whh"]), (bih[:, :], t["bih"]),
                     (bhh[:, :], t["bhh"]), (wslot[:, :], t["wslot"]), (wkey[:, :], t["wkey"]), (gw1[:, :], t["gw1"]),
                     (gb1[:, :], t["gb1"].to_broadcast([128, E1])), (b1T[:, :, :], t["b1T"]), (b2T[:, :], t["b2T"])]
            assert len(small) == SMALL
            for dst, src in small:
                sp.dma_start(dst, src).then_inc(ld_small, 16)
            with sp.Fori(1, B // KEY_BUFS) as i:
                for k in range(KEY_BUFS):
                    sp.wait_ge(key_sq, i * KEY_BUFS + (k - KEY_BUFS + 1))
                    sp.wait_ge(key_add, i * KEY_BUFS + (k - KEY_BUFS + 1))
                    load_batch(mctx[k], i * KEY_BUFS + k, ld_mctx[k])
            sp.wait_ge(items_ok, 1)
            n = sp.value_load(item_n[0:1, 0:1], min_val=1, max_val=ITEMS)

            def load_item(j, k):
                blk = sp.value_load(item_blk[0:1, bass.ds(j, 1)], min_val=0, max_val=B * KB - 1)
                sp.wait_ge(s_mm, j + 1)
                sp.dma_start(ictxT[k], t["ctxT_blk"][bass.ds(blk, 1), :, :].rearrange("a p c -> (a p) c")).then_inc(ld_itemT[k], 16)
                sp.dma_start(mask_row[k][0:1, 0:KN], t["kv_blk"][bass.ds(blk, 1), :]).then_inc(ld_itemT[k], 16)

            with sp.Fori(0, (n + 1) // 2) as i:
                for k in range(2):
                    load_item(sp.snap(i * 2 + k), k)
            for k in range(AHEAD):
                load_item(sp.snap((n + 1) // 2 * 2 + k), k)
            sp.wait_ge(ld_item[0], (n + 1) // 2 * 16 + 16)
            sp.wait_ge(x_new, 2)
            for g in range(GROUPS):
                for s in range(GB):
                    if g:
                        sp.wait_ge(u_mm, (g * PHASES - 2) * HB + 2 * s + 2)
                    for p0, p1 in ((0, 112), (112, CP)):
                        sp.dma_start(keys[p0:p1, s, :, 0:128],
                                     ctx_b[g * GB + s, p0:p1, :].rearrange("p (c d) -> p c d", c=CC)).then_inc(ld_keys[s], 16)
                    sp.dma_start(keysT[:, s, :], t["ctxT"][g * GB + s]).then_inc(ld_keys[s], 16)
            sp.wait_ge(u_mm, GROUPS * PHASES * HB)
            for e in range(0, E1 - EARLY, 4):
                sp.dma_start(late_w[:, e:e + 4, :], t["w12"][:, EARLY + e:EARLY + e + 4, :]).then_inc(ld_late[e // 4], 16)
            sp.wait_ge(st_xe, 16 * TOP1 * NT)
            for part, (j0, j1) in enumerate(((0, 8), (8, ST))):
                sp.dma_start(xe[:, j0:j1, :], xe_dram[j0 * 128:j1 * 128, :].rearrange("(n p) d -> p n d", p=128)).then_inc(ld_xe[part], 16)
            for c in range(YC):
                sp.wait_ge(yt_ev, c + 1)
                j0, j1 = 4 * c, min(4 * c + 4, ST)
                sp.dma_start(ys_dram[j0 * 128:j1 * 128, :].rearrange("(n p) d -> p n d", p=128), ysr[:, j0:j1, :]).then_inc(st_ys, 16)
            for j0, j1 in ((0, 4), (4, NT)):
                sp.wait_ge(out_s, 2 * j1)
                sp.dma_start(t["out"].rearrange("(n p) d -> p n d", p=128)[:, j0:j1, :], xtok[:, j0:j1, :]).then_inc(st_out, 16)
            sp.wait_ge(st_out, 32)

        @block.gpsimd
        def _(gp):
            gp.memset(mean_w[:, :], 1.0 / D).then_inc(const, 1)
            gp.memset(ones[:, :], 1.0).then_inc(const, 1)
            gp.memset(ones_b[:, :], 1.0).then_inc(const, 1)
            gp.memset(eps_ln[:, :], 1e-5).then_inc(const, 1)
            gp.memset(eps_rms[:, :], 1e-6).then_inc(const, 1)
            gp.memset(key_sel[:, :, :], 0.0).then_inc(const, 1)
            gp.memset(ident[:, :], 0.0).then_inc(const, 1)
            gp.wait_ge(const, 7)
            gp.affine_select(out=ident[:, :], in_=ident[:, :], compare_op=ALU.not_equal, fill=1.0, base=0,
                             pattern=[[-1, 128]], channel_multiplier=1).then_inc(const, 1)
            gp.affine_select(out=before[:, :], in_=ones[:, :], compare_op=ALU.is_gt, fill=0.0, base=0,
                             pattern=[[1, 128]], channel_multiplier=-1).then_inc(const, 1)
            gp.affine_select(out=bstep[:, :], in_=ones[:BT, 0:TILES - 1], compare_op=ALU.is_ge, fill=0.0,
                             base=-B, pattern=[[-B, TILES - 1]], channel_multiplier=1).then_inc(const, 1)
            gp.affine_select(out=key_sel[:, :, :], in_=key_sel[:, :, :], compare_op=ALU.not_equal, fill=1.0 / M,
                             base=0, pattern=[[1, B], [-1, B]], channel_multiplier=0).then_inc(const, 1)
            gp.iota(iota_e[:, :], pattern=[[1, E1]], base=0, channel_multiplier=0,
                    allow_small_or_imprecise_dtypes=True).then_inc(const, 1)
            gp.iota(iota_r, pattern=[[1, ITEMS]], base=0, channel_multiplier=0,
                    allow_small_or_imprecise_dtypes=True).then_inc(const, 1)
            gp.iota(btidx[:, :], pattern=[[0, 1]], base=0, channel_multiplier=1,
                    allow_small_or_imprecise_dtypes=True).then_inc(const, 1)
            gp.iota(trash[:, :, :], pattern=[[NT * 128, TOP1], [128, NT]], base=TRASH, channel_multiplier=1,
                    allow_small_or_imprecise_dtypes=True).then_inc(const, 1)
            gp.memset(item_bt[0:1, :], NOTHING).then_inc(const, 1)
            gp.memset(item_blk[0:1, :], 0).then_inc(const, 1)
            gp.memset(item_dst[0:1, :], UNUSED).then_inc(const, 1)
            gp.memset(not_first, 0.0).then_inc(const, 1)
            gp.memset(first_neg, 0.0).then_inc(const, 1)
            gp.memset(acc, 0.0).then_inc(const, 1)
            gp.memset(On, 0.0).then_inc(const, 1)
            gp.memset(m_run[:, :], 0.0).then_inc(const, 1)
            gp.memset(l_run[:, :], 1.0).then_inc(const, 1)
            gp.memset(zero, 0.0).then_inc(const, 1)
            gp.memset(tilesT[:, :, T:T + 2 * QT], 0.0).then_inc(const, 1)
            gp.wait_ge(const, CONSTS - 1)
            gp.tensor_copy(before_b[:, :], before[:, :]).then_inc(const, 1)
            gp.wait_ge(const, CONSTS)
            gp.dma_start(xe_dram[0:SLOTS, :].rearrange("(p n) d -> p (n d)", p=128), zero).then_inc(st_zero, 16)
            with gp.Fori(0, B // KEY_BUFS) as i:
                for k in range(KEY_BUFS):
                    gp.wait_ge(ld_mctx[k], i * 32 + 32)
                    gp.wait_ge(key_add3, i * KEY_BUFS + (k + 1))
                    gp.tensor_tensor(padd6[:CP, :], mctx[k][:CP, 0:CC // 2 * 128], mctx[k][:CP, CC // 2 * 128:], ALU.add).then_inc(key_add, 1)
                    gp.wait_ge(key_add, i * KEY_BUFS + (k + 1))
                    gp.wait_ge(key_sum, i * KEY_BUFS + (k + 1))
                    gp.tensor_tensor(padd[k % 2][:CP, :], padd6[:CP, 0:CC // 4 * 128], padd6[:CP, CC // 4 * 128:], ALU.add).then_inc(key_add3, 1)
            gp.wait_ge(key_sq, B)
            gp.wait_ge(key_sum, B + 2)
            gp.wait_ge(plan_list, 1)
            gp.dma_start(w13, t["w13"]).then_inc(ld_ffn0, 16)
            gp.dma_start(w2p, t["w2p"]).then_inc(ld_ffn0, 16)
            gp.wait_ge(items_ok, 1)
            gp.wait_ge(qa_ev, 2 * H)
            n = gp.value_load(item_n[0:1, 0:1], min_val=1, max_val=ITEMS)

            def item_queries(j, k, loads):
                bt = gp.value_load(item_bt[0:1, bass.ds(j, 1)], min_val=0, max_val=BT)
                gp.wait_ge(ld_itemT[k], loads)
                gp.wait_ge(s_mm, j + 1)
                gp.tensor_copy(Qk[k].rearrange("p (h q) -> p h q", h=H), tilesT[:, :, bass.ds(bt * QT, QT)])
                gp.tensor_scalar(mask_b[k][0:1, 0:KN], mask_row[k][0:1, 0:KN], -1.0, BIG, ALU.add, ALU.mult).then_inc(q_tile, 1)

            for k in range(AHEAD):
                item_queries(k, k, 32)
            with gp.Fori(0, (n + 1) // 2) as i:
                for k in range(2):
                    item_queries(gp.snap(i * 2 + (k + AHEAD)), k, i * 32 + 64)
            gp.tensor_copy(ident_b, ident[:, :]).then_inc(pair_ok, 1)
            gp.memset(parts, 0.0).then_inc(pair_ok, 1)
            gp.memset(pair_sel, 0.0).then_inc(pair_ok, 1)
            gp.wait_ge(pair_ok, 3)
            for r in range(0, PARTS, 32):
                rows = pair_sel[r:r + E0].rearrange("p e (a i) -> p e a i", a=2)
                gp.affine_select(out=rows, in_=rows, compare_op=ALU.not_equal, fill=1.0, base=0,
                                 pattern=[[-2, PAIRS], [-1, 2], [0, F0]], channel_multiplier=1).then_inc(pair_ok, 1)
            gp.wait_ge(pair_ok, 6)

            gp.wait_ge(x_new, 2)
            gp.memset(qT_all, 0.0).then_inc(q_pad, 1)
            gp.wait_ge(rk_sd, 1)

            def key_rms(g):
                for s in range(GB):
                    if g:
                        gp.wait_ge(u_mm, (g * PHASES - 2) * HB + 2 * s + 2)
                    gp.tensor_copy(keys[:, s, :, 128:KW], rms[:, g * GB + s, :].unsqueeze(2)).then_inc(key_col, 1)

            def slot_squares(u, k):
                gp.wait_ge(sl_ok, u + 1)
                gp.tensor_tensor(sq1, slots_x[:, k, :], slots_x[:, k, :], ALU.mult).then_inc(q_sq, 1)

            key_rms(0)
            gp.wait_ge(x_new, 4)
            gp.dma_start(early_w[:, :, :], t["w12"][:, 0:EARLY, :]).then_inc(ld_early, 16)
            slot_squares(0, 0)

            def phase(g, w, u):
                if prepares(g, w):
                    slot_squares(u + 1, 1 - w % 2)
                if w == PHASES - 1 and g + 1 < GROUPS:
                    key_rms(g + 1)

            phases(gp, phase)

            gp.wait_ge(ln_out, 8)
            gp.memset(xeT[:, SLOTS:], 0.0).then_inc(wide_ok, 1)
            for k in range(2):
                gp.memset(hT[k][:, FC * CAP:], 0.0).then_inc(wide_ok, 1)
            gp.wait_ge(slot_ok, 2)
            gp.wait_ge(tok_ev, 4)
            for k in range(TOP1):
                for j in range(NT):
                    gp.indirect_dma_start(xe_dram, bass.IndirectOffsetOnAxis(ap=sidx[:, k, j:j + 1].bitcast(U32), axis=0),
                                          xtok[:, j, :], None).then_inc(st_xe, 16)
            gp.wait_ge(st_ys, 16 * YC)
            for j in range(NT):
                for k in range(TOP1):
                    gp.indirect_dma_start(yg[:, k, j * 128:(j + 1) * 128], None, ys_dram,
                                          bass.IndirectOffsetOnAxis(ap=gidx[:, k, j:j + 1].bitcast(U32), axis=0)).then_inc(ld_yg[j // 2], 16)

        @block.scalar
        def _(act):
            def ln(k):
                for h in range(2):
                    act.wait_ge(ln_cent, 2 * k + h + 1)
                    act.activation(sq[:, half(h)], cen[:, half(h)], ACT.Square).then_inc(ln_sq, 1)
                act.wait_ge(ln_var, k + 1)
                act.activation(ln_s[:, :], ps[:, 2, 0:NT], ACT.Sqrt, bias=eps_ln[:, :]).then_inc(ln_sd, 1)

            act.wait_ge(const, CONSTS)
            ln(0)
            act.wait_ge(st_zero, 16)

            def squares(i, k, b):
                act.wait_ge(ld_mctx[k], i * 32 + 32)
                act.wait_ge(key_ss, b + 1)
                act.activation(msq[k % 2][:CP, :], mctx[k][:CP, :], ACT.Square).then_inc(key_sq, 1)

            for k in range(2):
                squares(0, k, k)
            for f in range(2):
                for q in range(4):
                    act.wait_ge(fold_mm, 4 * f + q + 1)
                    dst = (G, MO)[f].rearrange("p (m a) j -> p a m j", a=2)[:, q % 2, 4 * (q // 2):4 * (q // 2) + 4, :]
                    act.activation(dst, ps[:, 4 + q, :].rearrange("p (m j) -> p m j", m=4), ACT.Copy, scale=(DH ** -0.5 if f == 0 else 1.0)).then_inc(fold_ev, 1)

            def head_queries(b):
                for h in range(2):
                    act.wait_ge(qa_mm, b * 2 + (h + 1))
                    act.copy(tilesT[:, bass.ds(b, 1), half(h)], ps[:, h, 0:HALF].unsqueeze(1)).then_inc(qa_ev, 1)

            with act.Fori(0, B // KEY_BUFS - 1) as i:
                for k in range(KEY_BUFS):
                    head_queries(i * KEY_BUFS + k)
                    squares(i + (k + 2) // KEY_BUFS, (k + 2) % KEY_BUFS, i * KEY_BUFS + (k + 2))
            for b in range(B - KEY_BUFS, B):
                head_queries(b)
                if b + 2 < B:
                    squares((b + 2) // KEY_BUFS, (b + 2) % KEY_BUFS, b + 2)
            act.wait_ge(ld_small, 16 * SMALL)
            act.activation(gates[:, :], gates_in[:, :], ACT.Tanh).then_inc(gates_ok, 1)

            def probabilities(j, k):
                act.wait_ge(m_neg, j + 1)
                act.activation(rescale[:, bass.ds(j, 1)], m_before[:, k:k + 1], ACT.Exp, bias=m_minus[:, k:k + 1])
                act.activation(P[k], ps[:, k, 0:KN], ACT.Exp, bias=m_minus[:, k:k + 1],
                               accum_out=l_block[:, bass.ds(j, 1)]).then_inc(p_exp, 1)

            def keep_result(j):
                dst = act.value_load(item_dst[0:1, bass.ds(j, 1)], min_val=0, max_val=UNUSED)
                act.wait_ge(ot_mm, j + 1)
                act.copy(tilesT[:, :, bass.ds(dst * QT, QT)], ps[:, 4, 0:128].rearrange("p (h q) -> p h q", h=H)).then_inc(ot_ev, 1)

            def load_rows(j, k):
                blk = act.value_load(item_blk[0:1, bass.ds(j, 1)], min_val=0, max_val=B * KB - 1)
                act.dma_start(ictx[k][:KP, :, :], t["ctx_blk"][bass.ds(blk, 1), :, :].rearrange("a (p c) d -> (a p) c d", c=KC)).then_inc(ld_item[k], 16)

            act.wait_ge(items_ok, 1)
            n = act.value_load(item_n[0:1, 0:1], min_val=1, max_val=ITEMS)
            load_rows(0, 0)
            for k in range(AHEAD):
                probabilities(k, k)
            with act.Fori(0, (n + 1) // 2) as i:
                for k in range(2):
                    j = act.snap(i * 2 + k)
                    act.wait_ge(pt_mm, j + 1)
                    act.wait_ge(o_mm, j + 2)
                    act.copy(PT[:KP].rearrange("p c r -> p (c r)"), ps[:KP, 2, 0:KC * 128]).then_inc(pt_ev, 1)
                    load_rows(j + 1, 1 - k)
                    probabilities(j + AHEAD, k)
                    keep_result(j)
            keep_result(act.snap((n + 1) // 2 * 2))
            act.wait_ge(key_ss, B + 2)
            act.activation(rms[:, :, :], sumsq[:, :, :], ACT.Sqrt, bias=eps_rms[:CP, :], scale=1.0 / D).then_inc(rk_sd, 1)
            ln(1)
            act.wait_ge(lg0_mm, 1)
            act.activation(sc0[:, :, :].rearrange("p n e -> p (n e)"), ps[:, 4, 0:NT * E0], ACT.Sigmoid).then_inc(sc0_ok, 1)
            for j in range(2 * (PAIRS + 1)):
                p = 128 if j // 2 < PAIRS else F0
                act.wait_ge(e0_mm, j + 1)
                if j >= 2:
                    act.wait_ge(e0_up, j - 1)
                act.activation(sg[j % 2][:p, :], ps[:p, 2 * (j % 2), 0:HALF], ACT.Silu).then_inc(e0_act, 1)
            act.wait_ge(g1_mm, 2)
            act.copy(G1[:, :], ps[:, 6, 0:128]).then_inc(g1_ev, 1)
            act.copy(F1w[:, :], ps[:, 7, 0:3 * D]).then_inc(g1_ev, 1)
            ln(2)

            def exponentials(g, k, u, m):
                (s, h), a, b = divmod(m, 2), m // 2 % 2, g * GB + k * QB + m // 2
                act.wait_ge(a_neg, u * HB + (m + 1))
                if not isinstance(u, int) or u * HB + m >= 4:
                    act.wait_ge(u_mm, u * HB + (m - 3))
                for c in range(CH):
                    q = h * CH + c
                    i = act.activation(A[a][:CP, q, :], ps[:CP, 2 + 2 * a + h, c * S:(c + 1) * S], ACT.Exp,
                                       bias=nb[:, a, q:q + 1], scale=rkey[:, b, q:q + 1], accum_out=sm[:, a, q:q + 1])
                i.then_inc(a_exp, 1)

            def gates_of(v):
                act.wait_ge(gate_mm, v + 1)
                act.activation(rt, ps[:, 0, 0:QS], ACT.Tanh, bias=hb[:, 0:1], scale=0.5).then_inc(gru_t, 1)
                act.activation(zt, ps[:, 0, QS:2 * QS], ACT.Tanh, bias=hb[:, 1:2], scale=0.5).then_inc(gru_t, 1)

            def candidate_of(v):
                act.wait_ge(gru_v, v * 2 + 2)
                act.activation(nt, tmp, ACT.Tanh, bias=bih[:, 2:3]).then_inc(gru_n, 1)

            def slot_rms(u):
                act.wait_ge(q_var, u + 1)
                act.activation(rstd1, ps[:, 0, 0:QS], ACT.Sqrt, bias=eps_rms[:, :]).then_inc(q_sd, 1)

            slot_rms(0)
            for m in range(LOOK):
                exponentials(0, 0, 0, m)

            def phase(g, w, u):
                k = w % 2
                for m in range(HB):
                    if m == 0 and (g, w) != (0, 0):
                        gates_of(u - 1)
                    if m + LOOK < HB:
                        exponentials(g, k, u, m + LOOK)
                    elif prepares(g, w):
                        exponentials(g + w // (PHASES - 1), 1 - k, u + 1, m + LOOK - HB)
                    if m == 0 and (g, w) != (0, 0):
                        candidate_of(u - 1)
                    if m == 1 and prepares(g, w):
                        slot_rms(u + 1)

            phases(act, phase)
            gates_of(GROUPS * PHASES - 1)
            candidate_of(GROUPS * PHASES - 1)
            ln(3)
            act.wait_ge(rt1, 3)
            act.activation(pr, lg, ACT.Exp).then_inc(rt1_exp, 1)
            for c in range(4):
                act.wait_ge(tok_mm, c + 1)
                j0, j1 = ((0, 4), (4, NT))[c % 2]
                dst = (xtok, rtok)[c // 2][:, j0:j1, :].rearrange("p n d -> p (n d)")
                act.copy(dst, ps[:, 4 + c, 0:(j1 - j0) * 128]).then_inc(tok_ev, 1)
            def expert_rows(c):
                w = min(512, SLOTS - 512 * c)
                act.wait_ge(xe_mm, c + 1)
                act.copy(xeT[:, 512 * c:512 * c + w], ps[:, 4 + c % 2, 0:w]).then_inc(xe_ev, 1)

            expert_rows(0)
            expert_rows(1)

            def slot_rows(c):
                j0, j1 = 4 * c, min(4 * c + 4, ST)
                act.wait_ge(yt_mm, c + 1)
                act.copy(ysr[:, j0:j1, :].rearrange("p n d -> p (n d)"), ps[:, 6 + c % 2, 0:(j1 - j0) * 128]).then_inc(yt_ev, 1)

            for e in range(E1):
                act.wait_ge(h_b, e + 1)
                if e >= 2:
                    act.wait_ge(ye_mm, e - 1)
                act.activation(hT[e % 2][:, 0:FC * CAP], hx[e % 2].rearrange("p c n -> p (c n)"), ACT.Gelu).then_inc(h_ok, 1)
                for c in range(2, YC):
                    if expert_rows_after(c) + 1 == e:
                        expert_rows(c)
                for c in range(YC):
                    if slot_rows_after(c) + 2 == e:
                        slot_rows(c)
            for c in range(YC):
                if slot_rows_after(c) + 2 >= E1:
                    slot_rows(c)

        @block.vector
        def _(v):
            def ln(k):
                for h in range(2):
                    v.wait_ge(ln_mean, 2 * k + h + 1)
                    v.tensor_tensor(cen[:, half(h)], xT[:, half(h)], ps[:, h, 0:HALF], ALU.subtract).then_inc(ln_cent, 1)
                v.wait_ge(ln_sd, k + 1)
                v.reciprocal(ln_s[:, :], ln_s[:, :]).then_inc(ln_rec, 1)
                v.wait_ge(ln_rec, k + 1)
                diag = rstd.rearrange("p (n d) -> p n d", n=NT)
                for j0, j1 in ((0, 4), (4, NT)):
                    v.tensor_tensor(diag[:, j0:j1, :], ident[:, :].unsqueeze(1).to_broadcast([128, j1 - j0, 128]),
                                    bcast(ln_s[:, j0:j1], 128), ALU.mult).then_inc(ln_diag, 1)
                for h in range(2):
                    v.wait_ge(ln_bc, 2 * k + h + 1)
                    v.tensor_tensor(xln[:, half(h)], cen[:, half(h)], ps[:, h, 0:HALF], ALU.mult).then_inc(ln_out, 1)

            def chain(signal):
                count = [0]

                def step(ins, wait=True):
                    count[0] += 1
                    ins.then_inc(signal, 1)
                    if wait:
                        v.wait_ge(signal, count[0])

                step.count = count
                return step

            v.sem_inc(key_ss, 2)
            v.sem_inc(key_sum, 2)
            v.sem_inc(key_add3, 1)
            v.sem_inc(s_mm, 2)
            v.sem_inc(o_mm, 2)
            v.sem_inc(on_ok, 1)
            v.sem_inc(ot_ev, 1)
            v.wait_ge(const, CONSTS)
            v.wait_ge(ld_x, 16)
            ln(0)
            def key_squares(b, k):
                v.wait_ge(key_sq, b + 1)
                v.tensor_reduce(sumsq[:, bass.ds(b, 1), :], msq[k][:CP, :].rearrange("p (a c d) -> p a c d", a=1, d=D),
                                AX.X, ALU.add).then_inc(key_ss, 1)

            for b in range(2):
                key_squares(b, b % 2)
            step = chain(plan)
            v.wait_ge(ld_mask, 16 * (TILES + 1))
            step(v.tensor_copy(keepq[:, :], qm8[:, :]))
            step(v.tensor_reduce(act_q[:, :], keepq[:, :], AX.X, ALU.max))
            step(v.tensor_reduce(act_k[:, :], km8[:BT, 0:M].rearrange("p (k m) -> p k m", k=KB), AX.X, ALU.max))
            step(v.tensor_reduce(any_k[:, :], act_k[:, :], AX.X, ALU.max))
            step(v.tensor_scalar(keepq[:, :], keepq[:, :], any_k[:, 0:1], None, ALU.mult))
            step(v.tensor_scalar(active[:, :], act_k[:, :], act_q[:, 0:1], None, ALU.mult))
            step(v.memset(prefix[:, 0:1], 0.0))
            for b in range(1, KB):
                step(v.tensor_tensor(prefix[:, b:b + 1], prefix[:, b - 1:b], active[:, b - 1:b], ALU.add))
            v.tensor_reduce(rowsum[:, :], active[:, :], AX.X, ALU.add).then_inc(plan_rs, 1)
            for b in (2, 3):
                key_squares(b, b % 2)
            step(v.tensor_scalar(firstc[:, :], prefix[:, :], 0.0, None, ALU.is_equal))
            step(v.tensor_tensor(firstc[:, :], firstc[:, :], active[:, :], ALU.mult))
            step(v.tensor_tensor(lastc[:, :], prefix[:, :], active[:, :], ALU.add))
            v.wait_ge(plan_rs, 1)
            step(v.tensor_scalar(lastc[:, :], lastc[:, :], rowsum[:, 0:1], None, ALU.is_equal))
            step(v.tensor_tensor(lastc[:, :], lastc[:, :], active[:, :], ALU.mult))
            step(v.tensor_reduce(bidx[:, :], bstep[:, :], AX.X, ALU.add))
            step(v.scalar_tensor_tensor(btidx[:, :], bidx[:, :], -float(B), btidx[:, :], ALU.mult, ALU.add))
            for b in range(KB):
                step(v.tensor_scalar(lists_w[:, b, 1:2], btidx[:, :], float(KB), float(b), ALU.mult, ALU.add), wait=False)
                step(v.tensor_scalar(lists_w[:, b, 3:4], bidx[:, :], -1.0, float(TILES), ALU.mult, ALU.add), wait=False)
                step(v.tensor_copy(first_w[:, b, :], firstc[:, b:b + 1].to_broadcast([BT, 128])), wait=False)
            step(v.scalar_tensor_tensor(btidx[:, :], btidx[:, :], float(TILES), bidx[:, :], ALU.mult, ALU.add))
            for b in range(KB):
                step(v.tensor_scalar(lists_w[:, b, 0:1], btidx[:, :], -float(NOTHING), None, ALU.add), wait=False)
                step(v.tensor_scalar(lists_w[:, b, 2:3], btidx[:, :], -float(UNUSED), lastc[:, b:b + 1], ALU.add, ALU.mult))
            assert step.count[0] == PLAN_LISTS
            key_squares(4, 0)
            v.wait_ge(plan_rank, 2)
            step(v.tensor_scalar(rank[:, :], prefix[:, :], ps[:BT, 2, 0:1], None, ALU.add))
            for b in range(KB):
                v.tensor_scalar(hot_r[b][:BT, :], iota_r[:BT, :], rank[:, b:b + 1], active[:, b:b + 1],
                                ALU.is_equal, ALU.mult).then_inc(plan_hot, 1)
            key_squares(5, 1)
            v.tensor_tensor(keep_d[:BT, :].rearrange("p (b t q) -> p t b q", t=TILES, q=QT),
                            bcast(ident[:BT, 0:BT].rearrange("p (t b) -> p t b", t=TILES), QT),
                            keepq[:, :].unsqueeze(1).unsqueeze(1).to_broadcast([BT, TILES, B, QT]), ALU.mult).then_inc(plan_hot, 1)
            key_squares(6, 0)
            v.wait_ge(fold_ev, 8)
            v.tensor_reduce(MS[:, :], MO.rearrange("p h j -> p j h"), AX.X, ALU.add).then_inc(fold_sum, 1)

            for b in (7, 8):
                key_squares(b, b % 2)
            v.wait_ge(plan_list, 1)
            step(v.tensor_scalar(item_bt[0:1, 0:ITEMS], ps[0:1, 4, 0:ITEMS], float(NOTHING), None, ALU.add))
            step(v.tensor_scalar(item_dst[0:1, 1:ITEMS + 1], ps[0:1, 2, 8:8 + ITEMS], float(UNUSED), None, ALU.add))
            step(v.tensor_copy(item_blk[0:1, 0:ITEMS], ps[0:1, 5, 0:ITEMS]))
            step(v.tensor_scalar(not_first[:, 0:ITEMS], ps[:, 6, 0:ITEMS], -1.0, 1.0, ALU.mult, ALU.add))
            step(v.tensor_scalar(first_neg[:, 0:ITEMS], ps[:, 6, 0:ITEMS], -BIG, None, ALU.mult))
            v.tensor_scalar(item_n[:, :], ps[0:1, 2, 1:3], 1.0, None, ALU.max).then_inc(items_ok, 1)

            key_squares(9, 1)
            with v.Fori(5, B // 2) as i:
                for k in range(2):
                    key_squares(v.snap(i * 2 + k), k)
            v.wait_ge(key_sum, B + 2)
            v.tensor_reduce(mean_rows[:, :], ps[:B, 3, 0:CC // 4 * 128].rearrange("p (c d) -> p d c", d=D), AX.X, ALU.add).then_inc(mean_ev, 1)

            def block_maximum(j, k):
                v.wait_ge(s_mm, j + 3)
                v.scalar_tensor_tensor(m_before[:, k:k + 1], m_run[:, :], not_first[:, bass.ds(j, 1)],
                                       first_neg[:, bass.ds(j, 1)], ALU.mult, ALU.add).then_inc(m_prev, 1)
                v.tensor_reduce(m_block[:, k:k + 1], ps[:, k, 0:KN], AX.X, ALU.max).then_inc(s_max, 1)
                v.wait_ge(m_prev, j + 1)
                v.wait_ge(s_max, j + 1)
                v.tensor_tensor(m_run[:, :], m_block[:, k:k + 1], m_before[:, k:k + 1], ALU.max).then_inc(m_new, 1)
                v.wait_ge(m_new, j + 1)
                v.tensor_scalar(m_minus[:, k:k + 1], m_run[:, :], -1.0, None, ALU.mult).then_inc(m_neg, 1)

            def accumulate(j):
                v.wait_ge(p_exp, j + 1)
                v.scalar_tensor_tensor(l_run[:, :], l_run[:, :], rescale[:, bass.ds(j, 1)], l_block[:, bass.ds(j, 1)],
                                       ALU.mult, ALU.add).then_inc(l_ok, 1)
                v.wait_ge(l_ok, j + 1)
                v.reciprocal(l_inv[:, :], l_run[:, :]).then_inc(rl_ok, 1)
                v.wait_ge(o_mm, j + 3)
                v.scalar_tensor_tensor(acc, acc, rescale[:, bass.ds(j, 1)], ps[:, 3, 0:128],
                                       ALU.mult, ALU.add).then_inc(acc_ok, 1)
                v.wait_ge(acc_ok, j + 1)
                v.wait_ge(rl_ok, j + 1)
                v.tensor_scalar(On, acc, l_inv[:, :], None, ALU.mult).then_inc(on_ok, 1)

            v.wait_ge(ld_small, 16 * SMALL)
            v.tensor_scalar(hb[:, :], bih[:, :], 0.5, None, ALU.mult).then_inc(hb_ok, 1)
            v.wait_ge(hb_ok, 1)
            v.scalar_tensor_tensor(hb[:, :], bhh[:, :], 0.5, hb[:, :], ALU.mult, ALU.add).then_inc(hb_ok, 1)
            v.tensor_scalar(wkey_s[:, :], wkey[:, :], float(D) ** -0.5, None, ALU.mult).then_inc(hb_ok, 1)
            keep, base, part = cen, sq, rstd
            v.wait_ge(gates_ok, 1)
            v.wait_ge(keep_mm, 1)
            step = chain(y_keep)
            step(v.tensor_tensor(gate_bout[:, :], bout[:, :], gates[:, 0:1], ALU.mult), wait=False)
            for h in range(2):
                step(v.tensor_scalar(keep[:, half(h)], ps[:, 5 + h, 0:HALF], gates[:, 0:1], None, ALU.mult), wait=(h == 1))
            step(v.tensor_scalar(base, keep, -1.0, gates[:, 0:1], ALU.mult, ALU.add), wait=False)
            n = v.value_load(item_n[0:1, 0:1], min_val=1, max_val=ITEMS)
            tiles = v.value_load(item_n[0:1, 1:2], min_val=1, max_val=TILES)
            for k in range(AHEAD):
                block_maximum(k, k)
            with v.Fori(0, (n + 1) // 2) as i:
                for k in range(2):
                    j = v.snap(i * 2 + k)
                    block_maximum(j + AHEAD, k)
                    accumulate(j)
            v.wait_ge(mean_mm, 1)
            v.tensor_copy(meanT[:, :], ps[:, 7, 0:B]).then_inc(mean_ev, 1)
            base3 = base.rearrange("p (b s) -> p b s", b=B)
            v.wait_ge(ymean_mm, 1)
            step(v.tensor_copy(ymean[:, :], ps[:, 7, 0:B]))
            step(v.tensor_tensor(base3, base3, bcast(ymean[:, :], S), ALU.mult))
            step(v.scalar_tensor_tensor(xT[:, :], base, gate_bout[:, :], xT[:, :], ALU.add, ALU.add))
            assert step.count[0] == Y_KEEP + 3
            with v.Fori(0, tiles) as i:
                tile = bass.ds(TILES - 1 - i, 1)
                y = ps[:, bass.ds(i, 1), 0:B * QT].rearrange("p t (b q) -> p t b q", b=B)
                v.wait_ge(y_mm, i + 1)
                v.tensor_tensor(by_tile(part)[:, tile, :, :], y, by_tile(keep)[:, tile, :, :], ALU.mult).then_inc(y_keep, 1)
                v.wait_ge(y_keep, i * 2 + (Y_KEEP + 4))
                v.tensor_tensor(by_tile(xT[:, :])[:, tile, :, :], by_tile(xT[:, :])[:, tile, :, :],
                                by_tile(part)[:, tile, :, :], ALU.add).then_inc(y_keep, 1)
            v.wait_ge(y_keep, tiles * 2 + (Y_KEEP + 3))
            v.sem_inc(x_new, 2)
            ln(1)

            step = chain(rt0)
            v.wait_ge(sc0_ok, 1)
            step(v.tensor_tensor(bi0[:, :, :], sc0[:, :, :], over_tiles(gb0[:, :]), ALU.add))
            for j in range(NT):
                step(v.max(top8[:, j, :], bi0[:, j, :]), wait=j == NT - 1)
            for j in range(NT):
                step(v.max_index(idx8[:, j, :], top8[:, j, :], bi0[:, j, :]), wait=j == NT - 1)
            step(v.tensor_copy(idxf[:, :, :], idx8[:, :, :]))
            step(v.tensor_tensor(msk[:, :, :], over_tiles(iota_e[:, 0:E0]), bcast(idxf[:, :, 0], E0), ALU.is_equal))
            for k in range(1, TOP0):
                step(v.tensor_tensor(hot[:, :, :], over_tiles(iota_e[:, 0:E0]), bcast(idxf[:, :, k], E0), ALU.is_equal))
                step(v.tensor_tensor(msk[:, :, :], msk[:, :, :], hot[:, :, :], ALU.add))
            step(v.tensor_tensor(msk[:, :, :], msk[:, :, :], sc0[:, :, :], ALU.mult))
            step(v.tensor_reduce(den[:, :], msk[:, :, :], AX.X, ALU.add))
            step(v.reciprocal(den[:, :], den[:, :]))
            step(v.tensor_scalar(den[:, :], den[:, :], ROUTE, None, ALU.mult))
            step(v.tensor_tensor(msk[:, :, :], msk[:, :, :], bcast(den[:, :], E0), ALU.mult))
            v.wait_ge(pair_ok, 6)
            for r in range(0, PARTS, 32):
                step(v.tensor_copy(parts[:, :, r:r + E0], msk[:, :, :]))
                if r + 32 < PARTS:
                    step(v.tensor_tensor(msk[:, :, :], msk[:, :, :], parts[:, :, r:r + E0], ALU.subtract))
            v.sem_inc(comb_ok, 1)
            v.wait_ge(rk_sd, 1)
            v.reciprocal(rkey[:, :, :], rms[:, :, :]).then_inc(rk_ok, 1)
            v.wait_ge(combT_mm, 1)
            for h in range(2):
                v.tensor_copy(combT[:PARTS, half(h)], ps[:PARTS, 6 + h, 0:HALF]).then_inc(combT_ok, 1)
            for j in range(2 * (PAIRS + 1)):
                p = 128 if j // 2 < PAIRS else F0
                v.wait_ge(e0_act, j + 1)
                if j >= 2:
                    v.wait_ge(e0_y, j - 1)
                v.tensor_tensor(hh[j % 2][:p, :], sg[j % 2][:p, :], ps[:p, 2 * (j % 2) + 1, 0:HALF], ALU.mult).then_inc(e0_up, 1)
                v.wait_ge(e0_up, j + 1)
                if j // 2 < PAIRS:
                    v.wait_ge(e0_share, j + 1)
                    v.tensor_tensor(hh[j % 2], hh[j % 2], ps[:, 6 + j % 2, 0:HALF], ALU.mult).then_inc(e0_h, 1)
            v.wait_ge(e0_y, 2 * (PAIRS + 1))
            for h in range(2):
                v.scalar_tensor_tensor(xT[:, half(h)], ps[:, 4 + h, 0:HALF], gates[:, 2:3], xT[:, half(h)],
                                       ALU.mult, ALU.add).then_inc(x_new, 1)
            v.wait_ge(x_new, 4)
            ln(2)

            v.wait_ge(rk_ok, 1)
            v.wait_ge(ln_out, 6)
            v.wait_ge(hb_ok, 3)

            def maxima(g, k, u, m):
                (s, h), a, b, n = divmod(m, 2), m // 2 % 2, g * GB + k * QB + m // 2, u * HB + m
                c = slice(h * CH, (h + 1) * CH)
                v.wait_ge(a_mm, n + 1)
                v.tensor_reduce(mx[:, a, c], ps[:CP, 2 + 2 * a + h, 0:CH * S].rearrange("p (c s) -> p c s", s=S),
                                AX.X, ALU.max).then_inc(a_max, 1)
                v.wait_ge(a_max, n + 1)
                v.scalar_tensor_tensor(nb[:, a, c], mx[:, a, c], -1.0, rkey[:, b, c], ALU.mult, ALU.mult).then_inc(a_neg, 1)

            def attention(g, k, u, m):
                (s, h), a, b, n = divmod(m, 2), m // 2 % 2, g * GB + k * QB + m // 2, u * HB + m
                c = slice(h * CH, (h + 1) * CH)
                v.wait_ge(a_exp, n + 1)
                v.reciprocal(rs[:, a, c], sm[:, a, c]).then_inc(a_rec, 1)
                v.wait_ge(a_rec, n + 1)
                v.tensor_tensor(rs[:, a, c], rs[:, a, c], rkey[:, b, c], ALU.mult).then_inc(a_w, 1)
                v.wait_ge(a_w, n + 1)
                v.tensor_tensor(A[a][:CP, c, :], A[a][:CP, c, :], bcast(rs[:, a, c], S), ALU.mult).then_inc(a_att, 1)

            def update(u, s):
                n, a = u * QB + s, s % 2
                v.wait_ge(u_mm, u * HB + (2 * s + 2))
                v.tensor_scalar(zr[:, a, :], ps[:S, 6 + a, 128:KW], 1e-6, None, ALU.add).then_inc(z_add, 1)
                v.wait_ge(z_add, n + 1)
                v.reciprocal(zr[:, a, :], zr[:, a, :]).then_inc(z_rec, 1)
                v.wait_ge(z_rec, n + 1)
                v.tensor_scalar(UnN[:S, s, :], ps[:S, 6 + a, 0:128], zr[:, a, :], None, ALU.mult).then_inc(un_ok, 1)

            def gru_inputs(v_):
                v.wait_ge(ut_mm, v_ + 1)
                v.tensor_scalar(Un, ps[:, 1, 0:QS], wkey[:, 0:1], None, ALU.mult).then_inc(u_ok, 1)
                v.tensor_scalar(hn, ps[:, 1, QS:2 * QS], bhh[:, 2:3], None, ALU.add).then_inc(hn_ok, 1)

            def gru_candidate(v_):
                v.wait_ge(hn_ok, v_ + 1)
                v.wait_ge(gru_t, v_ * 2 + 2)
                v.scalar_tensor_tensor(tmp, rt, 1.0, hn, ALU.add, ALU.mult).then_inc(gru_v, 1)
                v.wait_ge(gru_v, v_ * 2 + 1)
                v.scalar_tensor_tensor(tmp, tmp, 0.5, ps[:, 1, 0:QS], ALU.mult, ALU.add).then_inc(gru_v, 1)

            def gru_slots_new(v_, k, dst):
                v.wait_ge(gru_n, v_ + 1)
                v.tensor_tensor(rt, slots_x[:, k, :], nt, ALU.subtract).then_inc(gru_new, 1)
                v.wait_ge(gru_new, v_ * 2 + 1)
                v.scalar_tensor_tensor(rt, zt, 1.0, rt, ALU.add, ALU.mult).then_inc(gru_new, 1)
                v.wait_ge(gru_new, v_ * 2 + 2)
                return v.scalar_tensor_tensor(dst, rt, 0.5, nt, ALU.mult, ALU.add)

            def finish(v_, g, k):
                gru_slots_new(v_, k, tmp).then_inc(gru_last, 1)
                v.wait_ge(gru_last, g * 2 + k + 1)
                v.scalar_tensor_tensor(xT[:, quad(g, k)], tmp, gates[:, 1:2], xT[:, quad(g, k)], ALU.mult, ALU.add).then_inc(x_new, 1)

            def slot_norm(u, k):
                v.wait_ge(q_sd, u + 1)
                v.reciprocal(rstd1, rstd1).then_inc(q_rec, 1)
                v.wait_ge(q_rec, u + 1)
                v.scalar_tensor_tensor(sn, slots_x[:, k, :], wslot[:, 0:1], rstd1, ALU.mult, ALU.mult).then_inc(q_sn, 1)

            def queries(u, k):
                v.wait_ge(q_mm, u + 1)
                v.tensor_scalar(qT[:, k, 0:QS], ps[:, 1, 0:QS], wkey_s[:, :], None, ALU.mult).then_inc(q_ok, 1)

            v.tensor_copy(slots_x[:, 0, :], xln[:, quad(0, 0)]).then_inc(sl_ok, 1)
            v.wait_ge(sl_ok, 1)
            slot_norm(0, 0)
            v.wait_ge(q_pad, 1)
            queries(0, 0)
            for m in range(LOOK):
                maxima(0, 0, 0, m)
            attention(0, 0, 0, 0)

            def phase(g, w, u):
                k = w % 2
                gru = (g, w) != (0, 0)
                for m in range(HB):
                    if m == 0 and gru:
                        update(u - 1, QB - 1)
                        gru_inputs(u - 1)
                    if m + 1 < HB:
                        attention(g, k, u, m + 1)
                    elif prepares(g, w):
                        attention(g + w // (PHASES - 1), 1 - k, u + 1, 0)
                    if m + LOOK < HB:
                        maxima(g, k, u, m + LOOK)
                    elif prepares(g, w):
                        maxima(g + w // (PHASES - 1), 1 - k, u + 1, m + LOOK - HB)
                    if m == 4 and prepares(g, w):
                        queries(u + 1, 1 - k)
                    if m == 0 and gru:
                        gru_candidate(u - 1)
                    if m == 1:
                        if w in (0, PHASES - 1):
                            if gru:
                                finish(u - 1, g - (w == 0), 1 - k)
                            if loads_next(g, w):
                                v.tensor_copy(slots_x[:, 1 - k, :], xln[:, quad(g + (w > 0), 1 - k)]).then_inc(sl_ok, 1)
                        else:
                            gru_slots_new(u - 1, 1 - k, slots_x[:, 1 - k, :]).then_inc(sl_ok, 1)
                    if m in (2, 4, 6):
                        update(u, m // 2 - 1)
                    if m == 2 and prepares(g, w):
                        v.wait_ge(sl_ok, u + 2)
                        slot_norm(u + 1, 1 - k)

            phases(v, phase)
            last = GROUPS * PHASES - 1
            update(last, QB - 1)
            gru_inputs(last)
            gru_candidate(last)
            finish(last, GROUPS - 1, 1)
            v.wait_ge(x_new, 4 + 2 * GROUPS)
            ln(3)

            step = chain(rt1)
            v.wait_ge(lg1_mm, 1)
            logits = ps[:, 0, 0:NT * E1].rearrange("p (n e) -> p n e", n=NT)
            step(v.tensor_tensor(lg, logits, over_tiles(gb1[:, :]), ALU.add))
            step(v.tensor_reduce(r1[:, :], lg, AX.X, ALU.max))
            step(v.tensor_tensor(lg, lg, bcast(r1[:, :], E1), ALU.subtract))
            v.wait_ge(rt1_exp, 1)
            step(v.tensor_reduce(r2[:, :], pr, AX.X, ALU.add))
            step(v.reciprocal(r2[:, :], r2[:, :]))
            step(v.tensor_tensor(pr, pr, bcast(r2[:, :], E1), ALU.mult))
            for j in range(NT):
                step(v.max(top8[:, j, :], pr[:, j, :]), wait=j == NT - 1)
            for j in range(NT):
                step(v.max_index(idx8[:, j, :], top8[:, j, :], pr[:, j, :]), wait=j == NT - 1)
            step(v.tensor_copy(idxf[:, :, :], idx8[:, :, :]))
            for k in range(TOP1):
                step(v.tensor_tensor(oh[k], over_tiles(iota_e[:, :]), bcast(idxf[:, :, k], E1), ALU.is_equal))
            v.tensor_tensor(ohb, oh[0], oh[1], ALU.add).then_inc(rt1_hot, 1)
            v.wait_ge(pos_mm, 1)
            places = ps[:, 1, 0:NT * E1].rearrange("p (n e) -> p n e", n=NT)
            for k in range(TOP1):
                step(v.tensor_tensor(posx, oh[k], places, ALU.mult))
                step(v.tensor_reduce(posk[:, k, :], posx, AX.X, ALU.add))
            step(v.tensor_scalar(valid[:, :, :], posk[:, :, :], float(CAP), None, ALU.is_lt))
            for k in range(TOP1):
                step(v.scalar_tensor_tensor(posk[:, k, :], idxf[:, :, k], float(CAP), posk[:, k, :], ALU.mult, ALU.add))
            step(v.tensor_tensor(posk[:, :, :], posk[:, :, :], valid[:, :, :], ALU.mult))
            v.tensor_copy(gidx[:, :, :], posk[:, :, :]).then_inc(slot_ok, 1)
            step(v.tensor_tensor(wk[:, :, :], trash[:, :, :], valid[:, :, :], ALU.mult))
            step(v.tensor_tensor(wk[:, :, :], trash[:, :, :], wk[:, :, :], ALU.subtract))
            v.tensor_tensor(sidx[:, :, :], posk[:, :, :], wk[:, :, :], ALU.add).then_inc(slot_ok, 1)
            step(v.tensor_tensor(r1[:, :], top8[:, :, 0], top8[:, :, 1], ALU.add))
            step(v.reciprocal(r1[:, :], r1[:, :]))
            v.wait_ge(slot_ok, 2)
            for k in range(TOP1):
                step(v.scalar_tensor_tensor(wk[:, k, :], top8[:, :, k], gates[:, 3:4], r1[:, :], ALU.mult, ALU.mult))
            step(v.tensor_tensor(wk[:, :, :], wk[:, :, :], valid[:, :, :], ALU.mult))
            for e in range(E1):
                v.wait_ge(h_mm, e + 1)
                if e >= 2:
                    v.wait_ge(h_ok, e - 1)
                v.tensor_tensor(hx[e % 2][:, :, :], ps[:, e % 2, 0:FC * CAP].rearrange("p (c n) -> p c n", c=FC),
                                bcast(b1T[:, e, :], CAP), ALU.add).then_inc(h_b, 1)
                if e % 4 == 3:
                    g = e // 4
                    v.wait_ge(ye_mm, e + 1)
                    v.tensor_tensor(ysT[:, 4 * g * CAP:4 * (g + 1) * CAP].rearrange("p (c n) -> p c n", c=4),
                                    ps[:, 2 + g % 2, 0:4 * CAP].rearrange("p (c n) -> p c n", c=4),
                                    bcast(b2T[:, 4 * g:4 * g + 4], CAP), ALU.add).then_inc(ye_ok, 1)
            v.wait_ge(st_xe, 16 * TOP1 * NT)
            for j in range(NT):
                v.wait_ge(ld_yg[j // 2], 16 * TOP1 * min(2, NT - j // 2 * 2))
                v.scalar_tensor_tensor(xtok[:, j, :], yg[:, 0, j * 128:(j + 1) * 128], wk[:, 0, j:j + 1], rtok[:, j, :],
                                       ALU.mult, ALU.add).then_inc(out_s, 1)
                v.wait_ge(out_s, 2 * j + 1)
                v.scalar_tensor_tensor(xtok[:, j, :], yg[:, 1, j * 128:(j + 1) * 128], wk[:, 1, j:j + 1], xtok[:, j, :],
                                       ALU.mult, ALU.add).then_inc(out_s, 1)

        @block.tensor
        def _(pe):
            def ln(k):
                for h in range(2):
                    if k:
                        pe.wait_ge(x_new, 4 + 2 * GROUPS if k == 3 else 2 * k - 1 + h)
                    pe.matmul(ps[:, h, 0:HALF], mean_w[:, :], xT[:, half(h)], start=True, stop=True).then_inc(ln_mean, 1)
                for j in range(NT):
                    pe.wait_ge(ln_sq, 2 * k + (1 if (j + 1) * 128 <= HALF else 2))
                    mm = pe.matmul(ps[:, 2, j:j + 1], sq[:, j * 128:(j + 1) * 128], mean_w[:, 0:1], start=True, stop=True)
                mm.then_inc(ln_var, 1)
                for h in range(2):
                    pe.wait_ge(ln_diag, 2 * k + h + 1)
                    pe.wait_ge(ln_cent, 2 * k + 2)
                    pe.matmul(ps[:, h, 0:HALF], ones[:, :], rstd[:, half(h)], start=True, stop=True).then_inc(ln_bc, 1)

            pe.wait_ge(const, CONSTS)
            pe.wait_ge(ld_x, 16)
            ln(0)
            pe.wait_ge(ld_attn, 64)
            for f, (left, right) in enumerate(((wqT, wkT), (wvT, wo))):
                for q in range(4):
                    if f:
                        pe.wait_ge(fold_ev, q + 1)
                    r0 = DH * (q % 2)
                    for m in range(4):
                        pair = 4 * (q // 2) + m
                        mm = pe.matmul(ps[:, 4 + q, m * 128:(m + 1) * 128], left[r0:r0 + DH, pair, :],
                                       right[r0:r0 + DH, pair, :], start=True, stop=True)
                    mm.then_inc(fold_mm, 1)
            pe.wait_ge(fold_ev, 8)
            pe.wait_ge(ln_out, 2)
            for b in range(B):
                pe.wait_ge(key_add3, b + 2)
                pe.matmul(ps[:B, 3, 0:CC // 4 * 128], key_sel[:, b, :], padd[b % 2][:CP, :],
                          start=(b == 0), stop=(b == B - 1), skip_group_check=True).then_inc(key_sum, 1)
                for h in range(2):
                    if b:
                        pe.wait_ge(qa_ev, 2 * b - 1 + h)
                    pe.matmul(ps[:, h, 0:HALF], G[:, b, :], xln[:, half(h)], start=True, stop=True).then_inc(qa_mm, 1)
                if b == 3:
                    pe.wait_ge(plan_rs, 1)
                    pe.matmul(ps[:BT, 2, 0:1], before[:BT, 0:BT], rowsum[:, :], start=True, stop=True).then_inc(plan_rank, 1)
                    pe.matmul(ps[0:1, 2, 1:2], ones[:BT, 0:1], rowsum[:, :], start=True, stop=True).then_inc(plan_rank, 1)
                if b == 6:
                    pe.wait_ge(plan_hot, KB)
                    pe.wait_ge(plan, PLAN_LISTS)
                    for bank, col, items, left in ((4, 0, ITEMS, lambda b: lists_w[:, b, 0:1]),
                                                   (5, 0, ITEMS, lambda b: lists_w[:, b, 1:2]),
                                                   (2, 8, ITEMS, lambda b: lists_w[:, b, 2:3]),
                                                   (2, 2, 1, lambda b: lists_w[:, b, 3:4]),
                                                   (6, 0, ITEMS, lambda b: first_w[:, b, :])):
                        rows = 128 if bank == 6 else 1
                        for blk in range(KB):
                            mm = pe.matmul(ps[:rows, bank, col:col + items], left(blk), hot_r[blk][:BT, 0:items],
                                           start=(blk == 0), stop=(blk == KB - 1))
                    mm.then_inc(plan_list, 1)
            pe.wait_ge(items_ok, 1)
            pe.wait_ge(plan_hot, KB + 1)
            for h in range(2):
                mm = pe.matmul(ps[:, 5 + h, 0:HALF], ones[:BT, :], keep_d[:BT, half(h)], start=True, stop=True)
            mm.then_inc(keep_mm, 1)

            def item_scores(j, k, loads):
                pe.wait_ge(ld_itemT[k], loads)
                pe.wait_ge(q_tile, j + 1)
                pe.matmul(ps[:, k, 0:KN], Qk[k], ictxT[k], start=True, stop=False)
                pe.matmul(ps[:, k, 0:KN], ones_b[0:1, :], mask_b[k][0:1, 0:KN], start=False, stop=True).then_inc(s_mm, 1)

            def transpose_result(j):
                pe.wait_ge(on_ok, j + 1)
                pe.wait_ge(ot_ev, j + 1)
                pe.matmul(ps[:, 4, 0:128], On, ident[:, :], start=True, stop=True).then_inc(ot_mm, 1)

            n = pe.value_load(item_n[0:1, 0:1], min_val=1, max_val=ITEMS)
            tiles = pe.value_load(item_n[0:1, 1:2], min_val=1, max_val=TILES)
            for k in range(AHEAD):
                item_scores(k, k, 32)
            with pe.Fori(0, (n + 1) // 2) as i:
                for k in range(2):
                    j = pe.snap(i * 2 + k)
                    pe.wait_ge(p_exp, j + 1)
                    for c in range(KC):
                        mm = pe.transpose(ps[:KP, 2, c * 128:(c + 1) * 128],
                                          P[k].rearrange("p (m c) -> p c m", c=KC)[:, c, :], ident[:, :])
                    mm.then_inc(pt_mm, 1)
                    item_scores(j + AHEAD, k, i * 32 + 64)
                    transpose_result(j)
                    pe.wait_ge(pt_ev, j + 1)
                    pe.wait_ge(ld_item[k], i * 16 + 16)
                    for c in range(KC):
                        mm = pe.matmul(ps[:, 3, 0:128], PT[:KP, c, :], ictx[k][:KP, c, :], start=(c == 0), stop=(c == KC - 1))
                    mm.then_inc(o_mm, 1)
            last = pe.snap((n + 1) // 2 * 2)
            transpose_result(last)
            pe.wait_ge(mean_ev, 1)
            pe.matmul(ps[:, 7, 0:B], mean_rows[:, :], ident[:B, 0:B], start=True, stop=True).then_inc(mean_mm, 1)
            pe.wait_ge(fold_sum, 1)
            pe.wait_ge(mean_ev, 2)
            pe.wait_ge(ot_ev, last + 2)
            pe.wait_ge(p_exp, last + AHEAD)
            pe.wait_ge(y_keep, Y_KEEP)
            pe.matmul(ps[:, 7, 0:B], MS[:, :], meanT[:, :], start=True, stop=True).then_inc(ymean_mm, 1)
            with pe.Fori(0, tiles) as i:
                tile = bass.ds(pe.snap(TILES - 1 - i), 1)
                for head in range(H):
                    mm = pe.matmul(ps[:, bass.ds(i, 1), 0:B * QT], MO[:, head, :],
                                   by_tile(tilesT[:, head, 0:T])[:, tile, :, :],
                                   start=(head == 0), stop=(head == H - 1))
                mm.then_inc(y_mm, 1)
            ln(1)

            pe.wait_ge(ld_small, 16 * SMALL)
            pe.wait_ge(ln_out, 4)
            for j in range(NT):
                mm = pe.matmul(ps[:, 4, j * E0:(j + 1) * E0], xln[:, j * 128:(j + 1) * 128], gw0[:, :], start=True, stop=True)
            mm.then_inc(lg0_mm, 1)
            def hidden(j):
                pair, h = divmod(j, 2)
                p = 128 if pair < PAIRS else F0
                if j >= 2:
                    pe.wait_ge(e0_up, j - 1)
                for g in range(2):
                    w = w13[:, g, pair * 2 * F0:(pair + 1) * 2 * F0] if pair < PAIRS else ws[:, g * F0:(g + 1) * F0]
                    mm = pe.matmul(ps[:p, 2 * (j % 2) + g, 0:HALF], w, xln[:, half(h)], start=True, stop=True)
                mm.then_inc(e0_mm, 1)

            def shares(j):
                pair, h = divmod(j, 2)
                if pair < PAIRS:
                    if j >= 2:
                        pe.wait_ge(e0_h, j - 1)
                    pe.matmul(ps[:, 6 + j % 2, 0:HALF], pair_sel[:PARTS, pair, :], combT[:PARTS, half(h)],
                              start=True, stop=True).then_inc(e0_share, 1)

            pe.wait_ge(ld_ffn0, 32)
            hidden(0)
            hidden(1)
            pe.wait_ge(comb_ok, 1)
            for j in range(NT):
                c = j * 128
                for c0, c1 in ((c, min(c + 128, max(c, HALF))), (max(c, min(HALF, c + 128)), c + 128)):
                    if c1 > c0:
                        mm = pe.matmul(ps[:PARTS, 6 + c0 // HALF, c0 % HALF:c0 % HALF + c1 - c0],
                                       parts[:, j, :], ident_b[:, c0 - c:c1 - c], start=True, stop=True)
            mm.then_inc(combT_mm, 1)
            pe.wait_ge(combT_ok, 2)
            shares(0)

            def down(j):
                pair, h = divmod(j, 2)
                if pair < PAIRS:
                    pe.wait_ge(e0_h, j + 1)
                else:
                    pe.wait_ge(e0_up, j + 1)
                w, x = (w2p[:, pair, :], hh[j % 2]) if pair < PAIRS else (w2s[:, :], hh[j % 2][:F0, :])
                pe.matmul(ps[:, 4 + h, 0:HALF], w, x, start=(pair == 0), stop=(pair == PAIRS),
                          skip_group_check=True).then_inc(e0_y, 1)

            last = 2 * (PAIRS + 1)
            for j in range(last):
                if j + 1 < last:
                    if j:
                        hidden(j + 1)
                    shares(j + 1)
                down(j)
            pe.wait_ge(e0_h, 2 * PAIRS)
            pe.matmul(ps[:, 6, 0:128], wq1[:, :], wk1[:, :], start=True, stop=True).then_inc(g1_mm, 1)
            pe.matmul(ps[:, 7, 0:3 * D], wv1[:, :], wih[:, :], start=True, stop=True).then_inc(g1_mm, 1)
            ln(2)

            pe.wait_ge(g1_ev, 2)

            def scores(g, k, u, m):
                (s, h), a, n = divmod(m, 2), m // 2 % 2, u * HB + m
                pe.wait_ge(q_ok, u + 1)
                pe.wait_ge(ld_keys[k * QB + s], (g + 1) * 48)
                if not isinstance(n, int) or n >= 4:
                    pe.wait_ge(a_exp, n - 3)
                for c in range(CH):
                    mm = pe.matmul(ps[:CP, 2 + 2 * a + h, c * S:c * S + WIDE],
                                   keysT[:, k * QB + s, :].rearrange("p (m c) -> p c m", c=CC)[:, h * CH + c, :],
                                   qT[:, k, s * S:s * S + WIDE], start=True, stop=True)
                mm.then_inc(a_mm, 1)

            def update(g, k, u, m):
                (s, h), a, n = divmod(m, 2), m // 2 % 2, u * QB + m // 2
                pe.wait_ge(a_att, u * HB + (m + 1))
                if h == 0:
                    pe.wait_ge(key_col, g * GB + k * QB + s + 1)
                    if not isinstance(n, int) or n >= 2:
                        pe.wait_ge(un_ok, n - 1)
                for c in range(h * CH, (h + 1) * CH):
                    mm = pe.matmul(ps[:S, 6 + a, 0:KW], A[a][:CP, c, :], keys[:, k * QB + s, c, :],
                                   start=(c == 0), stop=(c == CC - 1), skip_group_check=True)
                mm.then_inc(u_mm, 1)

            def gru_start(v_, k):
                if not isinstance(v_, int) or v_ > 0:
                    pe.wait_ge(gru_v, v_ * 2)
                for gate in range(2):
                    pe.matmul(ps[:, 0, gate * QS:(gate + 1) * QS], whh[:, gate * D:(gate + 1) * D],
                              slots_x[:, k, :], start=(gate == 0), stop=False, skip_group_check=True)
                pe.matmul(ps[:, 1, QS:2 * QS], whh[:, 2 * D:3 * D], slots_x[:, k, :], start=True, stop=True)
                pe.wait_ge(un_ok, (v_ + 1) * QB)
                for s in range(QB):
                    mm = pe.matmul(ps[:, 1, s * S:(s + 1) * S], UnN[:S, s, :], ident[:S, 0:S], start=True, stop=True)
                mm.then_inc(ut_mm, 1)

            def gru_gates(v_):
                pe.wait_ge(u_ok, v_ + 1)
                for gate in range(2):
                    pe.matmul(ps[:, 0, gate * QS:(gate + 1) * QS], F1w[:, gate * D:(gate + 1) * D], Un,
                              start=False, stop=True, skip_group_check=True)
                pe.wait_ge(hn_ok, v_ + 1)
                pe.matmul(ps[:, 1, 0:QS], F1w[:, 2 * D:3 * D], Un, start=True, stop=True).then_inc(gate_mm, 1)

            def slot_var(u):
                pe.wait_ge(q_sq, u + 1)
                pe.matmul(ps[:, 0, 0:QS], mean_w[:, :], sq1, start=True, stop=True).then_inc(q_var, 1)

            def queries(u):
                pe.wait_ge(q_sn, u + 1)
                pe.matmul(ps[:, 1, 0:QS], G1[:, :], sn, start=True, stop=True).then_inc(q_mm, 1)

            slot_var(0)
            queries(0)
            for m in range(LOOK):
                scores(0, 0, 0, m)

            def phase(g, w, u):
                k = w % 2
                gru = (g, w) != (0, 0)
                for m in range(HB):
                    if m == 0 and gru:
                        gru_start(u - 1, 1 - k)
                    if m + LOOK < HB:
                        scores(g, k, u, m + LOOK)
                    elif prepares(g, w):
                        scores(g + w // (PHASES - 1), 1 - k, u + 1, m + LOOK - HB)
                    if m == 0 and gru:
                        gru_gates(u - 1)
                    if m == 2 and prepares(g, w):
                        slot_var(u + 1)
                    if m == 4 and prepares(g, w):
                        queries(u + 1)
                    update(g, k, u, m)

            phases(pe, phase)
            gru_start(GROUPS * PHASES - 1, 1)
            gru_gates(GROUPS * PHASES - 1)
            ln(3)

            pe.wait_ge(ln_out, 8)
            for j in range(NT):
                mm = pe.matmul(ps[:, 0, j * E1:(j + 1) * E1], xln[:, j * 128:(j + 1) * 128], gw1[:, :], start=True, stop=True)
            mm.then_inc(lg1_mm, 1)
            for c in range(4):
                src = (xln, xT)[c // 2]
                j0, j1 = ((0, 4), (4, NT))[c % 2]
                for j in range(j0, j1):
                    mm = pe.transpose(ps[:, 4 + c, (j - j0) * 128:(j - j0 + 1) * 128], src[:, j * 128:(j + 1) * 128], ident[:, :])
                mm.then_inc(tok_mm, 1)
            pe.wait_ge(rt1_hot, 1)
            for j in range(NT):
                for i in range(j + 1):
                    mm = pe.matmul(ps[:, 1, j * E1:(j + 1) * E1], before_b[:, :] if i == j else ones_b[:, :],
                                   ohb[:, i, :], start=(i == 0), stop=(i == j))
            mm.then_inc(pos_mm, 1)
            pe.wait_ge(tok_ev, 4)

            def expert_rows(c):
                pe.wait_ge(ld_xe[c // 2 and 1], 16)
                if c >= 2:
                    pe.wait_ge(xe_ev, c - 1)
                for j in range(4 * c, min(4 * c + 4, ST)):
                    mm = pe.transpose(ps[:, 4 + c % 2, j % 4 * 128:(j % 4 + 1) * 128], xe[:, j, :], ident[:, :])
                mm.then_inc(xe_mm, 1)

            expert_rows(0)
            expert_rows(1)

            def weights(e):
                return early_w[:, e, :] if e < EARLY else late_w[:, e - EARLY, :]

            def hidden(e):
                if e == 0:
                    pe.wait_ge(ld_early, 16)
                    pe.wait_ge(wide_ok, 3)
                if e >= EARLY and (e - EARLY) % 4 == 0:
                    pe.wait_ge(ld_late[(e - EARLY) // 4], 16)
                pe.wait_ge(xe_ev, min(YC, (e * CAP + WIDE - 1) // 512 + 1))
                if e >= 2:
                    pe.wait_ge(h_b, e - 1)
                for c in range(FC):
                    mm = pe.matmul(ps[:, e % 2, c * CAP:c * CAP + WIDE], weights(e)[:, c * 128:(c + 1) * 128],
                                   xeT[:, e * CAP:e * CAP + WIDE], start=True, stop=True)
                mm.then_inc(h_mm, 1)

            def result(e):
                g = e // 4
                if e % 4 == 0 and g >= 2:
                    pe.wait_ge(ye_ok, g - 1)
                pe.wait_ge(h_ok, e + 1)
                for c in range(FC):
                    mm = pe.matmul(ps[:, 2 + g % 2, e % 4 * CAP:e % 4 * CAP + WIDE], weights(e)[:, F1 + c * 128:F1 + (c + 1) * 128],
                                   hT[e % 2][:, c * CAP:c * CAP + WIDE], start=(c == 0), stop=(c == FC - 1))
                mm.then_inc(ye_mm, 1)

            def slot_rows(c):
                pe.wait_ge(ye_ok, slot_rows_after(c) // 4 + 1)
                if c >= 2:
                    pe.wait_ge(yt_ev, c - 1)
                for j in range(4 * c, min(4 * c + 4, ST)):
                    mm = pe.transpose(ps[:, 6 + c % 2, j % 4 * 128:(j % 4 + 1) * 128], ysT[:, j * 128:(j + 1) * 128], ident[:, :])
                mm.then_inc(yt_mm, 1)

            hidden(0)
            for e in range(E1):
                if e + 1 < E1 and e % 4 != 3:
                    hidden(e + 1)
                result(e)
                if e + 1 < E1 and e % 4 == 3:
                    hidden(e + 1)
                for c in range(2, YC):
                    if expert_rows_after(c) == e:
                        expert_rows(c)
                for c in range(YC):
                    if slot_rows_after(c) + 1 == e:
                        slot_rows(c)
            for c in range(YC):
                if slot_rows_after(c) + 1 >= E1:
                    slot_rows(c)


SMALL = 20
CONSTS = 27
PLAN_LISTS = 38
Y_KEEP = 4


def kernel(**inputs):
    import numpy as np
    import concourse.bacc as _bacc
    from concourse import mybir as _mybir
    from concourse.bass_utils import run_bass_kernel_spmd as _run

    a = {k: np.asarray(v) for k, v in inputs.items()}

    def heads(w):
        return w.T.reshape(H // 2, 2 * DH, D).transpose(1, 0, 2)

    ctx = a["ctx_1024"]
    wkv = a["L0_xattn_Wkv"]
    w13 = a["L0_ffn_w13"]
    arrays = {
        "xT": a["x"].reshape(T, D).T,
        "ctx": ctx,
        "ctxT": ctx.transpose(0, 2, 1),
        "ctx_blk": ctx.reshape(B * KB, KN, D),
        "ctxT_blk": ctx.reshape(B * KB, KN, D).transpose(0, 2, 1),
        "kv_mask": a["mask_BxS2_bk0"],
        "kv_blk": a["mask_BxS2_bk0"].reshape(B * KB, KN),
        "q_mask": a["mask_BxS_bk0"].reshape(B, TILES, QT).transpose(1, 0, 2).reshape(BT, QT),
        "wqT": heads(a["L0_xattn_Wq"]),
        "wkT": heads(wkv[:, 0:H * DH]),
        "wvT": heads(wkv[:, H * DH:]),
        "wo": a["L0_xattn_Wout"].reshape(H // 2, 2 * DH, D).transpose(1, 0, 2),
        "bout": a["L0_xattn_bout"].reshape(D, 1),
        "g_xattn": a["g_xattn"].reshape(1, 2),
        "g_ffn": a["g_ffn"].reshape(1, 2),
        "gw0": a["L0_ffn_gate_w"].T,
        "gb0": a["L0_ffn_gate_b"].reshape(1, E0),
        "w13": w13.reshape(E0, 2, F0, D).transpose(3, 1, 0, 2).reshape(D, 2, E0 * F0),
        "w2p": a["L0_ffn_w2"].transpose(0, 2, 1).reshape(PAIRS, 2 * F0, D).transpose(1, 0, 2),
        "ws": a["L0_ffn_w13_s"].T,
        "w2s": a["L0_ffn_w2_s"].T,
        "wq1": a["L1_xattn_Wq"],
        "wk1": a["L1_xattn_Wk"],
        "wv1": a["L1_xattn_Wv"],
        "wih": a["L1_xattn_gru_wih"].T,
        "whh": a["L1_xattn_gru_whh"].T,
        "bih": a["L1_xattn_gru_bih"].reshape(3, D).T,
        "bhh": a["L1_xattn_gru_bhh"].reshape(3, D).T,
        "wslot": a["L1_xattn_slot_norm_w"].reshape(D, 1),
        "wkey": a["L1_xattn_input_norm_w"].reshape(D, 1),
        "gw1": a["L1_ffn_gate_w"],
        "gb1": a["L1_ffn_gate_b"].reshape(1, E1),
        "b1T": a["L1_ffn_b1"].reshape(E1, FC, 128).transpose(2, 0, 1),
        "b2T": a["L1_ffn_b2"].T,
        "w12": np.concatenate([a["L1_ffn_w1"].transpose(1, 0, 2),
                               a["L1_ffn_w2"].reshape(E1, FC, 128, D).transpose(2, 0, 1, 3).reshape(128, E1, F1)], axis=2),
    }
    arrays = {k: np.ascontiguousarray(v) for k, v in arrays.items()}
    nc = _bacc.Bacc("TRN2", target_bir_lowering=False, num_devices=1)
    tensors = {k: nc.dram_tensor(f"in_{k}", v.shape, U8 if v.dtype == bool else _mybir.dt.from_np(v.dtype),
                                 kind="ExternalInput").ap()
               for k, v in arrays.items()}
    tensors["xe_scratch"] = nc.dram_tensor("xe_scratch", (SLOTS + TOP1 * T, D), _mybir.dt.float32).ap()
    tensors["ys_scratch"] = nc.dram_tensor("ys_scratch", (SLOTS, D), _mybir.dt.float32).ap()
    tensors["out"] = nc.dram_tensor("out_x", (T, D), _mybir.dt.float32, kind="ExternalOutput").ap()
    build_program(nc, tensors)
    r = _run(nc, [{f"in_{k}": v for k, v in arrays.items()}], core_ids=[0])
    return r.results[0]["out_x"].reshape(B, S, D)
```
